# Optimizing a Trainium2 kernel written in Bass

```python
import numpy as np
import jax
import jax.numpy as jnp

def _softmax(x, axis=-1):
    return jax.nn.softmax(x, axis=axis)

def _gelu(x):
    return jax.nn.gelu(x, approximate=True)

def _silu(x):
    return jax.nn.silu(x)

def _sigmoid(x):
    return jax.nn.sigmoid(x)

def _layernorm(x, axis=-1, eps=1e-05):
    m = jnp.mean(x, axis=axis, keepdims=True)
    v = jnp.var(x, axis=axis, keepdims=True)
    return (x - m) / jnp.sqrt(v + eps)

def _scatter_add(tgt, idx, src, axis=0):
    return tgt.at[idx].add(src)

def _segment_sum(src, seg, n):
    return jax.ops.segment_sum(src, seg, n)
kernel_name = 'mk_sandwich_d2_jaxref_r4_96a8b0'

def setup_inputs(seed: int=0):
    np.random.seed(seed)
    _w = jnp.asarray

    def _L0_attn_setup():
        import jax, jax.numpy as jnp
        import numpy as np
        NUM_HEADS = 16
        WINDOW = 64
        key = jax.random.key(seed)
        k1, k2, k3 = jax.random.split(key, 3)
        B, T, C = (4, 1024, 256)
        x = jax.random.normal(k1, (B, T, C), dtype=jnp.float32)
        w_attn = jax.random.normal(k2, (3 * C, C), dtype=jnp.float32) * C ** (-0.5)
        w_proj = jax.random.normal(k3, (C, C), dtype=jnp.float32) * C ** (-0.5)
        return {'x': x, 'w_attn': w_attn, 'w_proj': w_proj}
    _L0_attn_in = _L0_attn_setup()

    def _L0_ffn_setup():
        import jax, jax.numpy as jnp
        import numpy as np
        DIM = 256
        HIDDEN = 1024
        E = 8
        K = 2

        def _ffn_hidden(h, multiple_of=64):
            h = int(2 * h / 3)
            return multiple_of * ((h + multiple_of - 1) // multiple_of)
        EXP_HID = _ffn_hidden(HIDDEN)
        SH_HID = _ffn_hidden(HIDDEN // 2)

        def _swiglu(t, a, b, c):
            return jax.nn.silu(t @ a) * (t @ c) @ b
        key = jax.random.key(seed)
        ks = jax.random.split(key, 8)

        def xavier(k, shape, fan_in, fan_out):
            lim = np.sqrt(6.0 / (fan_in + fan_out)).astype(np.float32)
            return jax.random.uniform(k, shape, jnp.float32, -lim, lim)
        return {'x': jax.random.normal(ks[0], (2, 512, DIM), jnp.float32), 'gate_w': xavier(ks[1], (E, DIM), DIM, E), 'w1': xavier(ks[2], (E, DIM, EXP_HID), DIM, EXP_HID), 'w2': xavier(ks[3], (E, EXP_HID, DIM), EXP_HID, DIM), 'w3': xavier(ks[4], (E, DIM, EXP_HID), DIM, EXP_HID), 'sw1': xavier(ks[5], (DIM, SH_HID), DIM, SH_HID), 'sw2': xavier(ks[6], (SH_HID, DIM), SH_HID, DIM), 'sw3': xavier(ks[7], (DIM, SH_HID), DIM, SH_HID)}
    _L0_ffn_in = _L0_ffn_setup()

    def _L1_attn_setup():
        import jax, jax.numpy as jnp
        import numpy as np
        EMBED_DIM = 256
        NUM_HEADS = 16
        HEAD_DIM = EMBED_DIM // NUM_HEADS
        BATCH = 2
        SEQ = 512
        BASE = 10000.0
        EPS = 1e-05

        def _lrpe(t, theta, offset=0):
            n = t.shape[-2]
            idx = (jnp.arange(n) + offset).reshape(1, -1, 1).astype(theta.dtype)
            ang = theta * idx
            return jnp.concatenate([t * jnp.cos(ang), t * jnp.sin(ang)], axis=-1)
        key = jax.random.key(seed)
        ks = jax.random.split(key, 8)
        d, h, hd = (EMBED_DIM, NUM_HEADS, HEAD_DIM)
        s = d ** (-0.5)
        x = jax.random.normal(ks[0], (BATCH, SEQ, d), dtype=jnp.float32)
        Wq = jax.random.normal(ks[1], (d, d), dtype=jnp.float32) * s
        Wk = jax.random.normal(ks[2], (d, d), dtype=jnp.float32) * s
        Wv = jax.random.normal(ks[3], (d, d), dtype=jnp.float32) * s
        Wo = jax.random.normal(ks[4], (d, d), dtype=jnp.float32) * s
        G1 = jax.random.normal(ks[5], (d, hd), dtype=jnp.float32) * s
        G2 = jax.random.normal(ks[6], (hd, d), dtype=jnp.float32) * hd ** (-0.5)
        gamma = jnp.ones((d,), jnp.float32)
        beta = jnp.zeros((d,), jnp.float32)
        theta = jnp.asarray((BASE ** (-2.0 / (h * hd) * np.arange(h * hd))).reshape(h, 1, hd), dtype=jnp.float32)
        return {'x': x, 'Wq': Wq, 'Wk': Wk, 'Wv': Wv, 'Wo': Wo, 'G1': G1, 'G2': G2, 'gamma': gamma, 'beta': beta, 'theta': theta}
    _L1_attn_in = _L1_attn_setup()

    def _L1_ffn_setup():
        import jax, jax.numpy as jnp
        import numpy as np
        from jax import lax
        T, B, I, M, O = (64, 64, 256, 256, 256)

        def _xavier(key, shape):
            fan_out, fan_in = shape
            limit = float(np.sqrt(6.0 / (fan_in + fan_out)))
            return jax.random.uniform(key, shape, jnp.float32, -limit, limit)
        key = jax.random.key(seed)
        ks = jax.random.split(key, 9)
        x = jax.random.normal(ks[0], (T, B, I), jnp.float32)
        return {'x': x, 'wf': _xavier(ks[1], (M, I)), 'uf': _xavier(ks[2], (M, M)), 'bf': jnp.zeros((M,), jnp.float32), 'wi': _xavier(ks[3], (M, I)), 'ui': _xavier(ks[4], (M, M)), 'bi': jnp.zeros((M,), jnp.float32), 'wc': _xavier(ks[5], (M, I)), 'uc': _xavier(ks[6], (M, M)), 'bc': jnp.zeros((M,), jnp.float32), 'wo': _xavier(ks[7], (O, I)), 'uo': _xavier(ks[8], (O, M)), 'bo': jnp.zeros((O,), jnp.float32), 'in_c': jnp.zeros((M,), jnp.float32)}
    _L1_ffn_in = _L1_ffn_setup()
    _d = {'L0_attn_x': _L0_attn_in['x'], 'L0_attn_w_attn': _L0_attn_in['w_attn'], 'L0_attn_w_proj': _L0_attn_in['w_proj'], 'L0_ffn_gate_w': _L0_ffn_in['gate_w'], 'L0_ffn_w1': _L0_ffn_in['w1'], 'L0_ffn_w2': _L0_ffn_in['w2'], 'L0_ffn_w3': _L0_ffn_in['w3'], 'L0_ffn_sw1': _L0_ffn_in['sw1'], 'L0_ffn_sw2': _L0_ffn_in['sw2'], 'L0_ffn_sw3': _L0_ffn_in['sw3'], 'L1_attn_Wq': _L1_attn_in['Wq'], 'L1_attn_Wk': _L1_attn_in['Wk'], 'L1_attn_Wv': _L1_attn_in['Wv'], 'L1_attn_Wo': _L1_attn_in['Wo'], 'L1_attn_G1': _L1_attn_in['G1'], 'L1_attn_G2': _L1_attn_in['G2'], 'L1_attn_gamma': _L1_attn_in['gamma'], 'L1_attn_beta': _L1_attn_in['beta'], 'L1_attn_theta': _L1_attn_in['theta'], 'L1_ffn_wf': _L1_ffn_in['wf'], 'L1_ffn_uf': _L1_ffn_in['uf'], 'L1_ffn_bf': _L1_ffn_in['bf'], 'L1_ffn_wi': _L1_ffn_in['wi'], 'L1_ffn_ui': _L1_ffn_in['ui'], 'L1_ffn_bi': _L1_ffn_in['bi'], 'L1_ffn_wc': _L1_ffn_in['wc'], 'L1_ffn_uc': _L1_ffn_in['uc'], 'L1_ffn_bc': _L1_ffn_in['bc'], 'L1_ffn_wo': _L1_ffn_in['wo'], 'L1_ffn_uo': _L1_ffn_in['uo'], 'L1_ffn_bo': _L1_ffn_in['bo'], 'L1_ffn_in_c': _L1_ffn_in['in_c']}
    _x0 = _d['L0_attn_x']
    _d['L0_attn_x'] = jax.random.normal(jax.random.fold_in(jax.random.key(seed), 1), (2, 2048, 256), dtype=_x0.dtype)
    del _x0
    return _d

def reference(L0_attn_x, L0_attn_w_attn, L0_attn_w_proj, L0_ffn_gate_w, L0_ffn_w1, L0_ffn_w2, L0_ffn_w3, L0_ffn_sw1, L0_ffn_sw2, L0_ffn_sw3, L1_attn_Wq, L1_attn_Wk, L1_attn_Wv, L1_attn_Wo, L1_attn_G1, L1_attn_G2, L1_attn_gamma, L1_attn_beta, L1_attn_theta, L1_ffn_wf, L1_ffn_uf, L1_ffn_bf, L1_ffn_wi, L1_ffn_ui, L1_ffn_bi, L1_ffn_wc, L1_ffn_uc, L1_ffn_bc, L1_ffn_wo, L1_ffn_uo, L1_ffn_bo, L1_ffn_in_c):

    def _L0_attn_ref(x, w_attn, w_proj):
        import jax, jax.numpy as jnp
        import numpy as np
        NUM_HEADS = 16
        WINDOW = 64
        B, T, C = x.shape
        H, W = (NUM_HEADS, WINDOW)
        D = C // H
        nW = T // W
        qkv = jnp.einsum('btc,ec->bte', x, w_attn)
        qkv = qkv.reshape(B, nW, W, 3, H, D)
        q, k, v = (qkv[:, :, :, 0], qkv[:, :, :, 1], qkv[:, :, :, 2])
        scale = 1.0 / jnp.sqrt(jnp.float32(D))
        att = jnp.einsum('bnihd,bnjhd->bnhij', q, k) * scale
        att = jax.nn.softmax(att, axis=-1)
        y = jnp.einsum('bnhij,bnjhd->bnihd', att, v)
        y = y.reshape(B, T, C)
        return jnp.einsum('btc,oc->bto', y, w_proj)

    def _L0_ffn_ref(x, gate_w, w1, w2, w3, sw1, sw2, sw3):
        import jax, jax.numpy as jnp
        import numpy as np
        DIM = 256
        HIDDEN = 1024
        E = 8
        K = 2

        def _ffn_hidden(h, multiple_of=64):
            h = int(2 * h / 3)
            return multiple_of * ((h + multiple_of - 1) // multiple_of)
        EXP_HID = _ffn_hidden(HIDDEN)
        SH_HID = _ffn_hidden(HIDDEN // 2)

        def _swiglu(t, a, b, c):
            return jax.nn.silu(t @ a) * (t @ c) @ b
        B, S, D = x.shape
        xt = x.reshape(-1, D)
        T = xt.shape[0]
        logits = xt @ gate_w.T
        scores = jax.nn.softmax(logits, axis=-1)
        topk_w, topk_i = jax.lax.top_k(scores, K)
        comb = jnp.zeros((T, E), x.dtype).at[jnp.arange(T)[:, None], topk_i].add(topk_w)
        y = jnp.zeros_like(xt)
        for e in range(E):
            y = y + comb[:, e:e + 1] * _swiglu(xt, w1[e], w2[e], w3[e])
        y = y.reshape(B, S, D)
        return y + _swiglu(x, sw1, sw2, sw3)

    def _L1_attn_ref(x, Wq, Wk, Wv, Wo, G1, G2, gamma, beta, theta):
        import jax, jax.numpy as jnp
        import numpy as np
        EMBED_DIM = 256
        NUM_HEADS = 16
        HEAD_DIM = EMBED_DIM // NUM_HEADS
        BATCH = 2
        SEQ = 512
        BASE = 10000.0
        EPS = 1e-05

        def _lrpe(t, theta, offset=0):
            n = t.shape[-2]
            idx = (jnp.arange(n) + offset).reshape(1, -1, 1).astype(theta.dtype)
            ang = theta * idx
            return jnp.concatenate([t * jnp.cos(ang), t * jnp.sin(ang)], axis=-1)
        b, n, d = x.shape
        h, hd = (NUM_HEADS, HEAD_DIM)
        q = jax.nn.silu(x @ Wq)
        k = jax.nn.silu(x @ Wk)
        v = x @ Wv
        split = lambda t: t.reshape(b, n, h, hd).transpose(0, 2, 1, 3)
        q, k, v = (split(q), split(k), split(v))
        q = _lrpe(q, theta)
        k = _lrpe(k, theta)
        mask = jnp.tril(jnp.ones((n, n), dtype=x.dtype))
        energy = jnp.einsum('bhnd,bhmd->bhnm', q, k) * mask
        out = jnp.einsum('bhnm,bhmd->bhnd', energy, v)
        out = out.transpose(0, 2, 1, 3).reshape(b, n, d)
        out = out @ Wo
        gate = jax.nn.sigmoid(x @ G1 @ G2)
        out = out * gate
        mu = jnp.mean(out, axis=-1, keepdims=True)
        var = jnp.var(out, axis=-1, keepdims=True)
        out = (out - mu) / jnp.sqrt(var + EPS) * gamma + beta
        return out

    def _L1_ffn_ref(x, wf, uf, bf, wi, ui, bi, wc, uc, bc, wo, uo, bo, in_c):
        import jax, jax.numpy as jnp
        import numpy as np
        from jax import lax
        T, B, I, M, O = (64, 64, 256, 256, 256)

        def _xavier(key, shape):
            fan_out, fan_in = shape
            limit = float(np.sqrt(6.0 / (fan_in + fan_out)))
            return jax.random.uniform(key, shape, jnp.float32, -limit, limit)
        batch = x.shape[1]
        c0 = jnp.broadcast_to(in_c, (batch, in_c.shape[0]))

        def step(c, xt):
            ft = jax.nn.sigmoid(xt @ wf.T + c @ uf.T + bf)
            it = jax.nn.sigmoid(xt @ wi.T + c @ ui.T + bi)
            gt = jnp.tanh(xt @ wc.T + c @ uc.T + bc)
            c = ft * c + it * gt
            return (c, None)
        c_final, _ = lax.scan(step, c0, x)
        h = jnp.tanh(jnp.einsum('tbi,oi->tbo', x, wo) + c_final @ uo.T + bo)
        return h
    x = L0_attn_x
    x = x + _layernorm(_L0_attn_ref(_layernorm(x, axis=-1), L0_attn_w_attn, L0_attn_w_proj), axis=-1)
    x = x + _layernorm(_L0_ffn_ref(_layernorm(x, axis=-1), L0_ffn_gate_w, L0_ffn_w1, L0_ffn_w2, L0_ffn_w3, L0_ffn_sw1, L0_ffn_sw2, L0_ffn_sw3), axis=-1)
    x = x + _layernorm(_L1_attn_ref(_layernorm(x, axis=-1), L1_attn_Wq, L1_attn_Wk, L1_attn_Wv, L1_attn_Wo, L1_attn_G1, L1_attn_G2, L1_attn_gamma, L1_attn_beta, L1_attn_theta), axis=-1)
    x = x + _layernorm(_L1_ffn_ref(_layernorm(x, axis=-1), L1_ffn_wf, L1_ffn_uf, L1_ffn_bf, L1_ffn_wi, L1_ffn_ui, L1_ffn_bi, L1_ffn_wc, L1_ffn_uc, L1_ffn_bc, L1_ffn_wo, L1_ffn_uo, L1_ffn_bo, L1_ffn_in_c), axis=-1)
    return x

_drawn_inputs = setup_inputs


def setup_inputs(seed=0):
    import zlib

    import numpy as np

    out = dict(_drawn_inputs(seed))
    spreads = {'L1_attn_gamma': (1.0, 0.2),
     'L1_attn_beta': (0.0, 0.1),
     'L1_ffn_bf': (0.0, 0.8),
     'L1_ffn_bi': (0.0, 0.8),
     'L1_ffn_bc': (0.0, 0.3),
     'L1_ffn_bo': (0.0, 0.1),
     'L1_ffn_in_c': (0.0, 0.354)}
    factors = {'L1_ffn_uf': 4.926}
    for name, (base, spread) in spreads.items():
        noise = np.random.default_rng([zlib.crc32(name.encode()), seed]).standard_normal(out[name].shape)
        drawn = base * np.exp(spread * noise) if base else spread * noise
        out[name] = jnp.asarray(drawn.astype(out[name].dtype))
    for name, factor in factors.items():
        out[name] = (out[name] * factor).astype(out[name].dtype)
    return out
```

```python
from contextlib import ExitStack, contextmanager

import numpy as np

import concourse.bass as bass
from concourse import mybir

P = 128
F32 = mybir.dt.float32
I32 = mybir.dt.int32
ALU = mybir.AluOpType
ACT = mybir.ActivationFunctionType
AX_X = mybir.AxisListType.X
LANES = (0, 1)
LN_EPS = 1e-5


class Loop:

    def __init__(self, nc, items, name):
        self.nc, self.items, self.name = nc, items, name
        self.queues = {e: [] for e in ("sync", "scalar", "vector", "gpsimd", "tensor")}
        self.sems, self.unit, self.lag = {}, {}, 0
        self.software = set()

    def step(self, engine, emit, reads=(), frees=(), done=None, dma=False, apart=False):
        if done is not None:
            self.sems[done] = self.nc.alloc_semaphore(f"{self.name}_{done}")
            self.unit[done] = 16 if dma else 1
            if engine == "gpsimd" and dma:
                self.software.add(done)
        assert not self.software & set(frees)
        waits = [(n, 1 if n in self.software else 2) for n in reads] + [(n, 1) for n in frees]
        self.queues[engine].append((emit, waits, done, apart or engine == "sync", self.lag))

    def run(self):
        passed = self.nc.alloc_semaphore(f"{self.name}_passed")
        with self.nc.Block() as block:
            for engine, queue in self.queues.items():
                if queue:
                    self._engine(block, engine, queue, passed)
        self.nc.clear_and_free_semaphores([passed, *self.sems.values()])
        self.nc.all_engine_barrier()

    def _engine(self, block, engine, queue, passed):
        decorate = {"sync": block.sync, "scalar": block.scalar, "vector": block.vector,
                    "gpsimd": block.gpsimd, "tensor": block.tensor}[engine]
        depth = max(q[-1] for qs in self.queues.values() for q in qs)
        results = [q[2] for q in queue if q[2] is not None]

        def work(eng, turn, due):
            for emit, waits, done, apart, lag in queue:
                if isinstance(turn, int) and not 0 <= turn - lag < self.items:
                    continue
                for n, ahead in waits:
                    eng.wait_ge(self.sems[n], due(lag, ahead, self.unit[n]))
                if apart and waits:
                    eng.sem_inc(passed, 1)
                last = emit(eng, turn - lag)
                if done is not None:
                    last.then_inc(self.sems[done], self.unit[done])

        def body(eng):
            for n in results:
                if n not in self.software:
                    eng.sem_inc(self.sems[n], self.unit[n])
            for turn in range(depth):
                work(eng, turn, lambda lag, ahead, u, turn=turn: (turn - lag + ahead) * u)
            with eng.Fori(depth, self.items) as turn:
                need = sorted({(lag, ahead, self.unit[n]) for _, w, _, _, lag in queue for n, ahead in w})
                regs = {k: eng.snap((turn + (k[1] - k[0])) * k[2]) for k in need}
                work(eng, turn, lambda *k: regs[k])
            for turn in range(self.items, self.items + depth):
                work(eng, turn, lambda lag, ahead, u, turn=turn: (turn - lag + ahead) * u)
            for n in results:
                if self.unit[n] == 16:
                    eng.wait_ge(self.sems[n], 16 * (self.items + (n not in self.software)))
        decorate(body)


@contextmanager
def memory(nc, phase):
    with ExitStack() as stack:
        def sb(name, shape, dt=F32):
            return stack.enter_context(nc.sbuf_tensor(f"{phase}_{name}", list(shape), dt))

        def ps(name, shape):
            return stack.enter_context(nc.psum_tensor(f"{phase}_{name}", list(shape), F32))
        yield sb, ps


def bc(ap, dim, n):
    return ap.unsqueeze(dim).broadcast_to([*ap.shape[:dim], n, *ap.shape[dim:]])


class LayerNorm:

    def __init__(self, sb, name, half):
        self.st, self.mv = sb(f"{name}_st", [P, 6]), sb(f"{name}_mv", [P, 2])
        self.ve, self.rstd, self.half = sb(f"{name}_ve", [P, 1]), sb(f"{name}_rs", [P, 1]), half

    def add(self, lp, tag, src, reads, out, frees=()):
        lp.step("vector", lambda e, t: e.bn_stats(self.st[:], src), reads, done=f"st_{tag}")
        lp.step("vector", lambda e, t: e.bn_aggr(self.mv[:], self.st[:]), [f"st_{tag}"], done=f"mv_{tag}",
                apart=True)
        lp.step("vector", lambda e, t: e.tensor_scalar(self.ve[:], self.mv[:, 1:2], LN_EPS, None, ALU.add),
                [f"mv_{tag}"], done=f"ve_{tag}")
        lp.step("gpsimd", lambda e, t: e.tensor_tensor(self.rstd[:], self.ve[:], self.half, ALU.pow),
                [f"ve_{tag}"], done=f"rs_{tag}")
        lp.step("vector", lambda e, t: e.tensor_scalar(out, src, self.mv[:, 0:1], self.rstd[:, 0:1],
                                                       ALU.subtract, ALU.mult),
                [f"rs_{tag}"], frees, done=f"ln_{tag}")


def const_layout(T=4096, C=256, heads=16, experts=8, slots=72):
    p, nt = np.arange(P), T // P
    e, t = np.divmod(np.arange(experts * nt), nt)
    return {
        "ident": np.eye(P),
        "half": np.full((P, 1), -0.5),
        "head_of_16": ((p % 64) // 16)[:, None] == np.arange(4),
        "before": p[:, None] < p[None, :],
        "ones": np.ones((P, P)),
        "rank": np.tile(experts - np.arange(experts), (P, 1)),
        "goes_on": np.tile(t > 0, (P, 1)),
        "one_e": np.ones((P, experts)),
        "slot": np.tile(np.arange(slots), (P, 1)),
        "causal": p[:, None] <= p[None, :],
        "own_head": (p // 32)[:, None] == (np.arange(64) // 16),
        "row": np.tile(p, (P, 1)),
        "quarter": np.where(p % 32 < 16, 0.25, 0.0)[:, None],
        "quarter_rad": np.where(p % 32 < 16, np.pi / 2, 0.0)[:, None],
    }


def build(nc, A, dram):
    T, C = A["x"].shape
    KC = C // P
    NT = T // P
    E = A["w1"].shape[0]
    SLOTS = 2 * (T * 2 // P + E) // 2
    x1, x2 = dram("x1", [T, C], F32), dram("x2", [T, C], F32)
    xn1, ysh = dram("xn1", [T, C], F32), dram("ysh", [T, C], F32)
    xg, yg = dram("xg", [SLOTS * P, C], F32), dram("yg", [SLOTS * P, C], F32)
    with ExitStack() as keep:
        def sb(name, shape, dt=F32):
            return keep.enter_context(nc.sbuf_tensor(name, list(shape), dt))
        lay = const_layout(T, C, HEADS, E, SLOTS)
        widths = {n: v.shape[1] for n, v in lay.items()}
        consts = sb("consts", [P, sum(widths.values())])
        K, at = {}, 0
        for n, w in widths.items():
            K[n] = consts[:, at:at + w]
            at += w
        load(nc, [(consts[:], A["consts"])])
        window_attention(nc, A, x1, K["ident"], K, T, C, KC, NT)
        with ExitStack() as moe:
            def sb2(name, shape, dt=F32):
                return moe.enter_context(nc.sbuf_tensor(name, list(shape), dt))
            logits = sb2("logits", [P, NT, E])
            weight, place = sb2("weight", [P, 2, NT]), sb2("place", [P, 2, NT], I32)
            expert = sb2("expert", [P, SLOTS], I32)
            shared_expert(nc, A, x1, xn1, ysh, logits, K, T, C, KC, NT, E)
            route(nc, logits, weight, place, expert, K, NT, E, SLOTS)
            dispatch(nc, xn1, xg, place, T, C, NT, SLOTS)
            experts(nc, A, xg, yg, expert, K, C, KC, E, SLOTS)
            combine(nc, x1, ysh, yg, weight, place, x2, K, T, C, NT)
        x3, xn3T = dram("x3", [T, C], F32), dram("xn3T", [C, T], F32)
        linear_attention(nc, A, x2, x3, xn3T, K, T, C, KC)
        gated_recurrence(nc, A, x3, xn3T, K, T, C, KC)


def load(nc, pairs):
    with nc.semaphore("load_sp") as s0, nc.semaphore("load_act") as s1, nc.Block() as block:
        def queue(e, part, sem):
            for dst, src in part:
                e.dma_start(dst, src).then_inc(sem, 16)
            e.wait_ge(sem, 16 * len(part))

        @block.sync
        def _(e):
            queue(e, pairs[0::2], s0)

        @block.scalar
        def _(e):
            queue(e, pairs[1::2], s1)
    nc.clear_and_free_semaphores([])
    nc.all_engine_barrier()


HEADS, WIN = 16, 64


def window_attention(nc, A, x1, ident, K, T, C, KC, NT):
    D = C // HEADS
    NB = HEADS // 2
    with memory(nc, "wa") as (sb, ps):
        wqkv, wp = sb("wqkv", [P, KC, 3 * C]), sb("wp", [P, KC, C])
        hm, half = K["head_of_16"], K["half"]
        lanes = []
        for L in LANES:
            d = {n: sb(f"{n}{L}", s) for n, s in (
                ("xa", [P, C]), ("xr", [P, C]), ("xn", [P, C]), ("xnT", [P, KC, P]), ("qT", [P, KC, P]),
                ("km", [P, KC, 4, P]), ("mx", [P, HEADS]), ("pr", [P, 2, 512]), ("pT", [P, NB, P]),
                ("rec", [P, HEADS]), ("yn", [P, C]), ("yT", [P, KC, P]), ("zn", [P, C]), ("xo", [P, C]),
                ("vb", [P, 2, NB, 2, D + 1]))}
            d["ln1"], d["ln2"] = LayerNorm(sb, f"lna{L}", half), LayerNorm(sb, f"lnb{L}", half)
            d["bank"] = [ps(f"bank{4 * L + i}", [P, 512]) for i in range(2)]
            d["S"] = ps(f"S{L}", [P, 2, 512])
            lanes.append(d)
        load(nc, [(wqkv[:], A["w_attnT"].rearrange("(k p) n -> p k n", p=P)),
                  (wp[:], A["w_projT"].rearrange("(k p) n -> p k n", p=P))])
        with nc.semaphore("vbz") as z, nc.Block() as block:
            @block.vector
            def _(e):
                for d in lanes:
                    e.memset(d["vb"][:], 0.0).then_inc(z, 1)
                e.wait_ge(z, 2)
                for d in lanes:
                    for w in range(2):
                        for h2 in range(2):
                            e.memset(d["vb"][64 * h2:64 * h2 + 64, w, :, h2, D:D + 1], 1.0)
        nc.clear_and_free_semaphores([])
        nc.all_engine_barrier()

        lp = Loop(nc, NT // 2, "wa")

        def rows(dr, t, L):
            return dr[bass.ds(t * 2 * P + L * P, P), :]

        def s_load(L):
            d = lanes[L]
            lp.step("sync", lambda e, t: e.dma_start(d["xa"][:], rows(A["x"], t, L)), frees=[f"ln_1{L}"],
                    done=f"xa{L}", dma=True)

        def s_load_r(L):
            d = lanes[L]
            lp.step("sync", lambda e, t: e.dma_start(d["xr"][:], rows(A["x"], t, L)), frees=[f"xo{L}"],
                    done=f"xr{L}", dma=True)

        def s_ln1(L):
            d = lanes[L]
            d["ln1"].add(lp, f"1{L}", d["xa"][:], [f"xa{L}"], d["xn"][:], frees=[f"xnTp{L}"])

        def s_xT(L):
            d = lanes[L]
            b0 = d["bank"][0]

            def tr(e, t):
                for k in range(KC):
                    i = e.transpose(b0[:, k * P:(k + 1) * P], d["xn"][:, k * P:(k + 1) * P], ident)
                return i
            lp.step("tensor", tr, [f"ln_1{L}"], frees=[f"pTa{L}"], done=f"xnTp{L}")
            lp.step("scalar", lambda e, t: e.copy(d["xnT"][:], b0[:, 0:C].rearrange("p (k n) -> p k n", k=KC)),
                    [f"xnTp{L}"], frees=[f"k{L}"], done=f"xnT{L}")

        def s_qkv(L):
            d = lanes[L]
            b0, b1 = d["bank"]

            def proj(out, col):
                def f(e, t):
                    for c in range(KC):
                        for k in range(KC):
                            i = e.matmul(out[:, c * P:(c + 1) * P], wqkv[:, k, col + c * P:col + (c + 1) * P],
                                         d["xnT"][:, k, :], start=(k == 0), stop=(k == KC - 1))
                    return i
                return f

            def v(e, t):
                for k in range(KC):
                    i = e.matmul(b1[:, C:2 * C], d["xnT"][:, k, :], wqkv[:, k, 2 * C:3 * C],
                                 start=(k == 0), stop=(k == KC - 1))
                return i
            lp.step("tensor", proj(b1[:, 0:C], 0), [f"xnT{L}"], frees=[f"pTb{L}"])
            lp.step("tensor", v, done=f"v{L}")
            lp.step("tensor", proj(b0[:, C:2 * C], C), done=f"k{L}")
            lp.step("scalar", lambda e, t: e.copy(d["qT"][:], b1[:, 0:C].rearrange("p (k n) -> p k n", k=KC)),
                    [f"v{L}"], frees=[f"S{L}"], done=f"qT{L}")

            def km(e, t):
                for c in range(KC):
                    i = e.tensor_tensor(d["km"][:, c], bc(b0[:, C + c * P:C + (c + 1) * P], 1, 4),
                                        bc(hm, 2, P), ALU.mult)
                return i
            lp.step("vector", km, [f"k{L}"], frees=[f"S{L}"], done=f"km{L}")

            def vb(e, t):
                for w in range(2):
                    for h2 in range(2):
                        src = b1[64 * w:64 * w + 64, C:2 * C].rearrange("p (b h d) -> p b h d", b=NB, h=2)
                        i = e.copy(d["vb"][64 * h2:64 * h2 + 64, w, :, h2, 0:D], src[:, :, h2, :])
                return i
            lp.step("scalar", vb, frees=[f"pv{L}"], done=f"vb{L}")

        def s_scores(L):
            d = lanes[L]
            S = d["S"]

            def sc(e, t):
                for c in range(KC):
                    for r in range(2):
                        for w in range(2):
                            i = e.matmul(S[64 * w:64 * w + 64, r, c * 256:(c + 1) * 256],
                                         d["qT"][64 * r:64 * r + 64, c, 64 * w:64 * w + 64],
                                         d["km"][64 * r:64 * r + 64, c, :, 64 * w:64 * w + 64],
                                         start=True, stop=True)
                return i
            lp.step("tensor", sc, [f"qT{L}", f"km{L}"], frees=[f"ln_2{L}"], done=f"S{L}", apart=True)
            S3 = S[:].rearrange("p r (h k) -> p (r h) k", k=WIN)
            pr3 = d["pr"][:].rearrange("p r (h k) -> p (r h) k", k=WIN)
            lp.step("vector", lambda e, t: e.tensor_reduce(d["mx"][:], S3, AX_X, ALU.max), [f"S{L}"], done=f"mx{L}")
            lp.step("vector", lambda e, t: e.tensor_tensor(pr3, S3, bc(d["mx"][:], 2, WIN), ALU.subtract),
                    [f"mx{L}"], frees=[f"pTp{L}"], done=f"sub{L}")
            lp.step("scalar", lambda e, t: e.activation(d["pr"][:], d["pr"][:], ACT.Exp, scale=float(D) ** -0.5),
                    [f"sub{L}"], done=f"exp{L}")

        def s_pT(L):
            d = lanes[L]

            def tr(e, t):
                for b in range(NB):
                    i = e.transpose(d["bank"][b // 4][:, (b % 4) * P:(b % 4 + 1) * P],
                                    d["pr"][:, b // 4, (b % 4) * P:(b % 4 + 1) * P], ident)
                return i
            lp.step("tensor", tr, [f"exp{L}", f"vb{L}"], done=f"pTp{L}")
            for n, e_, b in (("pTa", "scalar", 0), ("pTb", "vector", 1)):
                def cp(e, t, b=b):
                    f = e.copy if b == 0 else e.tensor_copy
                    return f(d["pT"][:, 4 * b:4 * b + 4, :], d["bank"][b][:].rearrange("p (b n) -> p b n", b=4))
                lp.step(e_, cp, [f"pTp{L}"], frees=[f"pv{L}"], done=f"{n}{L}")

        def s_pv(L):
            d = lanes[L]
            Y = d["S"][:, 0, 0:HEADS * (D + 1)]

            def pv(e, t):
                for c in range(KC):
                    for r in range(2):
                        for j in range(2):
                            bs, bv = r * 4 + c * 2 + j, c * 4 + r * 2 + j
                            for w in range(2):
                                i = e.matmul(Y[64 * w:64 * w + 64, bv * 34:(bv + 1) * 34],
                                             d["pT"][:, bs, 64 * w:64 * w + 64],
                                             d["vb"][:, w, bv].rearrange("p h d -> p (h d)"),
                                             start=True, stop=True)
                return i
            lp.step("tensor", pv, [f"pTa{L}", f"pTb{L}", f"sub{L}"], done=f"pv{L}")
            Y3 = Y.rearrange("p (h d) -> p h d", h=HEADS)
            lp.step("vector", lambda e, t: e.reciprocal(d["rec"][:], Y3[:, :, D]), [f"pv{L}"], done=f"rec{L}")
            lp.step("vector", lambda e, t: e.tensor_tensor(d["yn"][:].rearrange("p (h d) -> p h d", h=HEADS),
                                                           Y3[:, :, 0:D], bc(d["rec"][:], 2, D), ALU.mult),
                    [f"rec{L}"], done=f"yn{L}")

        def s_proj(L):
            d = lanes[L]
            B = d["S"]

            def tr(e, t):
                for k in range(KC):
                    i = e.transpose(B[:, 1, k * P:(k + 1) * P], d["yn"][:, k * P:(k + 1) * P], ident)
                return i
            lp.step("tensor", tr, [f"yn{L}"], done=f"yTp{L}")
            lp.step("scalar", lambda e, t: e.copy(d["yT"][:], B[:, 1, 0:C].rearrange("p (k n) -> p k n", k=KC)),
                    [f"yTp{L}"], done=f"yT{L}")

            def z(e, t):
                for k in range(KC):
                    i = e.matmul(B[:, 1, C:2 * C], d["yT"][:, k, :], wp[:, k, :], start=(k == 0), stop=(k == KC - 1))
                return i
            lp.step("tensor", z, [f"yT{L}"], done=f"z{L}")
            d["ln2"].add(lp, f"2{L}", B[:, 1, C:2 * C], [f"z{L}"], d["zn"][:], frees=[f"xo{L}"])
            lp.step("gpsimd", lambda e, t: e.tensor_tensor(d["xo"][:], d["zn"][:], d["xr"][:], ALU.add),
                    [f"ln_2{L}", f"xr{L}"], frees=[f"out{L}"], done=f"xo{L}")
            lp.step("sync", lambda e, t: e.dma_start(rows(x1, t, L), d["xo"][:]), [f"xo{L}"], done=f"out{L}", dma=True)

        for stage in (s_load, s_load_r, s_ln1, s_xT, s_qkv, s_scores, s_pT, s_pv, s_proj):
            for L in LANES:
                stage(L)
        lp.run()


def tile_rows(dr, t, L, n=P):
    return dr[bass.ds(t * 2 * n + L * n, n), :]


def chunks(ap, k):
    return ap.rearrange("p (k n) -> p k n", k=k)


def transposes(lp, L, tag, src, bank, dst, ident, reads, frees_pe=(), frees_dst=(), engine="scalar", n=2):
    def tr(e, t):
        for k in range(n):
            i = e.transpose(bank[:, k * P:(k + 1) * P], src[:, k * P:(k + 1) * P], ident)
        return i

    def cp(e, t):
        return (e.copy if engine == "scalar" else e.tensor_copy)(dst, chunks(bank[:, 0:n * P], n))
    lp.step("tensor", tr, reads, frees_pe, done=f"{tag}p{L}")
    lp.step(engine, cp, [f"{tag}p{L}"], frees_dst, done=f"{tag}{L}")


def shared_expert(nc, A, x1, xn1, ysh, logits, K, T, C, KC, NT, E):
    F = A["sw1"].shape[1]
    KF = F // P
    with memory(nc, "se") as (sb, ps):
        sw1, sw3 = sb("sw1", [P, KC, F]), sb("sw3", [P, KC, F])
        sw2, gate = sb("sw2", [P, KF, C]), sb("gate", [P, KC, E])
        load(nc, [(sw1[:], A["sw1"].rearrange("(k p) n -> p k n", p=P)),
                  (sw3[:], A["sw3"].rearrange("(k p) n -> p k n", p=P)),
                  (sw2[:], A["sw2"].rearrange("(k p) n -> p k n", p=P)),
                  (gate[:], A["gateT"].rearrange("(k p) n -> p k n", p=P))])
        lp = Loop(nc, NT // 2, "se")
        lanes = []
        for L in LANES:
            d = {n: sb(f"{n}{L}", s) for n, s in (
                ("xa", [P, C]), ("xn", [P, C]), ("xnT", [P, KC, P]), ("g", [P, KF, P]), ("gT", [P, KF, P]),
                ("yo", [P, C]))}
            d["ln"] = LayerNorm(sb, f"ln{L}", K["half"])
            d["b"] = [ps(f"b{L}{i}", [P, 512]) for i in range(4)]
            lanes.append(d)

        def s_in(L, d):
            lp.step("sync", lambda e, t: e.dma_start(d["xa"][:], tile_rows(x1, t, L)), frees=[f"ln_1{L}"],
                    done=f"xa{L}", dma=True)

        def s_ln(L, d):
            d["ln"].add(lp, f"1{L}", d["xa"][:], [f"xa{L}"], d["xn"][:], frees=[f"xnTp{L}", f"xno{L}"])
            lp.step("sync", lambda e, t: e.dma_start(tile_rows(xn1, t, L), d["xn"][:]), [f"ln_1{L}"],
                    done=f"xno{L}", dma=True)

        def s_xT(L, d):
            transposes(lp, L, "xnT", d["xn"], d["b"][0], d["xnT"][:], K["ident"], [f"ln_1{L}"],
                       frees_pe=[f"lg{L}"], frees_dst=[f"h{L}"])

        def s_h(L, d):
            def up(w, out):
                def f(e, t):
                    for c in range(KF):
                        for k in range(KC):
                            i = e.matmul(out[:, c * P:(c + 1) * P], w[:, k, c * P:(c + 1) * P], d["xnT"][:, k, :],
                                         start=(k == 0), stop=(k == KC - 1))
                    return i
                return f

            def lg(e, t):
                for k in range(KC):
                    i = e.matmul(d["b"][0][:, C:C + E], d["xnT"][:, k, :], gate[:, k, :],
                                 start=(k == 0), stop=(k == KC - 1))
                return i
            lp.step("tensor", lg, [f"xnT{L}"], done=f"lgp{L}")
            lp.step("tensor", up(sw1, d["b"][1]), frees=[f"g{L}"], done=f"h1{L}")
            lp.step("tensor", up(sw3, d["b"][2]), frees=[f"gT{L}"], done=f"h{L}")
            lp.step("vector", lambda e, t: e.tensor_copy(
                logits[:].rearrange("p (t l) e -> p t l e", l=2)[:, bass.ds(t, 1), L, :],
                d["b"][0][:, C:C + E].unsqueeze(1)), [f"lgp{L}"], done=f"lg{L}")
            lp.step("scalar", lambda e, t: e.activation(d["g"][:], chunks(d["b"][1][:, 0:F], KF), ACT.Silu),
                    [f"h1{L}"], frees=[f"gT{L}"], done=f"g{L}")
            lp.step("vector", lambda e, t: e.tensor_tensor(d["gT"][:], d["g"][:], chunks(d["b"][2][:, 0:F], KF),
                                                           ALU.mult), [f"g{L}", f"h{L}"], frees=[f"y{L}"],
                    done=f"gT{L}")

        def s_y(L, d):
            def y(e, t):
                for c in range(KF):
                    i = e.matmul(d["b"][3][:, 0:C], d["gT"][:, c, :], sw2[:, c, :], start=(c == 0),
                                 stop=(c == KF - 1))
                return i
            lp.step("tensor", y, [f"gT{L}"], frees=[f"yo{L}"], done=f"y{L}")
            lp.step("scalar", lambda e, t: e.copy(d["yo"][:], d["b"][3][:, 0:C]), [f"y{L}"], frees=[f"yst{L}"],
                    done=f"yo{L}")
            lp.step("sync", lambda e, t: e.dma_start(tile_rows(ysh, t, L), d["yo"][:]), [f"yo{L}"],
                    done=f"yst{L}", dma=True)

        for stage in (s_in, s_ln, s_xT, s_h, s_y):
            for L in LANES:
                stage(L, lanes[L])
        lp.run()


class Chain:

    def __init__(self, nc, name):
        self.nc, self.name, self.steps = nc, name, []

    def __call__(self, engine, emit):
        self.steps.append((engine, emit))

    def run(self):
        sem = self.nc.alloc_semaphore(self.name)
        with self.nc.Block() as block:
            for engine in sorted({e for e, _ in self.steps}):
                def body(eng, engine=engine):
                    for n, (on, emit) in enumerate(self.steps):
                        if on == engine:
                            eng.wait_ge(sem, n)
                            emit(eng).then_inc(sem, 1)
                {"scalar": block.scalar, "vector": block.vector, "gpsimd": block.gpsimd,
                 "tensor": block.tensor}[engine](body)
        self.nc.clear_and_free_semaphores([sem])
        self.nc.all_engine_barrier()


def route(nc, logits, weight, place, expert, K, NT, E, SLOTS):
    with memory(nc, "ro") as (sb, ps):
        m1, m2, top = sb("m1", [P, NT]), sb("m2", [P, NT]), sb("top", [P, NT])
        eq, ex = sb("eq", [P, NT, E]), sb("ex", [P, NT, E])
        pick = [sb("pick0", [P, NT, E]), sb("pick1", [P, NT, E])]
        rest, rs, dm = sb("rest", [P, NT, E]), sb("rs", [P, NT]), sb("dm", [P, NT])
        mask, inc, pos = sb("mask", [P, E, NT]), sb("inc", [P, E * NT]), sb("pos", [P, E, NT])
        tot = sb("tot", [P, E * NT])
        bi, blk, cum, first = sb("bi", [P, E], I32), sb("blk", [P, E]), sb("cum", [P, E]), sb("first", [P, E])
        cmp, se = sb("cmp", [P, SLOTS, E]), sb("se", [P, SLOTS])
        pfx, ptot = ps("pfx", [P, 512]), ps("ptot", [P, 512])
        ch = Chain(nc, "route")

        def tt(out, a, b, op):
            ch("vector", lambda e: e.tensor_tensor(out, a, b, op))

        def red(out, a, op):
            ch("vector", lambda e: e.tensor_reduce(out, a, AX_X, op))

        def one_hot(src, m, out):
            red(m[:], src[:], ALU.max)
            tt(eq[:], src[:], bc(m[:], 2, E), ALU.is_equal)
            tt(eq[:], eq[:], bc(K["rank"], 1, NT), ALU.mult)
            red(top[:], eq[:], ALU.max)
            tt(out[:], eq[:], bc(top[:], 2, E), ALU.is_equal)

        one_hot(logits, m1, pick[0])
        ch("vector", lambda e: e.scalar_tensor_tensor(rest[:], pick[0][:], -3.0e38, logits[:], ALU.mult, ALU.add))
        one_hot(rest, m2, pick[1])
        tt(ex[:], logits[:], bc(m1[:], 2, E), ALU.subtract)
        ch("scalar", lambda e: e.activation(ex[:], ex[:], ACT.Exp))
        red(rs[:], ex[:], ALU.add)
        ch("vector", lambda e: e.reciprocal(weight[:, 0, :], rs[:]))
        tt(dm[:], m2[:], m1[:], ALU.subtract)
        ch("scalar", lambda e: e.activation(dm[:], dm[:], ACT.Exp))
        tt(weight[:, 1, :], dm[:], weight[:, 0, :], ALU.mult)
        tt(mask[:], pick[0][:].rearrange("p t e -> p e t"), pick[1][:].rearrange("p t e -> p e t"), ALU.add)
        flat = mask[:].rearrange("p e t -> p (e t)")
        ch("tensor", lambda e: e.matmul(pfx[:, 0:E * NT], K["before"], flat, start=True, stop=True))
        ch("tensor", lambda e: e.matmul(ptot[:, 0:E * NT], K["ones"], flat, start=True, stop=True))
        ch("vector", lambda e: e.tensor_copy(tot[:], ptot[:, 0:E * NT]))
        ch("vector", lambda e: e.tensor_tensor_scan(inc[:], K["goes_on"], tot[:], 0.0, ALU.mult, ALU.add))
        last = inc[:].rearrange("p (e t) -> p e t", e=E)[:, :, NT - 1]
        ch("vector", lambda e: e.tensor_scalar(bi[:], last, float(P - 1), None, ALU.add))
        ch("vector", lambda e: e.tensor_scalar(bi[:], bi[:], 7, None, ALU.logical_shift_right))
        ch("vector", lambda e: e.tensor_copy(blk[:], bi[:]))
        ch("vector", lambda e: e.tensor_tensor_scan(cum[:], K["one_e"], blk[:], 0.0, ALU.mult, ALU.add))
        tt(first[:], cum[:], blk[:], ALU.subtract)
        ch("vector", lambda e: e.tensor_scalar(first[:], first[:], float(P), None, ALU.mult))
        tt(inc[:], inc[:], tot[:], ALU.subtract)
        tt(inc[:], inc[:], pfx[:, 0:E * NT], ALU.add)
        tt(pos[:], inc[:].rearrange("p (e t) -> p e t", e=E), bc(first[:], 2, NT), ALU.add)
        for k in range(2):
            tt(eq[:], pick[k][:], pos[:].rearrange("p e t -> p t e"), ALU.mult)
            red(top[:], eq[:], ALU.add)
            ch("vector", lambda e, k=k: e.tensor_copy(place[:, k, :], top[:]))
        tt(cmp[:], bc(cum[:], 1, SLOTS), bc(K["slot"], 2, E), ALU.is_le)
        red(se[:], cmp[:], ALU.add)
        ch("vector", lambda e: e.tensor_scalar(expert[:], se[:], float(E - 1), None, ALU.min))
        ch.run()


def dispatch(nc, xn1, xg, place, T, C, NT, SLOTS):
    R = SLOTS // 8
    with memory(nc, "dp") as (sb, ps):
        zero = sb("zero", [P, R * C])
        with nc.semaphore("xz") as z, nc.semaphore("xzd") as zd, nc.Block() as block:
            @block.vector
            def _(e):
                e.memset(zero[:], 0.0).then_inc(z, 1)

            @block.sync
            def _(e):
                e.wait_ge(z, 1)
                rows = xg.rearrange("(q p r) c -> q p (r c)", q=8, p=P)
                for q in range(8):
                    e.dma_start(rows[q], zero[:]).then_inc(zd, 16)
                e.wait_ge(zd, 16 * 8)
        nc.clear_and_free_semaphores([])
        nc.all_engine_barrier()
        lp = Loop(nc, NT // 2, "dp")
        for L in LANES:
            row, idx = sb(f"row{L}", [P, C]), sb(f"idx{L}", [P, 2], I32)
            lp.step("sync", lambda e, t, row=row, L=L: e.dma_start(row[:], tile_rows(xn1, t, L)),
                    frees=[f"sent{L}"], done=f"row{L}", dma=True)

            def idx_of(e, t, idx=idx, L=L):
                return e.tensor_copy(idx[:].unsqueeze(2), place[:].rearrange("p k (t l) -> p k t l", l=2)
                                     [:, :, bass.ds(t, 1), L])
            lp.step("gpsimd", idx_of, frees=[f"sent{L}"], done=f"idx{L}", apart=True)
            for k in range(2):
                lp.step("gpsimd", lambda e, t, k=k, idx=idx, row=row: e.indirect_dma_start(
                    xg, bass.IndirectOffsetOnAxis(ap=idx[:, k:k + 1], axis=0), row[:], None),
                    [f"row{L}", f"idx{L}"], done=f"s{k}{L}", dma=True, apart=True)
            lp.step("scalar", lambda e, t: e.nop(), [f"s0{L}", f"s1{L}"], done=f"sent{L}", apart=True)
        lp.run()


def experts(nc, A, xg, yg, expert, K, C, KC, E, SLOTS):
    F = A["w1"].shape[2]
    KF = -(-F // P)
    FR = F - (KF - 1) * P
    H = F // 2
    with memory(nc, "ex") as (sb, ps):
        w13, w2 = sb("w13", [P, E, KC, 2 * F]), sb("w2", [P, E, KF, C])
        pairs = []
        for x in range(E):
            pairs += [(w13[:, x, :, 0:F], A["w1"][x].rearrange("(k p) n -> p k n", p=P)),
                      (w13[:, x, :, F:2 * F], A["w3"][x].rearrange("(k p) n -> p k n", p=P)),
                      (w2[:, x, 0:KF - 1], A["w2"][x, 0:(KF - 1) * P].rearrange("(k p) n -> p k n", p=P)),
                      (w2[0:FR, x, KF - 1], A["w2"][x, (KF - 1) * P:F])]
        load(nc, pairs)
        lp = Loop(nc, SLOTS // 2, "ex")
        hb = [ps(f"hb{i}", [P, 512]) for i in range(4)]
        tb, xb, yb = [ps("tb0", [P, 512]), ps("tb1", [P, 512])], ps("xb", [P, 512]), ps("yb", [P, 512])
        lanes = [{n: sb(f"{n}{L}", s) for n, s in (
            ("xa", [P, C]), ("xT", [P, KC, P]), ("g", [P, F]), ("gT", [P, KF, P]), ("yo", [P, C]))} for L in LANES]
        which = {}

        def s_in(L, d):
            lp.step("sync", lambda e, t: e.dma_start(d["xa"][:], tile_rows(xg, t, L)), frees=[f"xTp{L}"],
                    done=f"xa{L}", dma=True)

        def s_xT(L, d):
            transposes(lp, L, "xT", d["xa"], xb, d["xT"][:], K["ident"],
                       [f"xa{L}"] + (["xT0"] if L else []), frees_pe=[] if L else ["xT1"], frees_dst=[f"h1{L}"])

        def s_h(L, d):
            def up(half, part):
                def f(e, t):
                    if half == 0 and part == 0:
                        which[L] = e.value_load(expert[0:1, bass.ds(2 * t + L, 1)], min_val=0, max_val=E - 1)
                    for k in range(KC):
                        i = e.matmul(hb[2 * half + part][:, 0:H], d["xT"][:, k, :],
                                     w13[:, bass.ds(which[L], 1), k, part * F + half * H:part * F + (half + 1) * H],
                                     start=(k == 0), stop=(k == KC - 1))
                    return i
                return f
            for half in range(2):
                lp.step("tensor", up(half, 0), [f"xT{L}"] + ([f"g{half}0"] if L else []),
                        frees=[] if L else [f"g{half}1"])
                lp.step("tensor", up(half, 1), done=f"h{half}{L}")
                g = d["g"][:, half * H:(half + 1) * H]
                lp.step("scalar", lambda e, t, g=g, half=half: e.activation(g, hb[2 * half][:, 0:H], ACT.Silu),
                        [f"h{half}{L}"], frees=[f"gTp{L}"], done=f"si{half}{L}")
                lp.step("vector", lambda e, t, g=g, half=half: e.tensor_tensor(g, g, hb[2 * half + 1][:, 0:H],
                                                                               ALU.mult),
                        [f"si{half}{L}"], done=f"g{half}{L}")

        def s_gT(L, d):
            def tr(e, t):
                for k in range(KF):
                    n = P if k < KF - 1 else FR
                    i = e.transpose(tb[k // 4][0:n, (k % 4) * P:(k % 4 + 1) * P], d["g"][:, k * P:k * P + n],
                                    K["ident"])
                return i
            lp.step("tensor", tr, [f"g1{L}"] + (["ta0", "tc0"] if L else []),
                    frees=[] if L else ["ta1", "tc1"], done=f"gTp{L}")
            lp.step("scalar", lambda e, t: e.copy(d["gT"][:, 0:4], chunks(tb[0][:], 4)), [f"gTp{L}"],
                    frees=[f"y{L}"], done=f"ta{L}")

            def rest(e, t):
                e.tensor_copy(d["gT"][:, 4, :], tb[1][:, 0:P])
                return e.tensor_copy(d["gT"][0:FR, 5, :], tb[1][0:FR, P:2 * P])
            lp.step("vector", rest, [f"gTp{L}"], frees=[f"y{L}"], done=f"tc{L}")

        def s_y(L, d):
            def y(e, t):
                for k in range(KF):
                    n = P if k < KF - 1 else FR
                    i = e.matmul(yb[:, 0:C], d["gT"][0:n, k, :], w2[0:n, bass.ds(which[L], 1), k, :],
                                 start=(k == 0), stop=(k == KF - 1))
                return i
            lp.step("tensor", y, [f"ta{L}", f"tc{L}"] + (["yo0"] if L else []), frees=[] if L else ["yo1"],
                    done=f"y{L}")
            lp.step("scalar", lambda e, t: e.copy(d["yo"][:], yb[:, 0:C]), [f"y{L}"], frees=[f"yst{L}"],
                    done=f"yo{L}")
            lp.step("sync", lambda e, t: e.dma_start(tile_rows(yg, t, L), d["yo"][:]), [f"yo{L}"],
                    done=f"yst{L}", dma=True)

        for stage in (s_in, s_xT, s_h, s_gT, s_y):
            for L in LANES:
                stage(L, lanes[L])
        lp.run()


def combine(nc, x1, ysh, yg, weight, place, x2, K, T, C, NT):
    with memory(nc, "co") as (sb, ps):
        lp = Loop(nc, NT // 2, "co")
        lanes = []
        for L in LANES:
            d = {n: sb(f"{n}{L}", [P, C]) for n in ("xr", "ys", "g0", "g1", "a0", "a1", "zn", "xo")}
            d["idx"], d["ln"] = sb(f"idx{L}", [P, 2], I32), LayerNorm(sb, f"ln{L}", K["half"])
            lanes.append(d)

        def s_in(L, d):
            lp.step("sync", lambda e, t: e.dma_start(d["xr"][:], tile_rows(x1, t, L)), frees=[f"xo{L}"],
                    done=f"xr{L}", dma=True)
            lp.step("sync", lambda e, t: e.dma_start(d["ys"][:], tile_rows(ysh, t, L)), frees=[f"a0{L}"],
                    done=f"ys{L}", dma=True)
            lp.step("gpsimd", lambda e, t: e.tensor_copy(
                d["idx"][:].unsqueeze(2), place[:].rearrange("p k (t l) -> p k t l", l=2)[:, :, bass.ds(t, 1), L]),
                frees=[f"a0{L}", f"a1{L}"], done=f"idx{L}", apart=True)
            for k in range(2):
                lp.step("gpsimd", lambda e, t, k=k: e.indirect_dma_start(
                    d[f"g{k}"][:], None, yg, bass.IndirectOffsetOnAxis(ap=d["idx"][:, k:k + 1], axis=0)),
                    [f"idx{L}"], frees=[f"a{k}{L}"], done=f"g{k}{L}", dma=True, apart=True)

        def s_sum(L, d):
            for k, src in ((0, "ys"), (1, "a0")):
                lp.step("vector", lambda e, t, k=k, src=src: e.scalar_tensor_tensor(
                    d[f"a{k}"][:], d[f"g{k}"][:],
                    weight[:].rearrange("p k (t l) -> p k t l", l=2)[:, k, bass.ds(t, 1), L],
                    d[src][:], ALU.mult, ALU.add), [f"g{k}{L}", f"ys{L}" if k == 0 else f"a0{L}"], done=f"a{k}{L}")
            d["ln"].add(lp, f"1{L}", d["a1"][:], [f"a1{L}"], d["zn"][:], frees=[f"xo{L}"])
            lp.step("gpsimd", lambda e, t: e.tensor_tensor(d["xo"][:], d["zn"][:], d["xr"][:], ALU.add),
                    [f"ln_1{L}", f"xr{L}"], frees=[f"out{L}"], done=f"xo{L}")
            lp.step("sync", lambda e, t: e.dma_start(tile_rows(x2, t, L), d["xo"][:]), [f"xo{L}"],
                    done=f"out{L}", dma=True)

        for stage in (s_in, s_sum):
            for L in LANES:
                stage(L, lanes[L])
        lp.run()


TWO_PI = 2 * np.pi
TURN_HI = 6.28125
TURN_MID = float(np.float32(round((TWO_PI - TURN_HI) * 2 ** 21) / 2 ** 21))
TURN_LO = float(TWO_PI - TURN_HI - TURN_MID)
TO_INT = 1.5 * 2 ** 23
PI_BELOW = float(np.nextafter(np.float32(np.pi), np.float32(0)))


def linear_attention(nc, A, x2, x3, xn3T, K, T, C, KC):
    S = T // 2
    CH = 4
    HD = C // HEADS
    with memory(nc, "la") as (sb, ps):
        wq, wk = sb("wq", [P, KC, 2 * C]), sb("wk", [P, KC, 2 * C])
        wv, wo = sb("wv", [P, KC, C]), sb("wo", [P, KC, C])
        g1, g2 = sb("g1", [P, KC, HD]), sb("g2", [HD, C])
        gamma, beta, theta = sb("gamma", [P, C]), sb("beta", [P, C]), sb("theta", [P, CH])

        def kcn(a):
            return a.rearrange("(k p) n -> p k n", p=P)
        load(nc, [(wq[:], kcn(A["Wq2"])), (wk[:], kcn(A["Wk2"])), (wv[:], kcn(A["Wv"])), (wo[:], kcn(A["Wo"])),
                  (g1[:], kcn(A["G1"])), (g2[:], A["G2"]), (gamma[:], A["gamma"].partition_broadcast(P)),
                  (beta[:], A["beta"].partition_broadcast(P)), (theta[:], A["theta2"])])
        pos = sb("pos", [P, P])
        ang, trn, red, cs = (sb(n, [P, CH, P]) for n in ("ang", "trn", "red", "cs"))
        lanes = []
        for L in LANES:
            d = {n: sb(f"{n}{L}", s) for n, s in (
                ("xa", [P, C]), ("xn", [P, C]), ("xnT", [P, KC, P]), ("t1", [HD, P]), ("gt", [P, C]),
                ("qs", [P, CH, P]), ("ks", [P, CH, P]), ("qT", [P, CH, P]), ("kT", [P, CH, P]), ("v", [P, C]),
                ("em", [P, 4, CH, P]), ("kt", [P, CH, P]), ("state", [P, CH, 64]), ("up", [P, CH, 64]),
                ("o", [P, C]), ("oT", [P, KC, P]), ("y", [P, C]), ("yn", [P, C]), ("zn", [P, C]), ("xo", [P, C]),
                ("w", [P, C]), ("wT", [P, KC, P]))}
            for n in ("ln0", "ln1", "ln2", "ln3"):
                d[n] = LayerNorm(sb, f"{n}{L}", K["half"])
            d["A"], d["B"] = ps(f"A{L}", [P, 512]), ps(f"B{L}", [P, 512])
            lanes.append(d)
        eb = ps("eb", [P, 4, 512])
        with nc.semaphore("la_state0") as z, nc.Block() as block:
            @block.vector
            def _(e):
                for d in lanes:
                    e.memset(d["state"][:], 0.0)
                e.tensor_copy(pos[:], K["row"]).then_inc(z, 1)
        nc.clear_and_free_semaphores([])
        nc.all_engine_barrier()
        lp = Loop(nc, S // P, "la")

        def rows(dr, t, L):
            return dr[bass.ds(t * P + L * S, P), :]

        def angles():
            def mul(e, t):
                for c in range(CH):
                    i = e.tensor_scalar(ang[:, c], pos[:], theta[:, c:c + 1], None, ALU.mult)
                return i
            lp.step("vector", mul, done="ang")
            lp.step("vector", lambda e, t: e.tensor_scalar(pos[:], pos[:], float(P), None, ALU.add), ["ang"],
                    done="pos")
            lp.step("vector", lambda e, t: e.tensor_scalar(trn[:], ang[:], float(1 / TWO_PI), K["quarter"],
                                                           ALU.mult, ALU.add), ["ang"], done="trn0")
            lp.step("vector", lambda e, t: e.tensor_scalar(trn[:], trn[:], TO_INT, TO_INT, ALU.add, ALU.subtract),
                    ["trn0"], done="trn")
            src, prev = ang, "trn"
            for n, part in (("hi", TURN_HI), ("mid", TURN_MID), ("lo", TURN_LO)):
                lp.step("vector", lambda e, t, src=src, part=part: e.scalar_tensor_tensor(
                    red[:], trn[:], -part, src[:], ALU.mult, ALU.add), [prev], frees=["cs"], done=n)
                src, prev = red, n
            lp.step("vector", lambda e, t: e.tensor_scalar(red[:], red[:], K["quarter_rad"], PI_BELOW,
                                                           ALU.add, ALU.min), ["lo"], done="cl")
            lp.step("vector", lambda e, t: e.tensor_scalar(red[:], red[:], -PI_BELOW, None, ALU.max), ["cl"],
                    done="red")
            lp.step("scalar", lambda e, t: e.activation(cs[:], red[:], ACT.Sin), ["red"], frees=["kT0", "kT1"],
                    done="cs")

        def s_in(L, d):
            lp.step("sync", lambda e, t: e.dma_start(d["xa"][:], rows(x2, t, L)), frees=[f"xo{L}"],
                    done=f"xa{L}", dma=True)
            d["ln0"].add(lp, f"0{L}", d["xa"][:], [f"xa{L}"], d["xn"][:], frees=[f"xnTp{L}"])

        def s_xT(L, d):
            transposes(lp, L, "xnT", d["xn"], d["B"], d["xnT"][:], K["ident"], [f"ln_0{L}"],
                       frees_pe=[f"wT{L}"], frees_dst=[f"v{L}"])

        def s_gate(L, d):
            def t1(e, t):
                for k in range(KC):
                    i = e.matmul(d["A"][0:HD, 0:P], g1[:, k, :], d["xnT"][:, k, :], start=(k == 0),
                                 stop=(k == KC - 1))
                return i
            lp.step("tensor", t1, [f"xnT{L}"], frees=[f"up{L}"], done=f"t1p{L}")
            lp.step("scalar", lambda e, t: e.copy(d["t1"][:], d["A"][0:HD, 0:P]), [f"t1p{L}"], done=f"t1{L}")
            lp.step("tensor", lambda e, t: e.matmul(d["A"][:, P:P + C], d["t1"][:], g2[:], start=True, stop=True),
                    [f"t1{L}"], done=f"g2{L}")
            lp.step("scalar", lambda e, t: e.activation(d["gt"][:], d["A"][:, P:P + C], ACT.Tanh, scale=0.5),
                    [f"g2{L}"], frees=[f"y{L}"], done=f"th{L}")
            lp.step("vector", lambda e, t: e.tensor_scalar(d["gt"][:], d["gt"][:], 0.5, 0.5, ALU.mult, ALU.add),
                    [f"th{L}"], done=f"gt{L}")

        def s_v(L, d):
            def v(e, t):
                for k in range(KC):
                    i = e.matmul(d["B"][:, C:2 * C], d["xnT"][:, k, :], wv[:, k, :], start=(k == 0),
                                 stop=(k == KC - 1))
                return i
            lp.step("tensor", v, [f"xnT{L}"], done=f"vp{L}")
            lp.step("scalar", lambda e, t: e.copy(d["v"][:], d["B"][:, C:2 * C]), [f"vp{L}"], frees=[f"ust{L}"],
                    done=f"v{L}")

        def s_qk(which):
            def stage(L, d):
                w = wq if which == "q" else wk

                def f(e, t):
                    for c in range(CH):
                        for k in range(KC):
                            i = e.matmul(d["A"][:, c * P:(c + 1) * P], w[:, k, c * P:(c + 1) * P],
                                         d["xnT"][:, k, :], start=(k == 0), stop=(k == KC - 1))
                    return i
                lp.step("tensor", f, [f"th{L}" if which == "q" else f"qs{L}"], done=f"{which}p{L}")
                lp.step("scalar", lambda e, t: e.activation(d[f"{which}s"][:], chunks(d["A"][:], CH), ACT.Silu),
                        [f"{which}p{L}"], frees=[f"{which}T{L}"], done=f"{which}s{L}")
                lp.step("gpsimd", lambda e, t: e.tensor_tensor(d[f"{which}T"][:], d[f"{which}s"][:], cs[:],
                                                               ALU.mult), [f"{which}s{L}", "cs"],
                        frees=[f"O{L}" if which == "q" else f"ktp{L}"], done=f"{which}T{L}")
            return stage

        def s_energy(L, d):
            def en(half):
                def f(e, t):
                    for c in range(CH):
                        for r in (2 * half, 2 * half + 1):
                            i = e.matmul(eb[:, r, c * P:(c + 1) * P], d["kT"][32 * r:32 * r + 32, c, :],
                                         d["qT"][32 * r:32 * r + 32, c, :], start=True, stop=True,
                                         tile_position=(32 * r, 0))
                    return i
                return f

            def em(half):
                def f(e, t):
                    for r in (2 * half, 2 * half + 1):
                        i = e.tensor_tensor(d["em"][:, r], chunks(eb[:, r], CH), bc(K["causal"], 1, CH), ALU.mult)
                    return i
                return f
            for half in range(2):
                lp.step("tensor", en(half), [f"qT{L}", f"kT{L}"] + ([f"em{half}0"] if L else []),
                        frees=[] if L else [f"em{half}1"], done=f"en{half}{L}")
                lp.step("vector", em(half), [f"en{half}{L}"], frees=[f"O{L}"], done=f"em{half}{L}")

        def s_kt(L, d):
            def tr(e, t):
                for c in range(CH):
                    i = e.transpose(d["A"][:, c * P:(c + 1) * P], d["kT"][:, c, :], K["ident"])
                return i
            lp.step("tensor", tr, done=f"ktp{L}")
            lp.step("scalar", lambda e, t: e.copy(d["kt"][:], chunks(d["A"][:], CH)), [f"ktp{L}"],
                    frees=[f"ust{L}"], done=f"kt{L}")

        def s_out(L, d):
            def o(e, t):
                for c in range(CH):
                    e.matmul(d["B"][:, c * 64:(c + 1) * 64], d["qT"][:, c, :], d["state"][:, c, :],
                             start=(c == 0), stop=False, skip_group_check=True)
                for c in range(CH):
                    for r in range(4):
                        h = 4 * c + r
                        i = e.matmul(d["B"][:, h * HD:(h + 1) * HD], d["em"][:, r, c, :],
                                     d["v"][:, h * HD:(h + 1) * HD], start=False, stop=(h == HEADS - 1),
                                     skip_group_check=True)
                return i
            lp.step("tensor", o, [f"em0{L}", f"em1{L}", f"v{L}"], frees=[f"st{L}"], done=f"O{L}")

            def u(e, t):
                for c in range(CH):
                    i = e.matmul(d["A"][:, c * 64:(c + 1) * 64], d["kt"][:, c, :], d["v"][:, c * 64:(c + 1) * 64],
                                 start=True, stop=True)
                return i
            lp.step("tensor", u, [f"kt{L}"], done=f"ust{L}")
            lp.step("vector", lambda e, t: e.tensor_copy(d["o"][:], d["B"][:, 0:C]), [f"O{L}"],
                    frees=[f"oTp{L}"], done=f"o{L}")
            lp.step("vector", lambda e, t: e.tensor_tensor(d["up"][:], chunks(d["A"][:, 0:C], CH),
                                                           bc(K["own_head"], 1, CH), ALU.mult), [f"ust{L}"],
                    done=f"up{L}")
            lp.step("vector", lambda e, t: e.tensor_tensor(d["state"][:], d["state"][:], d["up"][:], ALU.add),
                    [f"up{L}"], done=f"st{L}")

        def s_wo(L, d):
            transposes(lp, L, "oT", d["o"], d["B"], d["oT"][:], K["ident"], [f"o{L}"])

            def z(e, t):
                for k in range(KC):
                    i = e.matmul(d["B"][:, C:2 * C], d["oT"][:, k, :], wo[:, k, :], start=(k == 0),
                                 stop=(k == KC - 1))
                return i
            lp.step("tensor", z, [f"oT{L}"], done=f"z{L}")
            lp.step("vector", lambda e, t: e.tensor_tensor(d["y"][:], d["B"][:, C:2 * C], d["gt"][:], ALU.mult),
                    [f"z{L}", f"gt{L}"], done=f"y{L}")
            d["ln1"].add(lp, f"1{L}", d["y"][:], [f"y{L}"], d["yn"][:])
            lp.step("gpsimd", lambda e, t: e.tensor_tensor(d["yn"][:], d["yn"][:], gamma[:], ALU.mult),
                    [f"ln_1{L}"], done=f"ga{L}")
            lp.step("gpsimd", lambda e, t: e.tensor_tensor(d["yn"][:], d["yn"][:], beta[:], ALU.add),
                    [f"ga{L}"], done=f"be{L}")
            d["ln2"].add(lp, f"2{L}", d["yn"][:], [f"be{L}"], d["zn"][:])
            lp.step("gpsimd", lambda e, t: e.tensor_tensor(d["xo"][:], d["zn"][:], d["xa"][:], ALU.add),
                    [f"ln_2{L}"], frees=[f"out{L}"], done=f"xo{L}")
            lp.step("sync", lambda e, t: e.dma_start(rows(x3, t, L), d["xo"][:]), [f"xo{L}"], done=f"out{L}",
                    dma=True)

        def s_next(L, d):
            d["ln3"].add(lp, f"3{L}", d["xo"][:], [f"xo{L}"], d["w"][:])
            transposes(lp, L, "wT", d["w"], d["B"], d["wT"][:], K["ident"], [f"ln_3{L}"], frees_dst=[f"wst{L}"])
            lp.step("sync", lambda e, t: e.dma_start(
                xn3T.rearrange("(k p) n -> p k n", p=P)[:, :, bass.ds(t * P + L * S, P)], d["wT"][:]), [f"wT{L}"],
                done=f"wst{L}", dma=True)

        angles()
        for stage in (s_in, s_xT, s_gate, s_v, s_qk("q"), s_qk("k"), s_energy, s_kt, s_out, s_wo, s_next):
            for L in LANES:
                stage(L, lanes[L])
        lp.run()


def gated_recurrence(nc, A, x3, xn3T, K, T, C, KC):
    S = T // 2
    R = 256
    G = ("f", "i", "c")
    out = A["out"]
    with memory(nc, "gr") as (sb, ps):
        w = {n: sb(n, [P, KC, C]) for n in ("wf", "wi", "wc", "wo", "uf", "ui", "uc", "uo")}
        b = sb("bias", [P, 3, KC])
        b0 = sb("b_first", [P, 3, KC])
        c0, bo = sb("c_start", [P, KC]), sb("bo_row", [P, C])
        load(nc, [(w[n][:], A[n].rearrange("(k p) n -> p k n", p=P)) for n in w]
             + [(b[:, g, :], A[f"b{n}"]) for g, n in enumerate(G)]
             + [(c0[:], A["in_c"]), (bo[:], A["bo"].partition_broadcast(P))])
        gb = [[ps(f"g{L}{g}", [P, 512]) for g in range(3)] for L in LANES]
        ob = [ps(f"o{L}", [P, 512]) for L in LANES]
        ch = Chain(nc, "gr_bias")

        def uc0(e):
            for g, n in enumerate(G):
                for m in range(KC):
                    for k in range(KC):
                        i = e.matmul(ob[0][:, g * KC + m:g * KC + m + 1], w["u" + n][:, k, m * P:(m + 1) * P],
                                     c0[:, k:k + 1], start=(k == 0), stop=(k == KC - 1))
            return i
        ch("tensor", uc0)
        ch("vector", lambda e: e.tensor_tensor(b0[:], ob[0][:, 0:3 * KC].rearrange("p (g k) -> p g k", g=3), b[:],
                                               ALU.add))
        ch.run()
        lp = Loop(nc, S // (2 * R), "gr")
        lanes = [{n: sb(f"{n}{L}", s) for n, s in (
            ("x0", [P, KC, R]), ("x1", [P, KC, R]), ("f", [P, KC, R]), ("i", [P, KC, R]), ("c", [P, KC, R]),
            ("ig", [P, KC, R]), ("fc", [P, KC, R]), ("c1", [P, KC, R]), ("c2", [P, KC, R]),
            ("h0", [P, 2, C]), ("h1", [P, 2, C]), ("r0", [P, 2, C]), ("r1", [P, 2, C]),
            ("st", [P, 2, 6]), ("mv", [P, 2, 2]), ("ve", [P, 2]), ("rs", [P, 2]))} for L in LANES]

        def cols(s, t, L):
            return xn3T.rearrange("(k p) n -> p k n", p=P)[:, :, bass.ds(t * 2 * R + L * R + s * S, R)]

        def tok(dr, s, t, L):
            return dr[bass.ds(t * 2 * R + L * R + s * S, R), :].rearrange("(q p) c -> p q c", p=P)

        def s_in(L, d):
            for s in range(2):
                lp.step("sync", lambda e, t, s=s: e.dma_start(d[f"x{s}"][:], cols(s, t, L)),
                        frees=[f"o{s}{L}"], done=f"x{s}{L}", dma=True)
            for s in range(2):
                lp.step("sync", lambda e, t, s=s: e.dma_start(d[f"r{s}"][:], tok(x3, s, t, L)),
                        frees=[f"xo{s}{L}"], done=f"r{s}{L}", dma=True)

        def s_step(s):
            def stage(L, d):
                for g, n in enumerate(G):
                    bank = gb[L][g]

                    def wx(e, t, n=n, bank=bank):
                        for m in range(KC):
                            o = bank[:, m * R:(m + 1) * R]
                            for k in range(KC):
                                i = e.matmul(o, w["w" + n][:, k, m * P:(m + 1) * P], d[f"x{s}"][:, k, :],
                                             start=(k == 0), stop=(s == 0 and k == KC - 1))
                            if s:
                                for k in range(KC):
                                    i = e.matmul(o, w["u" + n][:, k, m * P:(m + 1) * P], d["c1"][:, k, :],
                                                 start=False, stop=(k == KC - 1))
                        return i
                    lp.step("tensor", wx, [f"x{s}{L}"] + ([f"n{n}0{L}", f"c1{L}"] if s else []),
                            frees=[] if s else [f"n{n}1{L}"], done=f"g{n}{s}{L}")

                    def act(e, t, n=n, bank=bank, g=g):
                        for m in range(KC):
                            i = e.activation(d[n][:, m], bank[:, m * R:(m + 1) * R],
                                             ACT.Tanh if n == "c" else ACT.Sigmoid,
                                             bias=(b if s else b0)[:, g, m:m + 1])
                        return i
                    lp.step("scalar", act, [f"g{n}{s}{L}"] + ([f"c1{L}"] if s else []),
                            frees=[] if s else [f"c2{L}"], done=f"n{n}{s}{L}")
                lp.step("vector", lambda e, t: e.tensor_tensor(d["ig"][:], d["i"][:], d["c"][:], ALU.mult),
                        [f"nc{s}{L}"], done=f"ig{s}{L}")
                if s == 0:
                    def c1(e, t):
                        for m in range(KC):
                            i = e.scalar_tensor_tensor(d["c1"][:, m], d["f"][:, m], c0[:, m:m + 1], d["ig"][:, m],
                                                       ALU.mult, ALU.add)
                        return i
                    lp.step("vector", c1, [f"ig0{L}"], done=f"c1{L}")
                else:
                    lp.step("vector", lambda e, t: e.tensor_tensor(d["fc"][:], d["f"][:], d["c1"][:], ALU.mult),
                            done=f"fc{L}")
                    lp.step("vector", lambda e, t: e.tensor_tensor(d["c2"][:], d["fc"][:], d["ig"][:], ALU.add),
                            [f"fc{L}", f"ig1{L}"], frees=[f"o1{L}"], done=f"c2{L}")
            return stage

        def s_out(s):
            def stage(L, d):
                h = d[f"h{s}"]

                def o(e, t):
                    for q in range(2):
                        for m, (a, wt) in enumerate(((d[f"x{s}"], w["wo"]), (d["c2"], w["uo"]))):
                            for k in range(KC):
                                i = e.matmul(ob[L][:, q * C:(q + 1) * C], a[:, k, q * P:(q + 1) * P], wt[:, k, :],
                                             start=(m == 0 and k == 0), stop=(m == 1 and k == KC - 1))
                    return i
                lp.step("tensor", o, [f"c2{L}"] + ([f"hb0{L}"] if s else []), frees=[] if s else [f"hb1{L}"],
                        done=f"o{s}{L}")
                lp.step("vector", lambda e, t: e.tensor_tensor(h[:], chunks(ob[L][:], 2), bc(bo[:], 1, 2), ALU.add),
                        [f"o{s}{L}"], frees=[f"out{s}{L}"], done=f"hb{s}{L}")
                lp.step("scalar", lambda e, t: e.activation(h[:], h[:], ACT.Tanh), [f"hb{s}{L}"], done=f"h{s}{L}")

                def each(fn):
                    def f(e, t):
                        for q in range(2):
                            i = fn(e, q)
                        return i
                    return f
                lp.step("vector", each(lambda e, q: e.bn_stats(d["st"][:, q], h[:, q])), [f"h{s}{L}"],
                        done=f"st{s}{L}")
                lp.step("vector", each(lambda e, q: e.bn_aggr(d["mv"][:, q], d["st"][:, q])), [f"st{s}{L}"],
                        done=f"mv{s}{L}", apart=True)
                lp.step("vector", lambda e, t: e.tensor_scalar(d["ve"][:], d["mv"][:, :, 1], LN_EPS, None, ALU.add),
                        [f"mv{s}{L}"], done=f"ve{s}{L}")
                lp.step("gpsimd", lambda e, t: e.tensor_tensor(d["rs"][:], d["ve"][:],
                                                               K["half"].broadcast_to([P, 2]), ALU.pow),
                        [f"ve{s}{L}"], done=f"rs{s}{L}")
                lp.step("vector", each(lambda e, q: e.tensor_scalar(h[:, q], h[:, q], d["mv"][:, q, 0:1],
                                                                    d["rs"][:, q:q + 1], ALU.subtract, ALU.mult)),
                        [f"rs{s}{L}"], done=f"ln{s}{L}")
                lp.step("gpsimd", lambda e, t: e.tensor_tensor(h[:], h[:], d[f"r{s}"][:], ALU.add),
                        [f"ln{s}{L}", f"r{s}{L}"], done=f"xo{s}{L}")
                lp.step("sync", lambda e, t: e.dma_start(tok(out, s, t, L), h[:]), [f"xo{s}{L}"],
                        done=f"out{s}{L}", dma=True)
            return stage

        for stage in (s_in, s_step(0), s_step(1), s_out(0), s_out(1)):
            for L in LANES:
                stage(L, lanes[L])
        lp.run()



def inputs(given):
    def g(name):
        return np.asarray(given[name])

    def t(name):
        return np.ascontiguousarray(g(name).T)

    def twice(a):
        a = a.reshape(*a.shape[:-1], HEADS, 1, -1)
        return np.ascontiguousarray(np.concatenate([a, a], -2).reshape(*a.shape[:-3], -1))
    ffn, att, rec = "L0_ffn_", "L1_attn_", "L1_ffn_"
    d = {"x": np.ascontiguousarray(g("L0_attn_x").reshape(-1, 256)), "w_attnT": t("L0_attn_w_attn"),
         "w_projT": t("L0_attn_w_proj"), "gateT": t(ffn + "gate_w")}
    d |= {n: g(ffn + n) for n in ("w1", "w2", "w3", "sw1", "sw2", "sw3")}
    d |= {n: g(att + n) for n in ("Wv", "Wo", "G1", "G2", "gamma", "beta")}
    d |= {"Wq2": twice(g(att + "Wq")), "Wk2": twice(g(att + "Wk")),
          "theta2": np.ascontiguousarray(twice(g(att + "theta").reshape(1, -1)).reshape(4, P).T)}
    d |= {n: t(rec + n) for n in ("wf", "wi", "wc", "wo", "uf", "ui", "uc", "uo")}
    d |= {n: np.ascontiguousarray(g(rec + n).reshape(-1, P).T) for n in ("bf", "bi", "bc", "in_c")}
    d["bo"] = g(rec + "bo")
    d["consts"] = np.concatenate([np.asarray(v, np.float32) for v in const_layout().values()], 1)
    return d


def kernel(**given):
    import concourse.bacc as bacc
    from concourse.bass_utils import run_bass_kernel_spmd

    nc = bacc.Bacc("TRN2", target_bir_lowering=False, num_devices=1)
    arrays, A = {}, {}
    for name, a in inputs(given).items():
        arrays[f"in_{name}"] = a
        A[name] = nc.dram_tensor(f"in_{name}", a.shape, mybir.dt.from_np(a.dtype), kind="ExternalInput").ap()
    shape = given["L0_attn_x"].shape
    A["out"] = nc.dram_tensor("out", [shape[0] * shape[1], shape[2]], F32, kind="ExternalOutput").ap()

    def dram(name, shape, dt):
        return nc.dram_tensor(name, list(shape), dt, kind="Internal").ap()
    build(nc, A, dram)
    r = run_bass_kernel_spmd(nc, [arrays], core_ids=[0])
    return r.results[0]["out"].reshape(shape)
```

```python
from contextlib import ExitStack, contextmanager

import numpy as np

import concourse.bass as bass
from concourse import mybir

P = 128
F32 = mybir.dt.float32
I32 = mybir.dt.int32
ALU = mybir.AluOpType
ACT = mybir.ActivationFunctionType
AX_X = mybir.AxisListType.X
LANES = (0, 1)
LN_EPS = 1e-5


class Loop:

    def __init__(self, nc, items, name):
        self.nc, self.items, self.name = nc, items, name
        self.queues = {e: [] for e in ("sync", "scalar", "vector", "gpsimd", "tensor")}
        self.count, self.lag = {}, 0
        self.laid = {}
        self.shared, self.start = {}, {}
        self.software = set()
        self.opening, self.asides = [], []

    def step(self, engine, emit, reads=(), frees=(), done=None, dma=False, apart=False, last=()):
        waits = [(n, 2) for n in reads] + [(n, 1) for n in frees]
        recent = [(n, len(self.laid)) for n in last]
        if done is not None:
            self.laid[done] = (len(self.laid), self.lag)
            if dma:
                sem = self.nc.alloc_semaphore(f"{self.name}_{done}")
                self.count[done] = (sem, 16, 0)
                if engine == "gpsimd":
                    self.software.add(done)
            elif done[-1] in "01":
                if done[:-1] not in self.shared:
                    self.shared[done[:-1]] = self.nc.alloc_semaphore(f"{self.name}_{done[:-1]}_lanes")
                sem = self.shared[done[:-1]]
                self.count[done] = (sem, 2, int(done[-1]) - 1)
            else:
                sem = self.nc.alloc_semaphore(f"{self.name}_{done}")
                self.count[done] = (sem, 1, 0)
            if done not in self.software:
                self.start[id(sem)] = (engine, sem, self.count[done][1])
        self.queues[engine].append((emit, waits, recent, done, dma, apart or engine == "sync", self.lag))

    def open(self, engine, emit, after=0):
        self.opening.append((engine, emit, after))

    def aside(self, engine, turn, emit):
        self.asides.append((engine, turn, emit))

    def before(self, name, L):
        return ([f"{name}0"], []) if L else ([], [f"{name}1"])

    def pipeline(self, stages, lanes):
        for slot in LANES:
            for h, stage in stages:
                L = (slot - h) % 2
                self.lag = (h - slot + L) // 2
                stage(L, lanes[L])
        self.lag = 0

    def _runs(self, name, lag, ahead):
        _, unit, offset = self.count[name]
        return lag, ahead - (name in self.software), unit, offset

    def run(self, loads=()):
        self.loads = loads
        opened = self.nc.alloc_semaphore(f"{self.name}_opened")
        for queue in self.queues.values():
            for _, waits, recent, _, _, _, lag in queue:
                for n, place in recent:
                    at, its_lag = self.laid[n]
                    waits.append((n, 2 + lag - its_lag - (at >= place)))
                furthest = {}
                for n, ahead in waits:
                    sem, unit, offset = self.count[n]
                    furthest.setdefault(id(sem), []).append((ahead * unit + offset, (n, ahead)))
                waits[:] = [max(w)[1] for w in furthest.values()]
        assert not any(n in self.software and ahead < 2 for q in self.queues.values() for s in q for n, ahead in s[1])
        passed = self.nc.alloc_semaphore(f"{self.name}_passed")
        with self.nc.Block() as block:
            for engine, queue in self.queues.items():
                if queue:
                    self._engine(block, engine, queue, passed, opened)
        sems = {id(c[0]): c[0] for c in self.count.values()}
        self.nc.clear_and_free_semaphores([passed, opened, *(x.sem for x in loads), *sems.values()])
        self.nc.all_engine_barrier()

    def _engine(self, block, engine, queue, passed, opened):
        decorate = {"sync": block.sync, "scalar": block.scalar, "vector": block.vector,
                    "gpsimd": block.gpsimd, "tensor": block.tensor}[engine]
        assert all(turn < max(q[-1] for qs in self.queues.values() for q in qs) for _, turn, _ in self.asides)
        depth = max(q[-1] for qs in self.queues.values() for q in qs)

        def work(eng, turn, due):
            peeled = isinstance(turn, int)
            for emit, waits, _, done, dma, apart, lag in queue:
                if peeled and not 0 <= turn - lag < self.items:
                    continue
                for n, ahead in waits:
                    if not peeled or turn - lag + ahead > 0:
                        eng.wait_ge(self.count[n][0], due(*self._runs(n, lag, ahead)))
                if apart and waits:
                    eng.sem_inc(passed, 1)
                last = emit(eng, turn - lag)
                if done is not None:
                    last.then_inc(self.count[done][0], 16 if dma else 1)

        def fixed(turn):
            return lambda lag, ahead, unit, offset: min(turn - lag + ahead, self.items + 1) * unit + offset

        def body(eng):
            for on, sem, units in self.start.values():
                if on == engine:
                    eng.sem_inc(sem, units)
            if engine != "sync":
                for x in self.loads:
                    eng.wait_ge(x.sem, 16 * x.n)
            for on, emit, after in self.opening:
                if on == engine:
                    if after:
                        eng.wait_ge(opened, after)
                    emit(eng).then_inc(opened, 1)
            if self.opening and engine not in ("sync", "gpsimd"):
                eng.wait_ge(opened, len(self.opening))
            for turn in range(depth):
                work(eng, turn, fixed(turn))
                for on, at, emit in self.asides:
                    if (on, at) == (engine, turn):
                        emit(eng)
            with eng.Fori(depth, self.items) as turn:
                need = sorted({self._runs(n, s[-1], ahead) for s in queue for n, ahead in s[1]})
                regs = {k: eng.snap((turn + (k[1] - k[0])) * k[2] + k[3]) for k in need}
                work(eng, turn, lambda *k: regs[k])
            for turn in range(self.items, self.items + depth):
                work(eng, turn, fixed(turn))
            for _, _, _, done, dma, _, _ in queue:
                if dma:
                    eng.wait_ge(self.count[done][0], 16 * (self.items + (done not in self.software)))
        decorate(body)


@contextmanager
def memory(nc, phase):
    with ExitStack() as stack:
        def sb(name, shape, dt=F32):
            return stack.enter_context(nc.sbuf_tensor(f"{phase}_{name}", list(shape), dt))

        def ps(name, shape):
            return stack.enter_context(nc.psum_tensor(f"{phase}_{name}", list(shape), F32))
        yield sb, ps


def bc(ap, dim, n):
    return ap.unsqueeze(dim).broadcast_to([*ap.shape[:dim], n, *ap.shape[dim:]])


class LayerNorm:

    def __init__(self, sb, name, half):
        self.st, self.mv = sb(f"{name}_st", [P, 6]), sb(f"{name}_mv", [P, 2])
        self.ve, self.rstd, self.half = sb(f"{name}_ve", [P, 1]), sb(f"{name}_rs", [P, 1]), half

    def stats(self, lp, tag, src, reads):
        lp.step("vector", lambda e, t: e.bn_stats(self.st[:], src), reads, done=f"st_{tag}")
        lp.step("vector", lambda e, t: e.bn_aggr(self.mv[:], self.st[:]), [f"st_{tag}"], [f"ln_{tag}"],
                done=f"mv_{tag}", apart=True)
        lp.step("gpsimd", lambda e, t: e.tensor_scalar(self.ve[:], self.mv[:, 1:2], LN_EPS, None, ALU.add),
                [f"mv_{tag}"], done=f"ve_{tag}", apart=True)
        lp.step("gpsimd", lambda e, t: e.tensor_tensor(self.rstd[:], self.ve[:], self.half, ALU.pow),
                [f"ve_{tag}"], [f"ln_{tag}"], done=f"rs_{tag}")

    def apply(self, lp, tag, src, out, reads=(), frees=()):
        lp.step("vector", lambda e, t: e.tensor_scalar(out, src, self.mv[:, 0:1], self.rstd[:, 0:1],
                                                       ALU.subtract, ALU.mult),
                [f"rs_{tag}", *reads], frees, done=f"ln_{tag}")


def const_layout(T=4096, C=256, heads=16, experts=8, slots=72):
    p, nt = np.arange(P), T // P
    e, t = np.divmod(np.arange(experts * nt), nt)
    return {
        "ident": np.eye(P),
        "half": np.full((P, 1), -0.5),
        "head_of_16": (p // 16)[:, None] == np.arange(8),
        "before": p[:, None] < p[None, :],
        "ones": np.ones((P, P)),
        "rank": np.tile(experts - np.arange(experts), (P, 1)),
        "goes_on": np.tile(t > 0, (P, 1)),
        "one_e": np.ones((P, experts)),
        "slot": np.tile(np.arange(slots), (P, 1)),
        "token": p[:, None] + P * np.arange(nt)[None, :],
        "causal": p[:, None] <= p[None, :],
        "own_head": (p // 32)[:, None] == (np.arange(64) // 16),
        "row": np.tile(p, (P, 1)),
        "quarter": np.where(p % 32 < 16, 0.25, 0.0)[:, None],
        "quarter_rad": np.where(p % 32 < 16, np.pi / 2, 0.0)[:, None],
    }


def tile_rows(dr, t, L, n=P):
    return dr[bass.ds(t * 2 * n + L * n, n), :]


def chunks(ap, k):
    return ap.rearrange("p (k n) -> p k n", k=k)


def build(nc, A, dram):
    T, C = A["x"].shape
    KC = C // P
    NT = T // P
    E, F = A["w13"].shape[0] // (2 * C), A["w13"].shape[1]
    KF = -(-F // P)
    SLOTS = (2 * T // P + E) // 2 * 2
    x1, xn1, ysh = dram("x1", [T, C], F32), dram("xn1", [T, C], F32), dram("ysh", [T, C], F32)
    yg = dram("yg", [SLOTS * P, C], F32)
    x2, x3, xn3T = dram("x2", [T, C], F32), dram("x3", [T, C], F32), dram("xn3T", [C, T], F32)
    with ExitStack() as keep:
        def sb(name, shape, dt=F32):
            return keep.enter_context(nc.sbuf_tensor(name, list(shape), dt))
        lay = const_layout(T, C, HEADS, E, SLOTS)
        consts = sb("consts", [P, sum(v.shape[1] for v in lay.values())])
        K, at = {}, 0
        for n, v in lay.items():
            K[n] = consts[:, at:at + v.shape[1]]
            at += v.shape[1]
        logits, weight = sb("logits", [P, NT, E]), sb("weight", [P, 2, NT])
        place, source = sb("place", [P, 2, NT], I32), sb("source", [P, SLOTS], I32)
        expert = sb("expert", [P, SLOTS], I32)
        W, attention_pairs = attention_weights(sb, A, C, KC)
        first = Loads(nc, "l_consts", [(consts[:], A["consts"])])
        pieces = NT // 2
        with ExitStack() as moe:
            w13 = moe.enter_context(nc.sbuf_tensor("w13", [P, 2 * E, KC, F], F32))
            assert 2 * E % pieces == 0 and E * KF % pieces == 0

            def w13_piece(e, t):
                n = 2 * E // pieces
                return e.dma_start(w13[:, bass.ds(t * n, n)].rearrange("p n k f -> p (n k) f"),
                                   A["w13"][bass.ds(t * n * C, n * C), :].rearrange("(k p) f -> p k f", p=P))

            def w2_piece(e, t):
                n = E * KF // pieces
                return e.dma_start(w2[:, bass.ds(t * n, n), :],
                                   A["w2"][bass.ds(t * n * P, n * P), :].rearrange("(k p) n -> p k n", p=P))
            S, shared_pairs = shared_weights(lambda n, z: moe.enter_context(nc.sbuf_tensor(f"se_{n}", z, F32)), A, C, KC)
            loads = window_attention(nc, A, x1, K, C, KC, NT, first, shared_pairs, attention_pairs, w13_piece)
            w2 = moe.enter_context(nc.sbuf_tensor("w2", [P, E * KF, C], F32))
            shared_expert(nc, A, S, x1, xn1, ysh, logits, K, C, KC, NT, E, loads[:1], w2_piece)
            route(nc, logits, weight, place, source, expert, K, NT, E, SLOTS)
            experts(nc, xn1, yg, w13, w2, source, expert, K, C, KC, E, SLOTS, F)
        with memory(nc, "gw") as (sb, _):
            w, pairs = recurrence_weights(sb, A, C, KC)
            gates = linear_attention(nc, A, W, x1, ysh, yg, weight, place, x2, x3, xn3T, K, T, C, KC,
                                     loads[1:], pairs)
            gated_recurrence(nc, A, w, x3, xn3T, K, T, C, KC, [gates])


class Loads:

    def __init__(self, nc, name, pairs, beside=None):
        self.n, self.sem = len(pairs), nc.alloc_semaphore(name)

        def start(e):
            for dst, src in pairs:
                e.dma_start(dst, src).then_inc(self.sem, 16)
        if beside is None:
            with nc.Block() as block:
                block.scalar(start)
        else:
            lp, turn = beside
            lp.aside("scalar", turn, start)


def kcn(a):
    return a.rearrange("(k p) n -> p k n", p=P)


HEADS, WIN = 16, 64


def window_attention(nc, A, x1, K, C, KC, NT, first, shared_pairs, attention_pairs, w13_piece):
    D = C // HEADS
    NB = HEADS // 2
    HC = P // D
    ident = K["ident"]
    with memory(nc, "wa") as (sb, ps):
        wqkv, wp = sb("wqkv", [P, KC, 3 * C]), sb("wp", [P, KC, C])
        own = Loads(nc, "l_wa", [(wqkv[:], kcn(A["w_attnT"])), (wp[:], kcn(A["w_projT"]))])
        lanes = []
        for L in LANES:
            d = {n: sb(f"{n}{L}", s) for n, s in (
                ("xa", [P, C]), ("xr", [P, C]), ("xn", [P, C]), ("xnT", [P, KC, P]), ("qT", [P, KC, P]),
                ("km", [P, KC, HC, P]), ("mx", [P, HEADS]), ("pr", [P, HEADS, WIN]), ("pT", [P, NB, P]),
                ("rec", [P, HEADS]), ("yn", [P, C]), ("yT", [P, KC, P]), ("zn", [P, C]), ("xo", [P, C]),
                ("vb", [P, 2, NB, 2, D + 1]))}
            d["ln1"], d["ln2"] = LayerNorm(sb, f"lna{L}", K["half"]), LayerNorm(sb, f"lnb{L}", K["half"])
            lanes.append(d)
        bxk, bqv, bS, bP = ps("xk", [P, 512]), ps("qv", [P, 512]), ps("S", [P, KC, 512]), ps("P", [P, 2, 512])
        bY, bZ = ps("Y", [P, 512]), ps("Z", [P, 512])
        lp = Loop(nc, NT // 2, "wa")
        for d, engine in zip(lanes, ("vector", "gpsimd")):
            lp.open(engine, lambda e, d=d: e.memset(d["vb"][:], 0.0))

        def ones(e):
            for d in lanes:
                for w in range(2):
                    for h2 in range(2):
                        i = e.memset(d["vb"][64 * h2:64 * h2 + 64, w, :, h2, D:D + 1], 1.0)
            return i
        lp.open("vector", ones, after=2)
        loads = [Loads(nc, "l_shared", shared_pairs, (lp, 0)), Loads(nc, "l_attention", attention_pairs, (lp, 1))]

        def s_load(L, d):
            lp.step("sync", lambda e, t: e.dma_start(d["xa"][:], tile_rows(A["x"], t, L)), frees=[f"ln_1{L}"],
                    done=f"xa{L}", dma=True)

        def s_piece(L, d):
            if L == 0:
                lp.step("sync", w13_piece, done="w13_loaded", dma=True)

        def s_norm(L, d):
            d["ln1"].stats(lp, f"1{L}", d["xa"][:], [f"xa{L}"])

        def s_again(L, d):
            lp.step("sync", lambda e, t: e.dma_start(d["xr"][:], tile_rows(A["x"], t, L)), frees=[f"xo{L}"],
                    done=f"xr{L}", dma=True)

        def s_xn(L, d):
            d["ln1"].apply(lp, f"1{L}", d["xa"][:], d["xn"][:], frees=[f"xnTp{L}"])

        def s_xT(L, d):
            r, f = lp.before("km", L)

            def tr(e, t):
                for k in range(KC):
                    i = e.transpose(bxk[:, k * P:(k + 1) * P], d["xn"][:, k * P:(k + 1) * P], ident)
                return i
            lp.step("tensor", tr, [f"ln_1{L}", *r], f, done=f"xnTp{L}")
            lp.step("scalar", lambda e, t: e.copy(d["xnT"][:], chunks(bxk[:, 0:C], KC)),
                    [f"xnTp{L}"], frees=[f"v{L}"], done=f"xnT{L}")

        def s_qkv(L, d):
            r, f = lp.before("vb", L)

            def proj(out, col):
                def f(e, t):
                    for c in range(KC):
                        for k in range(KC):
                            i = e.matmul(out[:, c * P:(c + 1) * P], wqkv[:, k, col + c * P:col + (c + 1) * P],
                                         d["xnT"][:, k, :], start=(k == 0), stop=(k == KC - 1))
                    return i
                return f

            def v(e, t):
                for k in range(KC):
                    i = e.matmul(bqv[:, C:2 * C], d["xnT"][:, k, :], wqkv[:, k, 2 * C:3 * C],
                                 start=(k == 0), stop=(k == KC - 1))
                return i
            lp.step("tensor", proj(bxk[:, C:2 * C], C), [f"xnT{L}"], done=f"k{L}")
            lp.step("tensor", proj(bqv[:, 0:C], 0), r, f)
            lp.step("tensor", v, done=f"v{L}")
            lp.step("scalar", lambda e, t: e.copy(d["qT"][:], chunks(bqv[:, 0:C], KC)),
                    [f"v{L}"], frees=[f"S{L}"], done=f"qT{L}")

            def vb(e, t):
                for w in range(2):
                    for h2 in range(2):
                        src = bqv[64 * w:64 * w + 64, C:2 * C].rearrange("p (b h d) -> p b h d", b=NB, h=2)
                        i = e.copy(d["vb"][64 * h2:64 * h2 + 64, w, :, h2, 0:D], src[:, :, h2, :])
                return i
            lp.step("scalar", vb, frees=[f"pv{L}"], done=f"vb{L}")

            def km(e, t):
                for c in range(KC):
                    i = e.tensor_tensor(d["km"][:, c], bc(bxk[:, C + c * P:C + (c + 1) * P], 1, HC),
                                        bc(K["head_of_16"], 2, P), ALU.mult)
                return i
            lp.step("vector", km, [f"k{L}"], frees=[f"S{L}"], done=f"km{L}")

        S3 = bS[:].rearrange("p c (h k) -> p (c h) k", k=WIN)

        def s_scores(L, d):
            r, f = lp.before("sub", L)

            def sc(e, t):
                for c in range(KC):
                    for w in range(2):
                        i = e.matmul(bS[64 * w:64 * w + 64, c, :], d["qT"][:, c, 64 * w:64 * w + 64],
                                     d["km"][:, c, :, 64 * w:64 * w + 64], start=True, stop=True)
                return i
            lp.step("tensor", sc, [f"qT{L}", f"km{L}", *r], f, done=f"S{L}", apart=True)
            lp.step("vector", lambda e, t: e.tensor_reduce(d["mx"][:], S3, AX_X, ALU.max), [f"S{L}"], done=f"mx{L}")
            lp.step("vector", lambda e, t: e.tensor_tensor(d["pr"][:], S3, bc(d["mx"][:], 2, WIN), ALU.subtract),
                    [f"mx{L}"], frees=[f"pTp{L}"], done=f"sub{L}")

        def s_exp(L, d):
            lp.step("scalar", lambda e, t: e.activation(d["pr"][:], d["pr"][:], ACT.Exp, scale=float(D) ** -0.5),
                    [f"sub{L}"], done=f"exp{L}")

        def s_pT(L, d):
            ra, fa = lp.before("pTa", L)
            rb, fb = lp.before("pTb", L)

            def tr(e, t):
                pr = d["pr"][:].rearrange("p h k -> p (h k)")
                for b in range(NB):
                    i = e.transpose(bP[:, b // 4, (b % 4) * P:(b % 4 + 1) * P], pr[:, b * P:(b + 1) * P], ident)
                return i
            lp.step("tensor", tr, [f"exp{L}", *ra, *rb], [*fa, *fb], done=f"pTp{L}")
            for n, e_, b in (("pTa", "scalar", 0), ("pTb", "vector", 1)):
                def cp(e, t, b=b):
                    f = e.copy if b == 0 else e.tensor_copy
                    return f(d["pT"][:, 4 * b:4 * b + 4, :], chunks(bP[:, b], 4))
                lp.step(e_, cp, [f"pTp{L}"], frees=[f"pv{L}"], done=f"{n}{L}")

        def s_pv(L, d):
            Y = bY[:, 0:HEADS * (D + 1)]
            r, f = lp.before("yn", L)

            def pv(e, t):
                for b in range(NB):
                    for w in range(2):
                        i = e.matmul(Y[64 * w:64 * w + 64, b * 34:(b + 1) * 34], d["pT"][:, b, 64 * w:64 * w + 64],
                                     d["vb"][:, w, b].rearrange("p h d -> p (h d)"), start=True, stop=True)
                return i
            lp.step("tensor", pv, [f"pTa{L}", f"pTb{L}", f"vb{L}", *r], f, done=f"pv{L}")
            Y3 = Y.rearrange("p (h d) -> p h d", h=HEADS)
            lp.step("vector", lambda e, t: e.reciprocal(d["rec"][:], Y3[:, :, D]), [f"pv{L}"], done=f"rec{L}")
            lp.step("vector", lambda e, t: e.tensor_tensor(d["yn"][:].rearrange("p (h d) -> p h d", h=HEADS),
                                                           Y3[:, :, 0:D], bc(d["rec"][:], 2, D), ALU.mult),
                    [f"rec{L}"], frees=[f"yTp{L}"], done=f"yn{L}")

        def s_yT(L, d):
            r, f = lp.before("ln_2", L)

            def tr(e, t):
                for k in range(KC):
                    i = e.transpose(bZ[:, k * P:(k + 1) * P], d["yn"][:, k * P:(k + 1) * P], ident)
                return i
            lp.step("tensor", tr, [f"yn{L}", *r], f, done=f"yTp{L}")
            lp.step("scalar", lambda e, t: e.copy(d["yT"][:], chunks(bZ[:, 0:C], KC)),
                    [f"yTp{L}"], frees=[f"z{L}"], done=f"yT{L}")

        def s_z(L, d):
            def z(e, t):
                for k in range(KC):
                    i = e.matmul(bZ[:, C:2 * C], d["yT"][:, k, :], wp[:, k, :], start=(k == 0), stop=(k == KC - 1))
                return i
            lp.step("tensor", z, [f"yT{L}"], done=f"z{L}")
            d["ln2"].stats(lp, f"2{L}", bZ[:, C:2 * C], [f"z{L}"])

        def s_out(L, d):
            d["ln2"].apply(lp, f"2{L}", bZ[:, C:2 * C], d["zn"][:], frees=[f"xo{L}"])
            lp.step("gpsimd", lambda e, t: e.tensor_tensor(d["xo"][:], d["zn"][:], d["xr"][:], ALU.add),
                    [f"ln_2{L}", f"xr{L}"], frees=[f"out{L}"], done=f"xo{L}")
            lp.step("sync", lambda e, t: e.dma_start(tile_rows(x1, t, L), d["xo"][:]), [f"xo{L}"], done=f"out{L}", dma=True)

        lp.pipeline([(0, s_load), (0, s_piece), (2, s_xT), (6, s_out), (1, s_norm), (3, s_scores), (3, s_exp), (4, s_pv),
                     (1, s_xn), (5, s_yT), (2, s_qkv), (3, s_pT), (5, s_z), (4, s_again)], lanes)
        lp.run([first, own])
        return loads


def transposes(lp, L, tag, src, bank, dst, ident, reads=(), frees=(), keeps=(), n=2, last=()):
    def tr(e, t):
        for k in range(n):
            i = e.transpose(bank[:, k * P:(k + 1) * P], src[:, k * P:(k + 1) * P], ident)
        return i
    lp.step("tensor", tr, reads, frees, last=last, done=f"{tag}p{L}")
    lp.step("scalar", lambda e, t: e.copy(dst, chunks(bank[:, 0:n * P], n)), [f"{tag}p{L}"], keeps,
            done=f"{tag}{L}")


def shared_weights(sb, A, C, KC):
    F, EW = A["sw1"].shape[1], A["gateT"].shape[1]
    W = {"sw1": sb("sw1", [P, KC, F]), "sw3": sb("sw3", [P, KC, F]), "sw2": sb("sw2", [P, F // P, C]),
         "gateT": sb("gate", [P, KC, EW])}
    return W, [(W[n][:], kcn(A[n])) for n in W]


def shared_expert(nc, A, W, x1, xn1, ysh, logits, K, C, KC, NT, E, loads, w2_piece):
    F = A["sw1"].shape[1]
    KF = F // P
    EW = A["gateT"].shape[1]
    with memory(nc, "se") as (sb, ps):
        sw1, sw3, sw2, gate = (W[n] for n in ("sw1", "sw3", "sw2", "gateT"))
        lp = Loop(nc, NT // 2, "se")
        lanes = []
        for L in LANES:
            d = {n: sb(f"{n}{L}", s) for n, s in (
                ("xa", [P, C]), ("xn", [P, C]), ("xnT", [P, KC, P]), ("g", [P, KF, P]), ("gT", [P, KF, P]),
                ("yo", [P, C]))}
            d["ln"] = LayerNorm(sb, f"ln{L}", K["half"])
            d["bx"] = ps(f"x{L}", [P, 512])
            lanes.append(d)
        b1, b3, blg, by = (ps(n, [P, 512]) for n in ("h1", "h3", "lg", "y"))

        def s_in(L, d):
            lp.step("sync", lambda e, t: e.dma_start(d["xa"][:], tile_rows(x1, t, L)), frees=[f"ln_1{L}"],
                    done=f"xa{L}", dma=True)
            if L == 0:
                lp.step("sync", w2_piece, done="w2_loaded", dma=True)

        def s_norm(L, d):
            d["ln"].stats(lp, f"1{L}", d["xa"][:], [f"xa{L}"])

        def s_xn(L, d):
            d["ln"].apply(lp, f"1{L}", d["xa"][:], d["xn"][:], frees=[f"xnTp{L}", f"xno{L}"])
            lp.step("sync", lambda e, t: e.dma_start(tile_rows(xn1, t, L), d["xn"][:]), [f"ln_1{L}"],
                    done=f"xno{L}", dma=True)

        def s_xT(L, d):
            transposes(lp, L, "xnT", d["xn"], d["bx"], d["xnT"][:], K["ident"], [f"ln_1{L}"],
                       frees=[f"xnT{L}"], keeps=[f"lgp{L}"])

        def up(d, w, out):
            def f(e, t):
                for c in range(KF):
                    for k in range(KC):
                        i = e.matmul(out[:, c * P:(c + 1) * P], w[:, k, c * P:(c + 1) * P], d["xnT"][:, k, :],
                                     start=(k == 0), stop=(k == KC - 1))
                return i
            return f

        def s_h1(L, d):
            r, f = lp.before("g", L)
            lp.step("tensor", up(d, sw1, b1), [f"xnT{L}", *r], f, done=f"h1{L}")
            lp.step("scalar", lambda e, t: e.activation(d["g"][:], chunks(b1[:, 0:F], KF), ACT.Silu),
                    [f"h1{L}"], frees=[f"gT{L}"], done=f"g{L}")

        def s_h3(L, d):
            r, f = lp.before("gT", L)
            lp.step("tensor", up(d, sw3, b3), r, f, done=f"h3{L}")
            lp.step("vector", lambda e, t: e.tensor_tensor(d["gT"][:], d["g"][:], chunks(b3[:, 0:F], KF),
                                                           ALU.mult), [f"g{L}", f"h3{L}"], frees=[f"y{L}"],
                    done=f"gT{L}")

        def s_lg(L, d):
            r, f = lp.before("lg", L)

            def lg(e, t):
                for k in range(KC):
                    i = e.matmul(blg[:, 0:EW], d["xnT"][:, k, :], gate[:, k, :], start=(k == 0), stop=(k == KC - 1))
                return i
            lp.step("tensor", lg, r, f, done=f"lgp{L}")
            lp.step("vector", lambda e, t: e.tensor_copy(
                logits[:].rearrange("p (t l) e -> p t l e", l=2)[:, bass.ds(t, 1), L, :],
                blg[:, 0:E].unsqueeze(1)), [f"lgp{L}"], done=f"lg{L}")

        def s_y(L, d):
            r, f = lp.before("yo", L)

            def y(e, t):
                for c in range(KF):
                    i = e.matmul(by[:, 0:C], d["gT"][:, c, :], sw2[:, c, :], start=(c == 0), stop=(c == KF - 1))
                return i
            lp.step("tensor", y, [f"gT{L}", *r], f, done=f"y{L}")
            lp.step("scalar", lambda e, t: e.copy(d["yo"][:], by[:, 0:C]), [f"y{L}"], frees=[f"yst{L}"],
                    done=f"yo{L}")
            lp.step("sync", lambda e, t: e.dma_start(tile_rows(ysh, t, L), d["yo"][:]), [f"yo{L}"],
                    done=f"yst{L}", dma=True)

        lp.pipeline([(0, s_in), (2, s_xT), (3, s_y), (1, s_norm), (2, s_h1), (1, s_xn), (2, s_h3), (2, s_lg)], lanes)
        lp.run(loads)


class Chain:

    def __init__(self, nc, name):
        self.nc, self.name, self.steps = nc, name, []

    def __call__(self, engine, emit):
        self.steps.append((engine, emit))

    def run(self):
        sem = self.nc.alloc_semaphore(self.name)
        with self.nc.Block() as block:
            for engine in sorted({e for e, _ in self.steps}):
                def body(eng, engine=engine):
                    for n, (on, emit) in enumerate(self.steps):
                        if on == engine:
                            eng.wait_ge(sem, n)
                            emit(eng).then_inc(sem, 1)
                {"scalar": block.scalar, "vector": block.vector, "gpsimd": block.gpsimd,
                 "tensor": block.tensor}[engine](body)
        self.nc.clear_and_free_semaphores([sem])
        self.nc.all_engine_barrier()


def route(nc, logits, weight, place, source, expert, K, NT, E, SLOTS):
    with memory(nc, "ro") as (sb, ps):
        m1, m2, top = sb("m1", [P, NT]), sb("m2", [P, NT]), sb("top", [P, NT])
        eq, ex = sb("eq", [P, NT, E]), sb("ex", [P, NT, E])
        pick = [sb("pick0", [P, NT, E]), sb("pick1", [P, NT, E])]
        rest, rs, dm = sb("rest", [P, NT, E]), sb("rs", [P, NT]), sb("dm", [P, NT])
        mask, inc, pos = sb("mask", [P, E, NT]), sb("inc", [P, E * NT]), sb("pos", [P, E, NT])
        tot = sb("tot", [P, E * NT])
        bi, blk, cum, first = sb("bi", [P, E], I32), sb("blk", [P, E]), sb("cum", [P, E]), sb("first", [P, E])
        cmp, se = sb("cmp", [P, SLOTS, E]), sb("se", [P, SLOTS])
        pfx, ptot = ps("pfx", [P, 512]), ps("ptot", [P, 512])
        pi, row, slot = sb("pi", [P, NT], I32), sb("row", [P, 2, NT]), sb("slot", [P, 2, NT])
        ch = Chain(nc, "route")

        def tt(out, a, b, op):
            ch("vector", lambda e: e.tensor_tensor(out, a, b, op))

        def red(out, a, op):
            ch("vector", lambda e: e.tensor_reduce(out, a, AX_X, op))

        def one_hot(src, m, out):
            red(m[:], src[:], ALU.max)
            tt(eq[:], src[:], bc(m[:], 2, E), ALU.is_equal)
            tt(eq[:], eq[:], bc(K["rank"], 1, NT), ALU.mult)
            red(top[:], eq[:], ALU.max)
            tt(out[:], eq[:], bc(top[:], 2, E), ALU.is_equal)

        one_hot(logits, m1, pick[0])
        ch("vector", lambda e: e.scalar_tensor_tensor(rest[:], pick[0][:], -3.0e38, logits[:], ALU.mult, ALU.add))
        one_hot(rest, m2, pick[1])
        tt(ex[:], logits[:], bc(m1[:], 2, E), ALU.subtract)
        ch("scalar", lambda e: e.activation(ex[:], ex[:], ACT.Exp))
        red(rs[:], ex[:], ALU.add)
        ch("vector", lambda e: e.reciprocal(weight[:, 0, :], rs[:]))
        tt(dm[:], m2[:], m1[:], ALU.subtract)
        ch("scalar", lambda e: e.activation(dm[:], dm[:], ACT.Exp))
        tt(weight[:, 1, :], dm[:], weight[:, 0, :], ALU.mult)
        tt(mask[:], pick[0][:].rearrange("p t e -> p e t"), pick[1][:].rearrange("p t e -> p e t"), ALU.add)
        flat = mask[:].rearrange("p e t -> p (e t)")
        ch("tensor", lambda e: e.matmul(pfx[:, 0:E * NT], K["before"], flat, start=True, stop=True))
        ch("tensor", lambda e: e.matmul(ptot[:, 0:E * NT], K["ones"], flat, start=True, stop=True))
        ch("vector", lambda e: e.tensor_copy(tot[:], ptot[:, 0:E * NT]))
        ch("vector", lambda e: e.tensor_tensor_scan(inc[:], K["goes_on"], tot[:], 0.0, ALU.mult, ALU.add))
        last = inc[:].rearrange("p (e t) -> p e t", e=E)[:, :, NT - 1]
        ch("vector", lambda e: e.tensor_scalar(bi[:], last, float(P - 1), None, ALU.add))
        ch("vector", lambda e: e.tensor_scalar(bi[:], bi[:], 7, None, ALU.logical_shift_right))
        ch("vector", lambda e: e.tensor_copy(blk[:], bi[:]))
        ch("vector", lambda e: e.tensor_tensor_scan(cum[:], K["one_e"], blk[:], 0.0, ALU.mult, ALU.add))
        tt(first[:], cum[:], blk[:], ALU.subtract)
        ch("vector", lambda e: e.tensor_scalar(first[:], first[:], float(P), None, ALU.mult))
        tt(inc[:], inc[:], tot[:], ALU.subtract)
        tt(inc[:], inc[:], pfx[:, 0:E * NT], ALU.add)
        tt(pos[:], inc[:].rearrange("p (e t) -> p e t", e=E), bc(first[:], 2, NT), ALU.add)
        for k in range(2):
            tt(eq[:], pick[k][:], pos[:].rearrange("p e t -> p t e"), ALU.mult)
            red(top[:], eq[:], ALU.add)
            ch("vector", lambda e, k=k: e.tensor_copy(place[:, k, :], top[:]))
            ch("vector", lambda e, k=k: e.tensor_scalar(pi[:], place[:, k, :], P - 1, None, ALU.bitwise_and))
            ch("vector", lambda e, k=k: e.tensor_copy(row[:, k, :], pi[:]))
            ch("vector", lambda e, k=k: e.tensor_scalar(pi[:], place[:, k, :], 7, None, ALU.logical_shift_right))
            ch("vector", lambda e, k=k: e.tensor_copy(slot[:, k, :], pi[:]))
        tt(cmp[:], bc(cum[:], 1, SLOTS), bc(K["slot"], 2, E), ALU.is_le)
        red(se[:], cmp[:], ALU.add)
        ch("vector", lambda e: e.tensor_scalar(expert[:], se[:], float(E - 1), None, ALU.min))
        ch.run()
        Q = 4
        lp = Loop(nc, NT // Q // 2 * 2, "sr")
        lanes = [{"r": sb(f"r_is{L}", [P, Q, P]), "s": sb(f"s_is{L}", [P, Q, SLOTS])} for L in LANES]
        psrc = pfx

        def s_hot(L, d):
            def at(a, t):
                return a[:, L, bass.ds(t * Q, Q)]
            lp.step("vector", lambda e, t: e.tensor_tensor(d["r"][:], bc(K["row"], 1, Q), bc(at(row, t), 2, P),
                                                           ALU.is_equal), frees=[f"mm{L}"])
            lp.step("vector", lambda e, t: e.tensor_tensor(d["s"][:], bc(K["slot"], 1, Q), bc(at(slot, t), 2, SLOTS),
                                                           ALU.is_equal), done=f"s1{L}")
            lp.step("vector", lambda e, t: e.tensor_tensor(d["s"][:], d["s"][:],
                                                           bc(K["token"][:, bass.ds(t * Q, Q)], 2, SLOTS), ALU.mult),
                    [f"s1{L}"], done=f"hot{L}")

            def mm(e, t):
                for q in range(Q):
                    i = e.matmul(psrc[:, 0:SLOTS], d["r"][:, q], d["s"][:, q], start=False, stop=False,
                                 skip_group_check=True)
                return i
            lp.step("tensor", mm, [f"hot{L}"], done=f"mm{L}")

        ch = Chain(nc, "clear")
        ch("vector", lambda e: e.memset(lanes[0]["s"][:], 0.0))
        ch("tensor", lambda e: e.matmul(psrc[:, 0:SLOTS], K["ones"], lanes[0]["s"][:, 0], start=True, stop=False,
                                        skip_group_check=True))
        ch.run()
        lp.pipeline([(0, s_hot)], lanes)
        lp.run()
        ch = Chain(nc, "source")
        ch("vector", lambda e: e.tensor_copy(source[:], psrc[:, 0:SLOTS]))
        ch.run()


def experts(nc, xn1, yg, w13, w2, source, expert, K, C, KC, E, SLOTS, F):
    KF = -(-F // P)
    FR = F - (KF - 1) * P
    H = F // 2
    with memory(nc, "ex") as (sb, ps):
        lp = Loop(nc, SLOTS // 2, "ex")
        hb = [ps(f"hb{i}", [P, 512]) for i in range(4)]
        tb, xb, yb = [ps("tb0", [P, 512]), ps("tb1", [P, 512])], ps("xb", [P, 512]), ps("yb", [P, 512])
        lanes = [{n: sb(f"{n}{L}", s, I32 if n == "idx" else F32) for n, s in (
            ("xa", [P, C]), ("xT", [P, KC, P]), ("g", [P, F]), ("gT", [P, KF, P]), ("yo", [P, C]),
            ("idx", [P, 1]))} for L in LANES]

        def s_in(L, d):
            lp.step("gpsimd", lambda e, t: e.tensor_copy(d["idx"][:], source[:, bass.ds(2 * t + L, 1)]),
                    frees=[f"xTp{L}"], done=f"idx{L}", apart=True)
            lp.step("gpsimd", lambda e, t: e.indirect_dma_start(
                d["xa"][:], None, xn1, bass.IndirectOffsetOnAxis(ap=d["idx"][:, 0:1], axis=0)),
                [f"idx{L}"], done=f"xa{L}", dma=True, apart=True)

        def s_xT(L, d):
            r, f = lp.before("xT", L)
            transposes(lp, L, "xT", d["xa"], xb, d["xT"][:], K["ident"], [f"xa{L}", *r], frees=f,
                       keeps=[f"h1{L}"])

        def s_expert(L, d):
            d["register"] = x = {}

            def load(e, t):
                x[0] = e.value_load(expert[0:1, bass.ds(2 * t + L, 1)], min_val=0, max_val=E - 1)
            lp.step("tensor", load)

        def s_h(L, d):
            x = d["register"]

            def up(half, part):
                def f(e, t):
                    for k in range(KC):
                        i = e.matmul(hb[2 * half + part][:, 0:H], d["xT"][:, k, :],
                                     w13[:, bass.ds(2 * x[0] + part, 1), k, half * H:(half + 1) * H],
                                     start=(k == 0), stop=(k == KC - 1))
                    return i
                return f
            for half in range(2):
                r, f = lp.before(f"g{half}", L)
                lp.step("tensor", up(half, 0), [f"xT{L}", *r], f)
                lp.step("tensor", up(half, 1), done=f"h{half}{L}")
                g = d["g"][:, half * H:(half + 1) * H]
                lp.step("scalar", lambda e, t, g=g, half=half: e.activation(g, hb[2 * half][:, 0:H], ACT.Silu),
                        [f"h{half}{L}"], frees=[f"gTp{L}"], done=f"si{half}{L}")
                lp.step("vector", lambda e, t, g=g, half=half: e.tensor_tensor(g, g, hb[2 * half + 1][:, 0:H],
                                                                               ALU.mult),
                        [f"si{half}{L}"], done=f"g{half}{L}")

        def s_gT(L, d):
            ra, fa = lp.before("ta", L)
            rc, fc = lp.before("tc", L)

            def tr(e, t):
                for k in range(KF):
                    n = P if k < KF - 1 else FR
                    i = e.transpose(tb[k // 4][0:n, (k % 4) * P:(k % 4 + 1) * P], d["g"][:, k * P:k * P + n],
                                    K["ident"])
                return i
            lp.step("tensor", tr, [f"g1{L}", *ra, *rc], [*fa, *fc], done=f"gTp{L}")
            lp.step("scalar", lambda e, t: e.copy(d["gT"][:, 0:4], chunks(tb[0][:], 4)), [f"gTp{L}"],
                    frees=[f"y{L}"], done=f"ta{L}")

            def rest(e, t):
                e.tensor_copy(d["gT"][:, 4, :], tb[1][:, 0:P])
                return e.tensor_copy(d["gT"][0:FR, 5, :], tb[1][0:FR, P:2 * P])
            lp.step("vector", rest, [f"gTp{L}"], frees=[f"y{L}"], done=f"tc{L}")

        def s_y(L, d):
            r, f = lp.before("yo", L)

            def y(e, t):
                x = e.value_load(expert[0:1, bass.ds(2 * t + L, 1)], min_val=0, max_val=E - 1)
                for k in range(KF):
                    n = P if k < KF - 1 else FR
                    i = e.matmul(yb[:, 0:C], d["gT"][0:n, k, :], w2[0:n, bass.ds(KF * x + k, 1), :],
                                 start=(k == 0), stop=(k == KF - 1))
                return i
            lp.step("tensor", y, [f"ta{L}", f"tc{L}", *r], f, done=f"y{L}", apart=True)
            lp.step("scalar", lambda e, t: e.copy(d["yo"][:], yb[:, 0:C]), [f"y{L}"], frees=[f"yst{L}"],
                    done=f"yo{L}")
            lp.step("sync", lambda e, t: e.dma_start(tile_rows(yg, t, L), d["yo"][:]), [f"yo{L}"],
                    done=f"yst{L}", dma=True)

        lp.pipeline([(0, s_in), (2, s_expert), (1, s_xT), (3, s_gT), (2, s_h), (3, s_y)], lanes)
        lp.run()


TWO_PI = 2 * np.pi
TURN_HI = 6.28125
TURN_MID = float(np.float32(round((TWO_PI - TURN_HI) * 2 ** 21) / 2 ** 21))
TURN_LO = float(TWO_PI - TURN_HI - TURN_MID)
TO_INT = 1.5 * 2 ** 23
PI_BELOW = float(np.nextafter(np.float32(np.pi), np.float32(0)))


def attention_weights(sb, A, C, KC):
    W = {n: sb(f"la_{n}", s) for n, s in (
        ("wq", [P, KC, 2 * C]), ("wk", [P, KC, 2 * C]), ("wv", [P, KC, C]), ("wo", [P, KC, C]),
        ("g1", [P, KC, P]), ("g2", [P, C]),
        ("gamma", [P, C]), ("beta", [P, C]), ("theta", [P, 4]))}
    return W, ([(W[n][:], kcn(A[a])) for n, a in (("wq", "Wq2"), ("wk", "Wk2"), ("wv", "Wv"), ("wo", "Wo"), ("g1", "G1"))]
               + [(W["g2"][:], A["G2"]), (W["theta"][:], A["theta2"])]
               + [(W[n][:], A[n].partition_broadcast(P)) for n in ("gamma", "beta")])


def linear_attention(nc, A, W, x1, ysh, yg, weight, place, x2, x3, xn3T, K, T, C, KC, loads,
                     later_pairs):
    S = T // 2
    CH = 4
    HD = C // HEADS
    ident = K["ident"]
    with memory(nc, "la") as (sb, ps):
        wq, wk, wv, wo, g1, g2, gamma, beta, theta = (W[n] for n in (
            "wq", "wk", "wv", "wo", "g1", "g2", "gamma", "beta", "theta"))
        pos = sb("pos", [P, P])
        ang, trn, red, cs = (sb(n, [P, CH, P]) for n in ("ang", "trn", "red", "cs"))
        lanes = []
        for L in LANES:
            d = {n: sb(f"{n}{L}", s) for n, s in (
                ("xa", [P, C]), ("ys", [P, C]), ("a0", [P, C]), ("a1", [P, C]), ("ym", [P, C]), ("zm", [P, C]),
                ("x2", [P, C]), ("xb", [P, C]), ("xn", [P, C]), ("xnT", [P, KC, P]), ("t1", [P, P]),
                ("gt", [P, C]), ("qs", [P, CH, P]), ("ks", [P, CH, P]), ("qT", [P, CH, P]), ("kT", [P, CH, P]),
                ("qM", [P, CH, 4, P]), ("v", [P, HEADS, 2 * HD]), ("state", [P, CH, 64]),
                ("em", [P, CH, 4, P]), ("kt", [P, CH, P]), ("up", [P, CH, 64]), ("oT", [P, KC, P]), ("y", [P, C]), ("yn", [P, C]),
                ("yb", [P, C]), ("zn", [P, C]), ("xo", [P, C]), ("w", [P, C]), ("wT", [P, KC, P]))}
            d["idx"] = sb(f"idx{L}", [P, 2], I32)
            for n in ("0", "x", "1", "2", "3"):
                d[f"ln{n}"] = LayerNorm(sb, f"ln{n}_{L}", K["half"])
            lanes.append(d)
        bE = ps("E", [P, CH, 512])
        bA, bB, bX, bO = ps("A", [P, 512]), ps("B", [P, 512]), ps("X", [P, 512]), ps("O", [P, 512])
        lp = Loop(nc, S // P, "la")
        lp.open("vector", lambda e: e.tensor_copy(pos[:], K["row"]))
        for d, engine in zip(lanes, ("vector", "gpsimd")):
            for n in ("state", "v", "qM"):
                lp.open(engine, lambda e, d=d, n=n: e.memset(d[n][:], 0.0))
        later = Loads(nc, "l_later", later_pairs, (lp, 1))

        def rows(dr, t, L):
            return dr[bass.ds(t * P + L * S, P), :]

        def s_turns(L, d):
            if L:
                return
            lp.lag = 0

            def mul(e, t):
                for c in range(CH):
                    i = e.tensor_scalar(ang[:, c], pos[:], theta[:, c:c + 1], None, ALU.mult)
                return i
            lp.step("vector", mul, done="ang")
            lp.step("vector", lambda e, t: e.tensor_scalar(pos[:], pos[:], float(P), None, ALU.add), ["ang"],
                    done="pos")
            lp.step("vector", lambda e, t: e.tensor_scalar(trn[:], ang[:], float(1 / TWO_PI), K["quarter"],
                                                           ALU.mult, ALU.add), ["ang"], done="trn_q")
            lp.step("vector", lambda e, t: e.tensor_scalar(trn[:], trn[:], TO_INT, TO_INT, ALU.add, ALU.subtract),
                    ["trn_q"], done="trn")

        def s_reduce(L, d):
            if not L:
                return
            lp.lag = 0
            src, prev = ang, "trn"
            for n, part in (("hi", TURN_HI), ("mid", TURN_MID), ("lo", TURN_LO)):
                lp.step("vector", lambda e, t, src=src, part=part: e.scalar_tensor_tensor(
                    red[:], trn[:], -part, src[:], ALU.mult, ALU.add), [prev], last=["cs"], done=n)
                src, prev = red, n
            lp.step("vector", lambda e, t: e.tensor_scalar(red[:], red[:], K["quarter_rad"], PI_BELOW,
                                                           ALU.add, ALU.min), ["lo"], done="cl")
            lp.step("vector", lambda e, t: e.tensor_scalar(red[:], red[:], -PI_BELOW, None, ALU.max), ["cl"],
                    done="red")

        def s_sin(L, d):
            if not L:
                return
            lp.lag = 1
            lp.step("scalar", lambda e, t: e.activation(cs[:], red[:], ACT.Sin), ["red"], frees=["kT0", "kT1"],
                    done="cs")

        def s_in(L, d):
            lp.step("sync", lambda e, t: e.dma_start(d["xa"][:], rows(x1, t, L)), frees=[f"x2{L}"],
                    done=f"xa{L}", dma=True)
            lp.step("sync", lambda e, t: e.dma_start(d["ys"][:], rows(ysh, t, L)), frees=[f"y0{L}"],
                    done=f"ys{L}", dma=True)
            lp.step("gpsimd", lambda e, t: e.tensor_copy(
                d["idx"][:].unsqueeze(2), place[:, :, bass.ds(t + L * (S // P), 1)]), frees=[f"y1{L}"],
                done=f"idx{L}", apart=True)
            for k in range(2):
                lp.step("gpsimd", lambda e, t, k=k: e.indirect_dma_start(
                    d[f"a{k}"][:], None, yg, bass.IndirectOffsetOnAxis(ap=d["idx"][:, k:k + 1], axis=0)),
                    [f"idx{L}"], done=f"a{k}{L}", dma=True, apart=True)

        def s_mix(L, d):
            src = d["ys"]
            for k in range(2):
                def mix(e, t, k=k, src=src):
                    return e.scalar_tensor_tensor(d["ym"][:], d[f"a{k}"][:],
                                                  weight[:, k, bass.ds(t + L * (S // P), 1)], src[:],
                                                  ALU.mult, ALU.add)
                lp.step("vector", mix, [f"a{k}{L}", f"ys{L}" if k == 0 else f"y0{L}"],
                        frees=[f"ln_0{L}"], done=f"y{k}{L}")
                src = d["ym"]
            d["ln0"].stats(lp, f"0{L}", d["ym"][:], [f"y1{L}"])

        def s_x2(L, d):
            d["ln0"].apply(lp, f"0{L}", d["ym"][:], d["zm"][:], frees=[f"x2{L}"])
            lp.step("gpsimd", lambda e, t: e.tensor_tensor(d["x2"][:], d["zm"][:], d["xa"][:], ALU.add),
                    [f"ln_0{L}", f"xa{L}"], frees=[f"x2st{L}", f"ln_x{L}"], done=f"x2{L}")
            lp.step("sync", lambda e, t: e.dma_start(rows(x2, t, L), d["x2"][:]), [f"x2{L}"], done=f"x2st{L}",
                    dma=True)

        def s_norm(L, d):
            d["lnx"].stats(lp, f"x{L}", d["x2"][:], [f"x2{L}"])

        def s_xn(L, d):
            d["lnx"].apply(lp, f"x{L}", d["x2"][:], d["xn"][:], frees=[f"xnTp{L}"])

        def s_xT(L, d):
            transposes(lp, L, "xnT", d["xn"], bX, d["xnT"][:], ident, [f"ln_x{L}"], keeps=[f"kp{L}"],
                       last=[f"wT{1 - L}", f"xnT{1 - L}"])

        def s_t1(L, d):
            def t1(e, t):
                for k in range(KC):
                    i = e.matmul(bO[:, C:C + P], g1[:, k, :], d["xnT"][:, k, :], start=(k == 0),
                                 stop=(k == KC - 1))
                return i
            lp.step("tensor", t1, [f"xnT{L}"], last=[f"oT{L}", f"t1{1 - L}"], done=f"t1p{L}")
            lp.step("scalar", lambda e, t: e.copy(d["t1"][:], bO[:, C:C + P]), [f"t1p{L}"], frees=[f"g2{L}"],
                    done=f"t1{L}")

        def s_gate(L, d):
            lp.step("tensor", lambda e, t: e.matmul(bA[:, 0:C], d["t1"][:], g2[:], start=True, stop=True),
                    [f"t1{L}"], last=[f"kt{1 - L}", f"th{1 - L}"], done=f"g2{L}")
            lp.step("scalar", lambda e, t: e.activation(d["gt"][:], bA[:, 0:C], ACT.Tanh, scale=0.5),
                    [f"g2{L}"], frees=[f"y{L}"], done=f"th{L}")
            lp.step("vector", lambda e, t: e.tensor_scalar(d["gt"][:], d["gt"][:], 0.5, 0.5, ALU.mult, ALU.add),
                    [f"th{L}"], done=f"gt{L}")

        def s_v(L, d):
            def v(e, t):
                for k in range(KC):
                    i = e.matmul(bB[:, 0:C], d["xnT"][:, k, :], wv[:, k, :], start=(k == 0), stop=(k == KC - 1))
                return i
            lp.step("tensor", v, last=[f"y{L}", f"v{1 - L}"], done=f"vp{L}")

            def cp(e, t):
                pair = d["v"][:].rearrange("p (b h) d -> p b (h d)", h=2)
                src = bB[:, 0:C].rearrange("p (b h d) -> p b h d", h=2, d=HD)
                for h in range(2):
                    i = e.copy(pair[:, :, 3 * HD * h:3 * HD * h + HD], src[:, :, h])
                return i
            lp.step("scalar", cp, [f"vp{L}"], frees=[f"O{L}", f"ust{L}"], done=f"v{L}")

        def s_qk(which):
            def stage(L, d):
                w, bank = (wq, bE[:, 2]) if which == "q" else (wk, bE[:, 3])

                def f(e, t):
                    for c in range(CH):
                        for k in range(KC):
                            i = e.matmul(bank[:, c * P:(c + 1) * P], w[:, k, c * P:(c + 1) * P],
                                         d["xnT"][:, k, :], start=(k == 0), stop=(k == KC - 1))
                    return i
                lp.step("tensor", f, last=[f"em{2 if which == 'q' else 3}{1 - L}", f"{which}s{1 - L}"],
                        done=f"{which}p{L}")
                lp.step("scalar", lambda e, t: e.activation(d[f"{which}s"][:], chunks(bank, CH), ACT.Silu),
                        [f"{which}p{L}"], frees=[f"{which}T{L}"], done=f"{which}s{L}")
                lp.step("gpsimd", lambda e, t: e.tensor_tensor(d[f"{which}T"][:], d[f"{which}s"][:], cs[:],
                                                               ALU.mult), [f"{which}s{L}", "cs"],
                        frees=[f"O{L}", f"qM{L}"] if which == "q" else [f"ktp{L}", f"en3{L}"], done=f"{which}T{L}")
            return stage

        def s_qM(L, d):
            def cp(e, t):
                for r in range(4):
                    i = e.copy(d["qM"][32 * r:32 * r + 32, :, r, :], d["qT"][32 * r:32 * r + 32])
                return i
            lp.step("scalar", cp, [f"qT{L}"], frees=[f"en3{L}"], done=f"qM{L}")

        def s_kt(L, d):
            def tr(e, t):
                for c in range(CH):
                    i = e.transpose(bA[:, c * P:(c + 1) * P], d["kT"][:, c, :], ident)
                return i
            lp.step("tensor", tr, [f"kT{L}"], last=[f"up{1 - L}"], done=f"ktp{L}")
            lp.step("scalar", lambda e, t: e.copy(d["kt"][:], chunks(bA[:], CH)), [f"ktp{L}"],
                    frees=[f"ust{L}"], done=f"kt{L}")

        def s_energy(L, d):
            for c in range(CH):
                lp.step("tensor", lambda e, t, c=c: e.matmul(
                    bE[:, c, :], d["kT"][:, c, :], d["qM"][:, c].rearrange("p r n -> p (r n)"), start=True, stop=True),
                    [f"kT{L}", f"qM{L}"], last=[f"em{c}{1 - L}", *((), (), (f"qs{L}",), (f"ks{L}",))[c]],
                    done=f"en{c}{L}")
            for c in range(CH):
                lp.step("vector", lambda e, t, c=c: e.tensor_tensor(
                    d["em"][:, c], chunks(bE[:, c], 4), bc(K["causal"], 1, 4), ALU.mult),
                    [f"en{c}{L}"], frees=[f"O{L}"], done=f"em{c}{L}")

        def s_state(L, d):
            def u(e, t):
                pair = d["v"][:].rearrange("p (b h) (x d) -> p b (h x) d", h=2, d=HD)
                for c in range(CH):
                    i = e.matmul(bA[:, c * P:(c + 1) * P], d["kt"][:, c, :], pair[:, 4 * (c // 2):4 * (c // 2) + 4, ::3],
                                 start=True, stop=True)
                return i
            lp.step("tensor", u, [f"kt{L}", f"v{L}"], last=[f"th{1 - L}"], done=f"ust{L}")
            own = bA[:].rearrange("p (b x n) -> p b x n", b=2, n=64)[:, :, ::3]
            mask = K["own_head"].unsqueeze(1).unsqueeze(1).broadcast_to([P, 2, 2, 64])
            lp.step("vector", lambda e, t: e.tensor_tensor(d["up"][:].rearrange("p (b x) n -> p b x n", b=2), own,
                                                           mask, ALU.mult), [f"ust{L}"], done=f"up{L}")
            lp.step("vector", lambda e, t: e.tensor_tensor(d["state"][:], d["state"][:], d["up"][:], ALU.add),
                    [f"up{L}", f"O{L}"], done=f"st{L}")

        def s_attend(L, d):
            def o(e, t):
                for c in range(CH):
                    i = e.matmul(bO[64 * (c % 2):64 * (c % 2) + 64, (c // 2) * P:(c // 2 + 1) * P],
                                 d["state"][:, c, :], d["qT"][:, c, :], start=(c < 2), stop=False,
                                 skip_group_check=True)
                for h in range(HEADS):
                    g = h // 2 % 4
                    i = e.matmul(bO[32 * g:32 * g + 32, (h // 8) * P:(h // 8 + 1) * P], d["v"][:, h, :],
                                 d["em"][:, h // 4, h % 4, :], start=False, stop=(h >= HEADS - 8),
                                 skip_group_check=True)
                return i
            lp.step("tensor", o, [*(f"em{c}{L}" for c in range(CH)), f"v{L}"], frees=[f"st{L}"],
                    last=[f"t1{1 - L}", f"oT{1 - L}"], done=f"O{L}", apart=True)
            lp.step("scalar", lambda e, t: e.copy(d["oT"][:], chunks(bO[:, 0:C], KC)), [f"O{L}"],
                    frees=[f"z{L}"], done=f"oT{L}")

        def s_z(L, d):
            def z(e, t):
                for k in range(KC):
                    i = e.matmul(bB[:, C:2 * C], d["oT"][:, k, :], wo[:, k, :], start=(k == 0), stop=(k == KC - 1))
                return i
            lp.step("tensor", z, [f"oT{L}"], last=[f"v{1 - L}", f"y{1 - L}"], done=f"z{L}")
            lp.step("vector", lambda e, t: e.tensor_tensor(d["y"][:], bB[:, C:2 * C], d["gt"][:], ALU.mult),
                    [f"z{L}", f"gt{L}"], done=f"y{L}")
            d["ln1"].stats(lp, f"1{L}", d["y"][:], [f"y{L}"])
            lp.step("sync", lambda e, t: e.dma_start(d["xb"][:], rows(x2, t, L)), [f"x2st{L}"], frees=[f"xo{L}"],
                    done=f"xb{L}", dma=True)

        def s_affine(L, d):
            d["ln1"].apply(lp, f"1{L}", d["y"][:], d["yn"][:], frees=[f"be{L}"])
            lp.step("gpsimd", lambda e, t: e.tensor_tensor(d["yb"][:], d["yn"][:], gamma[:], ALU.mult),
                    [f"ln_1{L}"], frees=[f"ln_2{L}"], done=f"ga{L}")
            lp.step("gpsimd", lambda e, t: e.tensor_tensor(d["yb"][:], d["yb"][:], beta[:], ALU.add),
                    [f"ga{L}"], done=f"be{L}")

        def s_norm2(L, d):
            d["ln2"].stats(lp, f"2{L}", d["yb"][:], [f"be{L}"])

        def s_x3(L, d):
            d["ln2"].apply(lp, f"2{L}", d["yb"][:], d["zn"][:], frees=[f"xo{L}"])
            lp.step("gpsimd", lambda e, t: e.tensor_tensor(d["xo"][:], d["zn"][:], d["xb"][:], ALU.add),
                    [f"ln_2{L}", f"xb{L}"], frees=[f"out{L}", f"ln_3{L}"], done=f"xo{L}")
            lp.step("sync", lambda e, t: e.dma_start(rows(x3, t, L), d["xo"][:]), [f"xo{L}"], done=f"out{L}",
                    dma=True)

        def s_norm3(L, d):
            d["ln3"].stats(lp, f"3{L}", d["xo"][:], [f"xo{L}"])

        def s_w(L, d):
            d["ln3"].apply(lp, f"3{L}", d["xo"][:], d["w"][:], frees=[f"wTp{L}"])

        def s_wT(L, d):
            transposes(lp, L, "wT", d["w"], bX[:, C:2 * C], d["wT"][:], ident, [f"ln_3{L}"], keeps=[f"wst{L}"],
                       last=[f"xnT{L}", f"wT{1 - L}"])
            lp.step("sync", lambda e, t: e.dma_start(
                xn3T.rearrange("(k p) n -> p k n", p=P)[:, :, bass.ds(t * P + L * S, P)], d["wT"][:]), [f"wT{L}"],
                done=f"wst{L}", dma=True)

        lp.pipeline([(0, s_in), (5, s_z), (3, s_xT), (4, s_kt), (2, s_x2), (4, s_energy), (7, s_wT),
                     (3, s_t1), (3, s_v), (5, s_affine), (3, s_gate), (0, s_sin), (6, s_x3), (2, s_norm),
                     (3, s_qk("q")), (4, s_attend), (5, s_norm2), (2, s_xn), (6, s_norm3), (1, s_mix), (6, s_w),
                     (3, s_qk("k")), (3, s_qM), (4, s_state), (0, s_turns), (0, s_reduce)], lanes)
        lp.run(loads)
        return later


def recurrence_weights(sb, A, C, KC):
    names = ("wf", "wi", "wc", "wo", "uf", "ui", "uc", "uo")
    W = {n: sb(n, [P, KC, C]) for n in names}
    W |= {"bias": sb("bias", [P, 3, KC]), "c_start": sb("c_start", [P, KC]), "bo": sb("bo_row", [P, C])}
    return W, ([(W[n][:], kcn(A[n])) for n in names]
               + [(W["bias"][:, g, :], A[n]) for g, n in enumerate(("bf", "bi", "bc"))]
               + [(W["c_start"][:], A["in_c"]), (W["bo"][:], A["bo"].partition_broadcast(P))])


def gated_recurrence(nc, A, w, x3, xn3T, K, T, C, KC, loads):
    S = T // 2
    R = 256
    G = ("f", "i", "c")
    out = A["out"]
    b, c0, bo = w["bias"], w["c_start"], w["bo"]
    with memory(nc, "gr") as (sb, ps):
        b0 = sb("b_first", [P, 3, KC])
        gb = [[ps(f"g{s}{g}", [P, 512]) for g in range(3)] for s in range(2)]
        ob = [ps(f"o{s}", [P, 512]) for s in range(2)]
        lp = Loop(nc, S // (2 * R), "gr")

        def uc0(e):
            for g, n in enumerate(G):
                for m in range(KC):
                    for k in range(KC):
                        i = e.matmul(ob[0][:, g * KC + m:g * KC + m + 1], w["u" + n][:, k, m * P:(m + 1) * P],
                                     c0[:, k:k + 1], start=(k == 0), stop=(k == KC - 1))
            return i
        lp.open("tensor", uc0)
        lp.open("vector", lambda e: e.tensor_tensor(b0[:], ob[0][:, 0:3 * KC].rearrange("p (g k) -> p g k", g=3), b[:],
                                                    ALU.add), after=1)
        lanes = [{n: sb(f"{n}{L}", s) for n, s in (
            ("x0", [P, KC, R]), ("x1", [P, KC, R]), ("y0", [P, KC, R]), ("y1", [P, KC, R]),
            ("f", [P, KC, R]), ("i", [P, KC, R]), ("c", [P, KC, R]),
            ("ig", [P, KC, R]), ("fc", [P, KC, R]), ("c1", [P, KC, R]), ("c2", [P, KC, R]),
            ("h0", [P, 2, C]), ("h1", [P, 2, C]), ("r0", [P, 2, C]), ("r1", [P, 2, C]),
            *((f"{n}_{s}_", z) for s in range(2) for n, z in (
                ("st", [P, 2, 6]), ("mv", [P, 2, 2]), ("ve", [P, 2]), ("rs", [P, 2]))))} for L in LANES]

        def cols(s, t, L):
            return xn3T.rearrange("(k p) n -> p k n", p=P)[:, :, bass.ds(t * 2 * R + L * R + s * S, R)]

        def tok(dr, s, t, L):
            return dr[bass.ds(t * 2 * R + L * R + s * S, R), :].rearrange("(q p) c -> p q c", p=P)

        def s_load(name, s, used):
            def stage(L, d):
                lp.step("sync", lambda e, t: e.dma_start(d[f"{name}{s}"][:], cols(s, t, L)), frees=[f"{used}{L}"],
                        done=f"{name}{s}{L}", dma=True)
            return stage

        def s_rows(s):
            def stage(L, d):
                lp.step("sync", lambda e, t: e.dma_start(d[f"r{s}"][:], tok(x3, s, t, L)), frees=[f"xo{s}{L}"],
                        done=f"r{s}{L}", dma=True)
            return stage

        def s_gates(s):
            def stage(L, d):
                for g, n in enumerate(G):
                    bank = gb[s][g]

                    def wx(e, t, n=n, bank=bank):
                        for m in range(KC):
                            o = bank[:, m * R:(m + 1) * R]
                            for k in range(KC):
                                i = e.matmul(o, w["w" + n][:, k, m * P:(m + 1) * P], d[f"x{s}"][:, k, :],
                                             start=(k == 0), stop=(s == 0 and k == KC - 1))
                            if s:
                                for k in range(KC):
                                    i = e.matmul(o, w["u" + n][:, k, m * P:(m + 1) * P], d["c1"][:, k, :],
                                                 start=False, stop=(k == KC - 1))
                        return i
                    lp.step("tensor", wx, [f"x{s}{L}"] + ([f"c1{L}"] if s else []), last=[f"n{n}{s}{1 - L}"],
                            done=f"g{n}{s}{L}")

                    def act(e, t, n=n, bank=bank, g=g):
                        for m in range(KC):
                            i = e.activation(d[n][:, m], bank[:, m * R:(m + 1) * R],
                                             ACT.Tanh if n == "c" else ACT.Sigmoid,
                                             bias=(b if s else b0)[:, g, m:m + 1])
                        return i
                    lp.step("scalar", act, [f"g{n}{s}{L}"] + ([f"c1{L}"] if s else []),
                            frees=[] if s else [f"c2{L}"], done=f"n{n}{s}{L}")
                lp.step("vector", lambda e, t: e.tensor_tensor(d["ig"][:], d["i"][:], d["c"][:], ALU.mult),
                        [f"nc{s}{L}"], done=f"ig{s}{L}")
                if s == 0:
                    def c1(e, t):
                        for m in range(KC):
                            i = e.scalar_tensor_tensor(d["c1"][:, m], d["f"][:, m], c0[:, m:m + 1], d["ig"][:, m],
                                                       ALU.mult, ALU.add)
                        return i
                    lp.step("vector", c1, [f"ig0{L}"], frees=[f"gc1{L}"], done=f"c1{L}")
                else:
                    lp.step("vector", lambda e, t: e.tensor_tensor(d["fc"][:], d["f"][:], d["c1"][:], ALU.mult),
                            done=f"fc{L}")
                    lp.step("vector", lambda e, t: e.tensor_tensor(d["c2"][:], d["fc"][:], d["ig"][:], ALU.add),
                            [f"fc{L}", f"ig1{L}"], frees=[f"o1{L}"], done=f"c2{L}")
            return stage

        def s_out(s):
            def stage(L, d):
                h = d[f"h{s}"]
                st, mv, ve, rs = (d[f"{n}_{s}_"] for n in ("st", "mv", "ve", "rs"))

                def o(e, t):
                    for q in range(2):
                        for m, (a, wt) in enumerate(((d[f"y{s}"], w["wo"]), (d["c2"], w["uo"]))):
                            for k in range(KC):
                                i = e.matmul(ob[s][:, q * C:(q + 1) * C], a[:, k, q * P:(q + 1) * P], wt[:, k, :],
                                             start=(m == 0 and k == 0), stop=(m == 1 and k == KC - 1))
                    return i
                lp.step("tensor", o, [f"c2{L}", f"y{s}{L}"], last=[f"hb{s}{1 - L}"], done=f"o{s}{L}")
                lp.step("vector", lambda e, t: e.tensor_tensor(h[:], chunks(ob[s][:], 2), bc(bo[:], 1, 2), ALU.add),
                        [f"o{s}{L}"], frees=[f"out{s}{L}"], done=f"hb{s}{L}")
                lp.step("scalar", lambda e, t: e.activation(h[:], h[:], ACT.Tanh), [f"hb{s}{L}"], done=f"h{s}{L}")

                def each(fn):
                    def f(e, t):
                        for q in range(2):
                            i = fn(e, q)
                        return i
                    return f
                lp.step("vector", each(lambda e, q: e.bn_stats(st[:, q], h[:, q])), [f"h{s}{L}"], done=f"st{s}{L}")
                lp.step("vector", each(lambda e, q: e.bn_aggr(mv[:, q], st[:, q])), [f"st{s}{L}"],
                        done=f"mv{s}{L}", apart=True)
                lp.step("gpsimd", lambda e, t: e.tensor_scalar(ve[:], mv[:, :, 1], LN_EPS, None, ALU.add),
                        [f"mv{s}{L}"], done=f"ve{s}{L}", apart=True)
                lp.step("gpsimd", lambda e, t: e.tensor_tensor(rs[:], ve[:], K["half"].broadcast_to([P, 2]), ALU.pow),
                        [f"ve{s}{L}"], done=f"rs{s}{L}")
                lp.step("vector", each(lambda e, q: e.tensor_scalar(h[:, q], h[:, q], mv[:, q, 0:1], rs[:, q:q + 1],
                                                                    ALU.subtract, ALU.mult)),
                        [f"rs{s}{L}"], done=f"ln{s}{L}")
                lp.step("gpsimd", lambda e, t: e.tensor_tensor(h[:], h[:], d[f"r{s}"][:], ALU.add),
                        [f"ln{s}{L}", f"r{s}{L}"], done=f"xo{s}{L}")
                lp.step("sync", lambda e, t: e.dma_start(tok(out, s, t, L), h[:]), [f"xo{s}{L}"],
                        done=f"out{s}{L}", dma=True)
            return stage

        lp.pipeline([(0, s_load("x", 0, "gc0")), (1, s_load("x", 1, "gc1")), (2, s_load("y", 0, "o0")),
                     (2, s_load("y", 1, "o1")), (2, s_rows(0)), (2, s_rows(1)), (2, s_gates(1)), (3, s_out(0)),
                     (1, s_gates(0)), (3, s_out(1))], lanes)
        lp.run(loads)



def inputs(given):
    def g(name):
        return np.asarray(given[name])

    def t(name):
        return np.ascontiguousarray(g(name).T)

    def twice(a):
        a = a.reshape(*a.shape[:-1], HEADS, 1, -1)
        return np.ascontiguousarray(np.concatenate([a, a], -2).reshape(*a.shape[:-3], -1))

    def padded(a, shape):
        out = np.zeros(shape, a.dtype)
        out[:a.shape[0], :a.shape[1]] = a
        return out
    ffn, att, rec = "L0_ffn_", "L1_attn_", "L1_ffn_"
    d = {"x": np.ascontiguousarray(g("L0_attn_x").reshape(-1, 256)), "w_attnT": t("L0_attn_w_attn"),
         "w_projT": t("L0_attn_w_proj"), "gateT": padded(t(ffn + "gate_w"), (256, 96)),
         "G1": padded(g(att + "G1"), (256, P)), "G2": padded(g(att + "G2"), (P, 256))}
    d |= {n: g(ffn + n) for n in ("sw1", "sw2", "sw3")}
    d["w13"] = np.stack([g(ffn + "w1"), g(ffn + "w3")], 1).reshape(-1, g(ffn + "w1").shape[-1])
    d["w2"] = np.concatenate([padded(a, (-(-a.shape[0] // P) * P, 256)) for a in g(ffn + "w2")])
    d |= {n: g(att + n) for n in ("Wv", "Wo", "gamma", "beta")}
    d |= {"Wq2": twice(g(att + "Wq")), "Wk2": twice(g(att + "Wk")),
          "theta2": np.ascontiguousarray(twice(g(att + "theta").reshape(1, -1)).reshape(4, P).T)}
    d |= {n: t(rec + n) for n in ("wf", "wi", "wc", "wo", "uf", "ui", "uc", "uo")}
    d |= {n: np.ascontiguousarray(g(rec + n).reshape(-1, P).T) for n in ("bf", "bi", "bc", "in_c")}
    d["bo"] = g(rec + "bo")
    d["consts"] = np.concatenate([np.asarray(v, np.float32) for v in const_layout().values()], 1)
    return d


def kernel(**given):
    import concourse.bacc as bacc
    from concourse.bass_utils import run_bass_kernel_spmd

    nc = bacc.Bacc("TRN2", target_bir_lowering=False, num_devices=1)
    arrays, A = {}, {}
    for name, a in inputs(given).items():
        arrays[f"in_{name}"] = a
        A[name] = nc.dram_tensor(f"in_{name}", a.shape, mybir.dt.from_np(a.dtype), kind="ExternalInput").ap()
    shape = given["L0_attn_x"].shape
    A["out"] = nc.dram_tensor("out", [shape[0] * shape[1], shape[2]], F32, kind="ExternalOutput").ap()

    def dram(name, shape, dt):
        return nc.dram_tensor(name, list(shape), dt, kind="Internal").ap()
    build(nc, A, dram)
    r = run_bass_kernel_spmd(nc, [arrays], core_ids=[0])
    return r.results[0]["out"].reshape(shape)
```

```python
from contextlib import ExitStack, contextmanager

import numpy as np

import concourse.bass as bass
from concourse import mybir

P = 128
F32 = mybir.dt.float32
F16 = mybir.dt.float16
I32 = mybir.dt.int32
ALU = mybir.AluOpType
ACT = mybir.ActivationFunctionType
AX_X = mybir.AxisListType.X
LANES = (0, 1)
LN_EPS = 1e-5


class Loop:

    def __init__(self, nc, items, name):
        self.nc, self.items, self.name = nc, items, name
        self.queues = {e: [] for e in ("sync", "scalar", "vector", "gpsimd", "tensor")}
        self.count, self.lag = {}, 0
        self.laid = {}
        self.shared, self.start = {}, {}
        self.software = set()
        self.opening, self.asides, self.ahead = [], [], ("sync", "gpsimd")

    def step(self, engine, emit, reads=(), frees=(), done=None, dma=False, apart=False, last=()):
        waits = [(n, 2) for n in reads] + [(n, 1) for n in frees]
        recent = [(n, len(self.laid)) for n in last]
        if done is not None:
            self.laid[done] = (len(self.laid), self.lag)
            if dma:
                sem = self.nc.alloc_semaphore(f"{self.name}_{done}")
                self.count[done] = (sem, 16, 0)
                if engine == "gpsimd":
                    self.software.add(done)
            elif done[-1] in "01":
                if done[:-1] not in self.shared:
                    self.shared[done[:-1]] = self.nc.alloc_semaphore(f"{self.name}_{done[:-1]}_lanes")
                sem = self.shared[done[:-1]]
                self.count[done] = (sem, 2, int(done[-1]) - 1)
            else:
                sem = self.nc.alloc_semaphore(f"{self.name}_{done}")
                self.count[done] = (sem, 1, 0)
            if done not in self.software:
                self.start[id(sem)] = (engine, sem, self.count[done][1])
        self.queues[engine].append((emit, waits, recent, done, dma, apart or engine == "sync", self.lag))

    def open(self, engine, emit, after=0):
        self.opening.append((engine, emit, after))

    def aside(self, engine, turn, emit):
        self.asides.append((engine, turn, emit))

    def before(self, name, L):
        return ([f"{name}0"], []) if L else ([], [f"{name}1"])

    def pipeline(self, stages, lanes):
        for slot in LANES:
            for h, stage in stages:
                L = (slot - h) % 2
                self.lag = (h - slot + L) // 2
                stage(L, lanes[L])
        self.lag = 0

    def _runs(self, name, lag, ahead):
        _, unit, offset = self.count[name]
        return lag, ahead - (name in self.software), unit, offset

    def run(self, loads=()):
        self.loads = loads
        opened = self.nc.alloc_semaphore(f"{self.name}_opened")
        for queue in self.queues.values():
            for _, waits, recent, _, _, _, lag in queue:
                for n, place in recent:
                    at, its_lag = self.laid[n]
                    waits.append((n, 2 + lag - its_lag - (at >= place)))
                furthest = {}
                for n, ahead in waits:
                    sem, unit, offset = self.count[n]
                    furthest.setdefault(id(sem), []).append((ahead * unit + offset, (n, ahead)))
                waits[:] = [max(w)[1] for w in furthest.values()]
        assert not any(n in self.software and ahead < 2 for q in self.queues.values() for s in q for n, ahead in s[1])
        passed = self.nc.alloc_semaphore(f"{self.name}_passed")
        with self.nc.Block() as block:
            for engine, queue in self.queues.items():
                if queue or any(on == engine for on, _, _ in self.opening):
                    self._engine(block, engine, queue, passed, opened)
        sems = {id(c[0]): c[0] for c in self.count.values()}
        self.nc.clear_and_free_semaphores([passed, opened, *(x.sem for x in loads), *sems.values()])
        self.nc.all_engine_barrier()

    def _engine(self, block, engine, queue, passed, opened):
        decorate = {"sync": block.sync, "scalar": block.scalar, "vector": block.vector,
                    "gpsimd": block.gpsimd, "tensor": block.tensor}[engine]
        assert all(turn < max(q[-1] for qs in self.queues.values() for q in qs) for _, turn, _ in self.asides)
        depth = max(q[-1] for qs in self.queues.values() for q in qs)

        def work(eng, turn, due):
            peeled = isinstance(turn, int)
            for emit, waits, _, done, dma, apart, lag in queue:
                if peeled and not 0 <= turn - lag < self.items:
                    continue
                for n, ahead in waits:
                    if not peeled or turn - lag + ahead > 0:
                        eng.wait_ge(self.count[n][0], due(*self._runs(n, lag, ahead)))
                if apart and waits:
                    eng.sem_inc(passed, 1)
                last = emit(eng, turn - lag)
                if done is not None:
                    last.then_inc(self.count[done][0], 16 if dma else 1)

        def fixed(turn):
            return lambda lag, ahead, unit, offset: min(turn - lag + ahead, self.items + 1) * unit + offset

        def body(eng):
            for on, sem, units in self.start.values():
                if on == engine:
                    eng.sem_inc(sem, units)
            if engine != "sync":
                for x in self.loads:
                    eng.wait_ge(x.sem, 16 * x.n)
            for on, emit, after in self.opening:
                if on == engine:
                    if after:
                        eng.wait_ge(opened, after)
                    emit(eng).then_inc(opened, 1)
            if not queue:
                return
            if self.opening and engine not in self.ahead:
                eng.wait_ge(opened, len(self.opening))
            for turn in range(depth):
                work(eng, turn, fixed(turn))
                for on, at, emit in self.asides:
                    if (on, at) == (engine, turn):
                        emit(eng)
            with eng.Fori(depth, self.items) as turn:
                need = sorted({self._runs(n, s[-1], ahead) for s in queue for n, ahead in s[1]})
                regs = {k: eng.snap((turn + (k[1] - k[0])) * k[2] + k[3]) for k in need}
                work(eng, turn, lambda *k: regs[k])
            for turn in range(self.items, self.items + depth):
                work(eng, turn, fixed(turn))
            for _, _, _, done, dma, _, _ in queue:
                if dma:
                    eng.wait_ge(self.count[done][0], 16 * (self.items + (done not in self.software)))
        decorate(body)


@contextmanager
def memory(nc, phase):
    with ExitStack() as stack:
        def sb(name, shape, dt=F32):
            return stack.enter_context(nc.sbuf_tensor(f"{phase}_{name}", list(shape), dt))

        def ps(name, shape):
            return stack.enter_context(nc.psum_tensor(f"{phase}_{name}", list(shape), F32))
        yield sb, ps


def bc(ap, dim, n):
    return ap.unsqueeze(dim).broadcast_to([*ap.shape[:dim], n, *ap.shape[dim:]])


class LayerNorm:

    def __init__(self, sb, name, half):
        self.st, self.mv = sb(f"{name}_st", [P, 6]), sb(f"{name}_mv", [P, 2])
        self.ve, self.rstd, self.half = sb(f"{name}_ve", [P, 1]), sb(f"{name}_rs", [P, 1]), half

    def stats(self, lp, tag, src, reads):
        lp.step("vector", lambda e, t: e.bn_stats(self.st[:], src), reads, done=f"st_{tag}")
        lp.step("vector", lambda e, t: e.bn_aggr(self.mv[:], self.st[:]), [f"st_{tag}"], [f"ln_{tag}"],
                done=f"mv_{tag}", apart=True)
        lp.step("gpsimd", lambda e, t: e.tensor_scalar(self.ve[:], self.mv[:, 1:2], LN_EPS, None, ALU.add),
                [f"mv_{tag}"], done=f"ve_{tag}", apart=True)
        lp.step("gpsimd", lambda e, t: e.tensor_tensor(self.rstd[:], self.ve[:], self.half, ALU.pow),
                [f"ve_{tag}"], [f"ln_{tag}"], done=f"rs_{tag}")

    def apply(self, lp, tag, src, out, reads=(), frees=()):
        lp.step("vector", lambda e, t: e.tensor_scalar(out, src, self.mv[:, 0:1], self.rstd[:, 0:1],
                                                       ALU.subtract, ALU.mult),
                [f"rs_{tag}", *reads], frees, done=f"ln_{tag}")


def const_layout(T=4096, C=256, heads=16, experts=8, slots=72):
    p, nt = np.arange(P), T // P
    e, t = np.divmod(np.arange(experts * nt), nt)
    return {
        "ident": np.eye(P),
        "half": np.full((P, 1), -0.5),
        "head_of_16": (p // 16)[:, None] == np.arange(8),
        "before": p[:, None] < p[None, :],
        "ones": np.ones((P, P)),
        "rank": np.tile(experts - np.arange(experts), (P, 1)),
        "goes_on": np.tile(t > 0, (P, 1)),
        "one_e": np.ones((P, experts)),
        "slot": np.tile(np.arange(slots), (P, 1)),
        "token": p[:, None] + P * np.arange(nt)[None, :] - T // 2,
        "causal": p[:, None] <= p[None, :],
        "own_head": (p // 32)[:, None] == (np.arange(64) // 16),
        "row": np.tile(p, (P, 1)),
    }


def tile_rows(dr, t, L, n=P):
    return dr[bass.ds(t * 2 * n + L * n, n), :]


def chunks(ap, k):
    return ap.rearrange("p (k n) -> p k n", k=k)


def build(nc, A, dram):
    T, C = A["x"].shape
    KC = C // P
    NT = T // P
    E, F = A["w13"].shape[0] // (2 * C), A["w13"].shape[1]
    KF = -(-F // P)
    SLOTS = (2 * T // P + E) // 2 * 2
    x1, xn1, ysh = dram("x1", [T, C], F32), dram("xn1", [T, C], F32), dram("ysh", [T, C], F32)
    yg = dram("yg", [SLOTS * P, C], F32)
    x2, x3, xn3T = dram("x2", [T, C], F32), dram("x3", [T, C], F32), dram("xn3T", [C, T], F32)
    with ExitStack() as keep:
        def sb(name, shape, dt=F32):
            return keep.enter_context(nc.sbuf_tensor(name, list(shape), dt))
        lay = const_layout(T, C, HEADS, E, SLOTS)
        consts = sb("consts", [P, sum(v.shape[1] for v in lay.values())])
        K, at = {}, 0
        for n, v in lay.items():
            K[n] = consts[:, at:at + v.shape[1]]
            at += v.shape[1]
        logits, weight = sb("logits", [P, NT, E]), sb("weight", [P, 2, NT])
        place, source = sb("place", [P, 2, NT], I32), sb("source", [P, SLOTS], I32)
        expert = sb("expert", [P, SLOTS], I32)
        W, attention_pairs = attention_weights(sb, A, C, KC)
        first = Loads(nc, "l_consts", [(consts[:], A["consts"])])
        pieces = NT // 2
        with ExitStack() as moe:
            w13 = moe.enter_context(nc.sbuf_tensor("w13", [P, 2 * E, KC, F], F32))
            assert 2 * E % pieces == 0 and E * KF % pieces == 0

            def w13_piece(e, t):
                n = 2 * E // pieces
                return e.dma_start(w13[:, bass.ds(t * n, n)].rearrange("p n k f -> p (n k) f"),
                                   A["w13"][bass.ds(t * n * C, n * C), :].rearrange("(k p) f -> p k f", p=P))

            def w2_piece(e, t):
                n = E * KF // pieces
                return e.dma_start(w2[:, bass.ds(t * n, n), :],
                                   A["w2"][bass.ds(t * n * P, n * P), :].rearrange("(k p) n -> p k n", p=P))
            S, shared_pairs = shared_weights(lambda n, z: moe.enter_context(nc.sbuf_tensor(f"se_{n}", z, F32)), A, C, KC)
            loads = window_attention(nc, A, x1, K, C, KC, NT, first, shared_pairs, attention_pairs, w13_piece)
            w2 = moe.enter_context(nc.sbuf_tensor("w2", [P, E * KF, C], F32))
            shared_expert(nc, A, S, x1, xn1, ysh, logits, K, C, KC, NT, E, loads[:1], w2_piece)
            route(nc, logits, weight, place, source, expert, K, T, NT, E, SLOTS)
            experts(nc, xn1, yg, w13, w2, source, expert, K, C, KC, E, SLOTS, F)
        with memory(nc, "gw") as (sb, _):
            w, pairs = recurrence_weights(sb, A, C, KC)
            gates = linear_attention(nc, A, W, x1, ysh, yg, weight, place, x2, x3, xn3T, K, T, C, KC,
                                     loads[1:], pairs)
            gated_recurrence(nc, A, w, x3, xn3T, K, T, C, KC, [gates])


class Loads:

    def __init__(self, nc, name, pairs, beside=None):
        self.n, self.sem = len(pairs), nc.alloc_semaphore(name)

        def start(e):
            for dst, src in pairs:
                e.dma_start(dst, src).then_inc(self.sem, 16)
        if beside is None:
            with nc.Block() as block:
                block.scalar(start)
        else:
            lp, turn = beside
            lp.aside("scalar", turn, start)


def kcn(a):
    return a.rearrange("(k p) n -> p k n", p=P)


HEADS, WIN = 16, 64


def window_attention(nc, A, x1, K, C, KC, NT, first, shared_pairs, attention_pairs, w13_piece):
    D = C // HEADS
    NB = HEADS // 2
    HC = P // D
    ident = K["ident"]
    with memory(nc, "wa") as (sb, ps):
        wqkv, wp = sb("wqkv", [P, KC, 3 * C]), sb("wp", [P, KC, C])
        own = Loads(nc, "l_wa", [(wqkv[:], kcn(A["w_attnT"])), (wp[:], kcn(A["w_projT"]))])
        lanes = []
        for L in LANES:
            d = {n: sb(f"{n}{L}", s) for n, s in (
                ("xa", [P, C]), ("xr", [P, C]), ("xn", [P, C]), ("xnT", [P, KC, P]), ("qT", [P, KC, P]),
                ("km", [P, KC, HC, P]), ("k1", [P, P]), ("mx", [P, HEADS]), ("pr", [P, HEADS, WIN]), ("pT", [P, NB, P]),
                ("rec", [P, HEADS]), ("yn", [P, C]), ("yT", [P, KC, P]), ("zn", [P, C]), ("xo", [P, C]),
                ("vb", [P, 2, NB, 2, D + 1]))}
            d["ln1"], d["ln2"] = LayerNorm(sb, f"lna{L}", K["half"]), LayerNorm(sb, f"lnb{L}", K["half"])
            lanes.append(d)
        bxk, bqv, bS, bP = ps("xk", [P, 512]), ps("qv", [P, 512]), ps("S", [P, KC, 512]), ps("P", [P, 2, 512])
        bY, bZ = ps("Y", [P, 512]), ps("Z", [P, 512])
        lp = Loop(nc, NT // 2, "wa")
        for d, engine in zip(lanes, ("vector", "gpsimd")):
            lp.open(engine, lambda e, d=d: e.memset(d["vb"][:], 0.0))

        def ones(e):
            for d in lanes:
                for w in range(2):
                    for h2 in range(2):
                        i = e.memset(d["vb"][64 * h2:64 * h2 + 64, w, :, h2, D:D + 1], 1.0)
            return i
        lp.open("vector", ones, after=2)
        loads = [Loads(nc, "l_shared", shared_pairs, (lp, 0)), Loads(nc, "l_attention", attention_pairs, (lp, 1))]

        def s_load(L, d):
            lp.step("sync", lambda e, t: e.dma_start(d["xa"][:], tile_rows(A["x"], t, L)), frees=[f"ln_1{L}"],
                    done=f"xa{L}", dma=True)

        def s_piece(L, d):
            if L == 0:
                lp.step("sync", w13_piece, done="w13_loaded", dma=True)

        def s_norm(L, d):
            d["ln1"].stats(lp, f"1{L}", d["xa"][:], [f"xa{L}"])

        def s_again(L, d):
            lp.step("sync", lambda e, t: e.dma_start(d["xr"][:], tile_rows(A["x"], t, L)), frees=[f"xo{L}"],
                    done=f"xr{L}", dma=True)

        def s_xn(L, d):
            d["ln1"].apply(lp, f"1{L}", d["xa"][:], d["xn"][:], frees=[f"xnTp{L}"])

        def s_xT(L, d):
            r, f = lp.before("km", L)

            def tr(e, t):
                for k in range(KC):
                    i = e.transpose(bxk[:, k * P:(k + 1) * P], d["xn"][:, k * P:(k + 1) * P], ident)
                return i
            lp.step("tensor", tr, [f"ln_1{L}", *r], f, done=f"xnTp{L}")
            lp.step("scalar", lambda e, t: e.copy(d["xnT"][:], chunks(bxk[:, 0:C], KC)),
                    [f"xnTp{L}"], frees=[f"v{L}"], done=f"xnT{L}")

        def s_qkv(L, d):
            r, f = lp.before("vb", L)

            def proj(out, col):
                def f(e, t):
                    for c in range(KC):
                        for k in range(KC):
                            i = e.matmul(out[:, c * P:(c + 1) * P], wqkv[:, k, col + c * P:col + (c + 1) * P],
                                         d["xnT"][:, k, :], start=(k == 0), stop=(k == KC - 1))
                    return i
                return f

            def v(e, t):
                for k in range(KC):
                    i = e.matmul(bqv[:, C:2 * C], d["xnT"][:, k, :], wqkv[:, k, 2 * C:3 * C],
                                 start=(k == 0), stop=(k == KC - 1))
                return i
            lp.step("tensor", proj(bxk[:, C:2 * C], C), [f"xnT{L}"], done=f"k{L}")
            lp.step("tensor", proj(bqv[:, 0:C], 0), r, f)
            lp.step("tensor", v, done=f"v{L}")
            lp.step("scalar", lambda e, t: e.copy(d["k1"][:], bxk[:, C + P:C + 2 * P]), [f"k{L}"],
                    frees=[f"kmg{L}"], done=f"k1{L}")
            lp.step("vector", lambda e, t: e.tensor_tensor(d["km"][:, 0], bc(bxk[:, C:C + P], 1, HC),
                                                           bc(K["head_of_16"], 2, P), ALU.mult),
                    [f"k1{L}"], frees=[f"S{L}"], done=f"km{L}")
            lp.step("gpsimd", lambda e, t: e.tensor_tensor(d["km"][:, 1], bc(d["k1"][:], 1, HC),
                                                           bc(K["head_of_16"], 2, P), ALU.mult),
                    [f"k1{L}"], frees=[f"S{L}"], done=f"kmg{L}")
            lp.step("scalar", lambda e, t: e.copy(d["qT"][:], chunks(bqv[:, 0:C], KC)),
                    [f"v{L}"], frees=[f"S{L}"], done=f"qT{L}")

            def vb(e, t):
                for w in range(2):
                    for h2 in range(2):
                        src = bqv[64 * w:64 * w + 64, C:2 * C].rearrange("p (b h d) -> p b h d", b=NB, h=2)
                        i = e.copy(d["vb"][64 * h2:64 * h2 + 64, w, :, h2, 0:D], src[:, :, h2, :])
                return i
            lp.step("scalar", vb, frees=[f"pv{L}"], done=f"vb{L}")


        S3 = bS[:].rearrange("p c (h k) -> p (c h) k", k=WIN)

        def s_scores(L, d):
            r, f = lp.before("sub", L)

            def sc(e, t):
                for c in range(KC):
                    for w in range(2):
                        i = e.matmul(bS[64 * w:64 * w + 64, c, :], d["qT"][:, c, 64 * w:64 * w + 64],
                                     d["km"][:, c, :, 64 * w:64 * w + 64], start=True, stop=True)
                return i
            lp.step("tensor", sc, [f"qT{L}", f"km{L}", f"kmg{L}", *r], f, done=f"S{L}", apart=True)
            lp.step("vector", lambda e, t: e.tensor_reduce(d["mx"][:], S3, AX_X, ALU.max), [f"S{L}"], done=f"mx{L}")
            lp.step("vector", lambda e, t: e.tensor_tensor(d["pr"][:], S3, bc(d["mx"][:], 2, WIN), ALU.subtract),
                    [f"mx{L}"], frees=[f"pTp{L}"], done=f"sub{L}")

        def s_exp(L, d):
            lp.step("scalar", lambda e, t: e.activation(d["pr"][:], d["pr"][:], ACT.Exp, scale=float(D) ** -0.5),
                    [f"sub{L}"], done=f"exp{L}")

        def s_pT(L, d):
            ra, fa = lp.before("pTa", L)
            rb, fb = lp.before("pTb", L)

            def tr(e, t):
                pr = d["pr"][:].rearrange("p h k -> p (h k)")
                for b in range(NB):
                    i = e.transpose(bP[:, b // 4, (b % 4) * P:(b % 4 + 1) * P], pr[:, b * P:(b + 1) * P], ident)
                return i
            lp.step("tensor", tr, [f"exp{L}", *ra, *rb], [*fa, *fb], done=f"pTp{L}")
            for b in range(2):
                lp.step("scalar", lambda e, t, b=b: e.copy(d["pT"][:, 4 * b:4 * b + 4, :], chunks(bP[:, b], 4)),
                        [f"pTp{L}"], frees=[f"pv{L}"], done=f"pT{'ab'[b]}{L}")

        def s_pv(L, d):
            Y = bY[:, 0:HEADS * (D + 1)]
            r, f = lp.before("yn", L)

            def pv(e, t):
                for b in range(NB):
                    for w in range(2):
                        i = e.matmul(Y[64 * w:64 * w + 64, b * 34:(b + 1) * 34], d["pT"][:, b, 64 * w:64 * w + 64],
                                     d["vb"][:, w, b].rearrange("p h d -> p (h d)"), start=True, stop=True)
                return i
            lp.step("tensor", pv, [f"pTa{L}", f"pTb{L}", f"vb{L}", *r], f, done=f"pv{L}")
            Y3 = Y.rearrange("p (h d) -> p h d", h=HEADS)
            lp.step("vector", lambda e, t: e.reciprocal(d["rec"][:], Y3[:, :, D]), [f"pv{L}"], done=f"rec{L}")
            lp.step("vector", lambda e, t: e.tensor_tensor(d["yn"][:].rearrange("p (h d) -> p h d", h=HEADS),
                                                           Y3[:, :, 0:D], bc(d["rec"][:], 2, D), ALU.mult),
                    [f"rec{L}"], frees=[f"yTp{L}"], done=f"yn{L}")

        def s_yT(L, d):
            r, f = lp.before("ln_2", L)

            def tr(e, t):
                for k in range(KC):
                    i = e.transpose(bZ[:, k * P:(k + 1) * P], d["yn"][:, k * P:(k + 1) * P], ident)
                return i
            lp.step("tensor", tr, [f"yn{L}", *r], f, done=f"yTp{L}")
            lp.step("scalar", lambda e, t: e.copy(d["yT"][:], chunks(bZ[:, 0:C], KC)),
                    [f"yTp{L}"], frees=[f"z{L}"], done=f"yT{L}")

        def s_z(L, d):
            def z(e, t):
                for k in range(KC):
                    i = e.matmul(bZ[:, C:2 * C], d["yT"][:, k, :], wp[:, k, :], start=(k == 0), stop=(k == KC - 1))
                return i
            lp.step("tensor", z, [f"yT{L}"], done=f"z{L}")
            d["ln2"].stats(lp, f"2{L}", bZ[:, C:2 * C], [f"z{L}"])

        def s_out(L, d):
            d["ln2"].apply(lp, f"2{L}", bZ[:, C:2 * C], d["zn"][:], frees=[f"xo{L}"])
            lp.step("gpsimd", lambda e, t: e.tensor_tensor(d["xo"][:], d["zn"][:], d["xr"][:], ALU.add),
                    [f"ln_2{L}", f"xr{L}"], frees=[f"out{L}"], done=f"xo{L}")
            lp.step("sync", lambda e, t: e.dma_start(tile_rows(x1, t, L), d["xo"][:]), [f"xo{L}"], done=f"out{L}", dma=True)

        lp.pipeline([(0, s_load), (0, s_piece), (2, s_xT), (6, s_out), (3, s_scores), (1, s_norm), (3, s_exp), (4, s_pv),
                     (1, s_xn), (5, s_yT), (2, s_qkv), (3, s_pT), (5, s_z), (4, s_again)], lanes)
        lp.run([first, own])
        return loads


def transposes(lp, L, tag, src, bank, dst, ident, reads=(), frees=(), keeps=(), n=2, last=()):
    def tr(e, t):
        for k in range(n):
            i = e.transpose(bank[:, k * P:(k + 1) * P], src[:, k * P:(k + 1) * P], ident)
        return i
    lp.step("tensor", tr, reads, frees, last=last, done=f"{tag}p{L}")
    lp.step("scalar", lambda e, t: e.copy(dst, chunks(bank[:, 0:n * P], n)), [f"{tag}p{L}"], keeps,
            done=f"{tag}{L}")


def shared_weights(sb, A, C, KC):
    F, EW = A["sw1"].shape[1], A["gateT"].shape[1]
    W = {"sw1": sb("sw1", [P, KC, F]), "sw3": sb("sw3", [P, KC, F]), "sw2": sb("sw2", [P, F // P, C]),
         "gateT": sb("gate", [P, KC, EW])}
    return W, [(W[n][:], kcn(A[n])) for n in W]


def shared_expert(nc, A, W, x1, xn1, ysh, logits, K, C, KC, NT, E, loads, w2_piece):
    F = A["sw1"].shape[1]
    KF = F // P
    EW = A["gateT"].shape[1]
    with memory(nc, "se") as (sb, ps):
        sw1, sw3, sw2, gate = (W[n] for n in ("sw1", "sw3", "sw2", "gateT"))
        lp = Loop(nc, NT // 2, "se")
        lanes = []
        for L in LANES:
            d = {n: sb(f"{n}{L}", s) for n, s in (
                ("xa", [P, C]), ("xn", [P, C]), ("xnT", [P, KC, P]), ("g", [P, KF, P]), ("gT", [P, KF, P]),
                ("yo", [P, C]))}
            d["ln"] = LayerNorm(sb, f"ln{L}", K["half"])
            d["bx"] = ps(f"x{L}", [P, 512])
            lanes.append(d)
        b1, b3, blg, by = (ps(n, [P, 512]) for n in ("h1", "h3", "lg", "y"))

        def s_in(L, d):
            lp.step("sync", lambda e, t: e.dma_start(d["xa"][:], tile_rows(x1, t, L)), frees=[f"ln_1{L}"],
                    done=f"xa{L}", dma=True)
            if L == 0:
                lp.step("sync", w2_piece, done="w2_loaded", dma=True)

        def s_norm(L, d):
            d["ln"].stats(lp, f"1{L}", d["xa"][:], [f"xa{L}"])

        def s_xn(L, d):
            d["ln"].apply(lp, f"1{L}", d["xa"][:], d["xn"][:], frees=[f"xnTp{L}", f"xno{L}"])
            lp.step("sync", lambda e, t: e.dma_start(tile_rows(xn1, t, L), d["xn"][:]), [f"ln_1{L}"],
                    done=f"xno{L}", dma=True)

        def s_xT(L, d):
            transposes(lp, L, "xnT", d["xn"], d["bx"], d["xnT"][:], K["ident"], [f"ln_1{L}"],
                       frees=[f"xnT{L}"], keeps=[f"lgp{L}"])

        def up(d, w, out):
            def f(e, t):
                for c in range(KF):
                    for k in range(KC):
                        i = e.matmul(out[:, c * P:(c + 1) * P], w[:, k, c * P:(c + 1) * P], d["xnT"][:, k, :],
                                     start=(k == 0), stop=(k == KC - 1))
                return i
            return f

        def s_h1(L, d):
            r, f = lp.before("g", L)
            lp.step("tensor", up(d, sw1, b1), [f"xnT{L}", *r], f, done=f"h1{L}")
            lp.step("scalar", lambda e, t: e.activation(d["g"][:], chunks(b1[:, 0:F], KF), ACT.Silu),
                    [f"h1{L}"], frees=[f"gT{L}"], done=f"g{L}")

        def s_h3(L, d):
            r, f = lp.before("gT", L)
            lp.step("tensor", up(d, sw3, b3), r, f, done=f"h3{L}")
            lp.step("vector", lambda e, t: e.tensor_tensor(d["gT"][:], d["g"][:], chunks(b3[:, 0:F], KF),
                                                           ALU.mult), [f"g{L}", f"h3{L}"], frees=[f"y{L}"],
                    done=f"gT{L}")

        def s_lg(L, d):
            r, f = lp.before("lg", L)

            def lg(e, t):
                for k in range(KC):
                    i = e.matmul(blg[:, 0:EW], d["xnT"][:, k, :], gate[:, k, :], start=(k == 0), stop=(k == KC - 1))
                return i
            lp.step("tensor", lg, r, f, done=f"lgp{L}")
            lp.step("vector", lambda e, t: e.tensor_copy(
                logits[:].rearrange("p (t l) e -> p t l e", l=2)[:, bass.ds(t, 1), L, :],
                blg[:, 0:E].unsqueeze(1)), [f"lgp{L}"], done=f"lg{L}")

        def s_y(L, d):
            r, f = lp.before("yo", L)

            def y(e, t):
                for c in range(KF):
                    i = e.matmul(by[:, 0:C], d["gT"][:, c, :], sw2[:, c, :], start=(c == 0), stop=(c == KF - 1))
                return i
            lp.step("tensor", y, [f"gT{L}", *r], f, done=f"y{L}")
            lp.step("scalar", lambda e, t: e.copy(d["yo"][:], by[:, 0:C]), [f"y{L}"], frees=[f"yst{L}"],
                    done=f"yo{L}")
            lp.step("sync", lambda e, t: e.dma_start(tile_rows(ysh, t, L), d["yo"][:]), [f"yo{L}"],
                    done=f"yst{L}", dma=True)

        lp.pipeline([(0, s_in), (1, s_norm), (2, s_h1), (3, s_y), (1, s_xn), (2, s_h3), (1, s_xT), (2, s_lg)], lanes)
        lp.run(loads)


class Chain:

    def __init__(self, nc, name):
        self.nc, self.name, self.steps = nc, name, []

    def __call__(self, engine, emit):
        self.steps.append((engine, emit))

    def run(self):
        sem = self.nc.alloc_semaphore(self.name)
        with self.nc.Block() as block:
            for engine in sorted({e for e, _ in self.steps}):
                def body(eng, engine=engine):
                    for n, (on, emit) in enumerate(self.steps):
                        if on == engine:
                            eng.wait_ge(sem, n)
                            emit(eng).then_inc(sem, 1)
                {"scalar": block.scalar, "vector": block.vector, "gpsimd": block.gpsimd,
                 "tensor": block.tensor}[engine](body)
        self.nc.clear_and_free_semaphores([sem])
        self.nc.all_engine_barrier()


def route(nc, logits, weight, place, source, expert, K, T, NT, E, SLOTS):
    with memory(nc, "ro") as (sb, ps):
        m1, m2, top = sb("m1", [P, NT]), sb("m2", [P, NT]), sb("top", [P, NT])
        eq, ex = sb("eq", [P, NT, E]), sb("ex", [P, NT, E])
        pick = [sb("pick0", [P, NT, E]), sb("pick1", [P, NT, E])]
        rest, rs, dm = sb("rest", [P, NT, E]), sb("rs", [P, NT]), sb("dm", [P, NT])
        mask, inc, pos = sb("mask", [P, E, NT]), sb("inc", [P, E * NT]), sb("pos", [P, E, NT])
        tot = sb("tot", [P, E * NT])
        bi, blk, cum, first = sb("bi", [P, E], I32), sb("blk", [P, E]), sb("cum", [P, E]), sb("first", [P, E])
        cmp, se = sb("cmp", [P, SLOTS, E]), sb("se", [P, SLOTS])
        pfx, ptot = ps("pfx", [P, 512]), ps("ptot", [P, 512])
        pi, row, slot = sb("pi", [P, NT], I32), sb("row", [P, 2, NT]), sb("slot", [P, 2, NT])
        ch = Chain(nc, "route")

        def tt(out, a, b, op):
            ch("vector", lambda e: e.tensor_tensor(out, a, b, op))

        def red(out, a, op):
            ch("vector", lambda e: e.tensor_reduce(out, a, AX_X, op))

        def one_hot(src, m, out):
            red(m[:], src[:], ALU.max)
            tt(eq[:], src[:], bc(m[:], 2, E), ALU.is_equal)
            tt(eq[:], eq[:], bc(K["rank"], 1, NT), ALU.mult)
            red(top[:], eq[:], ALU.max)
            tt(out[:], eq[:], bc(top[:], 2, E), ALU.is_equal)

        one_hot(logits, m1, pick[0])
        ch("vector", lambda e: e.scalar_tensor_tensor(rest[:], pick[0][:], -3.0e38, logits[:], ALU.mult, ALU.add))
        one_hot(rest, m2, pick[1])
        tt(ex[:], logits[:], bc(m1[:], 2, E), ALU.subtract)
        ch("scalar", lambda e: e.activation(ex[:], ex[:], ACT.Exp))
        red(rs[:], ex[:], ALU.add)
        ch("vector", lambda e: e.reciprocal(weight[:, 0, :], rs[:]))
        tt(dm[:], m2[:], m1[:], ALU.subtract)
        ch("scalar", lambda e: e.activation(dm[:], dm[:], ACT.Exp))
        tt(weight[:, 1, :], dm[:], weight[:, 0, :], ALU.mult)
        tt(mask[:], pick[0][:].rearrange("p t e -> p e t"), pick[1][:].rearrange("p t e -> p e t"), ALU.add)
        flat = mask[:].rearrange("p e t -> p (e t)")
        ch("tensor", lambda e: e.matmul(pfx[:, 0:E * NT], K["before"], flat, start=True, stop=True))
        ch("tensor", lambda e: e.matmul(ptot[:, 0:E * NT], K["ones"], flat, start=True, stop=True))
        ch("vector", lambda e: e.tensor_copy(tot[:], ptot[:, 0:E * NT]))
        ch("vector", lambda e: e.tensor_tensor_scan(inc[:], K["goes_on"], tot[:], 0.0, ALU.mult, ALU.add))
        last = inc[:].rearrange("p (e t) -> p e t", e=E)[:, :, NT - 1]
        ch("vector", lambda e: e.tensor_scalar(bi[:], last, float(P - 1), None, ALU.add))
        ch("vector", lambda e: e.tensor_scalar(bi[:], bi[:], 7, None, ALU.logical_shift_right))
        ch("vector", lambda e: e.tensor_copy(blk[:], bi[:]))
        ch("vector", lambda e: e.tensor_tensor_scan(cum[:], K["one_e"], blk[:], 0.0, ALU.mult, ALU.add))
        tt(first[:], cum[:], blk[:], ALU.subtract)
        ch("vector", lambda e: e.tensor_scalar(first[:], first[:], float(P), None, ALU.mult))
        tt(inc[:], inc[:], tot[:], ALU.subtract)
        tt(inc[:], inc[:], pfx[:, 0:E * NT], ALU.add)
        tt(pos[:], inc[:].rearrange("p (e t) -> p e t", e=E), bc(first[:], 2, NT), ALU.add)
        for k in range(2):
            tt(eq[:], pick[k][:], pos[:].rearrange("p e t -> p t e"), ALU.mult)
            red(top[:], eq[:], ALU.add)
            ch("vector", lambda e, k=k: e.tensor_copy(place[:, k, :], top[:]))
            ch("vector", lambda e, k=k: e.tensor_scalar(pi[:], place[:, k, :], P - 1, None, ALU.bitwise_and))
            ch("vector", lambda e, k=k: e.tensor_copy(row[:, k, :], pi[:]))
            ch("vector", lambda e, k=k: e.tensor_scalar(pi[:], place[:, k, :], 7, None, ALU.logical_shift_right))
            ch("vector", lambda e, k=k: e.tensor_copy(slot[:, k, :], pi[:]))
        tt(cmp[:], bc(cum[:], 1, SLOTS), bc(K["slot"], 2, E), ALU.is_le)
        red(se[:], cmp[:], ALU.add)
        ch("vector", lambda e: e.tensor_scalar(expert[:], se[:], float(E - 1), None, ALU.min))
        assert T <= 4096
        Q = 4
        lp = Loop(nc, 2 * NT // Q // 2, "sr")
        lp.ahead = ("sync",)
        lanes = [{"r": sb(f"r_is{L}", [P, Q, P], F16), "eq": sb(f"slot_is{L}", [P, Q, SLOTS], F16),
                  "s": sb(f"s_is{L}", [P, Q, SLOTS], F16)} for L in LANES]
        token = sb("token", [P, Q])
        psrc = ps("src", [P, 512])

        ch("vector", lambda e: e.tensor_copy(token[:], K["token"][:, 0:Q]))
        ch("vector", lambda e: e.memset(lanes[0]["r"][:], 0.0))
        ch("tensor", lambda e: e.matmul(psrc[:, 0:SLOTS], lanes[0]["r"][:, 0], lanes[0]["r"][:, 0, 0:SLOTS],
                                        start=True, stop=False, skip_group_check=True))
        for n, (engine, emit) in enumerate(ch.steps):
            lp.open(engine, emit, after=n)

        def s_hot(L, d):
            def at(a, t):
                return a[:, L, bass.ds(t * Q, Q)]
            lp.step("vector", lambda e, t: e.tensor_tensor(d["eq"][:], bc(K["slot"], 1, Q), bc(at(slot, t), 2, SLOTS),
                                                           ALU.is_equal), frees=[f"hot{L}"], done=f"eq{L}")
            lp.step("gpsimd", lambda e, t: e.tensor_tensor(d["s"][:], d["eq"][:], bc(token[:], 2, SLOTS), ALU.mult),
                    [f"eq{L}"], frees=[f"mm{L}"], last=["token"], done=f"hot{L}")
            if L:
                lp.step("gpsimd", lambda e, t: e.tensor_scalar(token[:], token[:], float(Q * P), None, ALU.add),
                        ["hot1"], done="token", apart=True)
            lp.step("vector", lambda e, t: e.tensor_tensor(d["r"][:], bc(K["row"], 1, Q), bc(at(row, t), 2, P),
                                                           ALU.is_equal), frees=[f"mm{L}"], done=f"rows{L}")

            def mm(e, t):
                for q in range(Q):
                    i = e.matmul(psrc[:, 0:SLOTS], d["r"][:, q], d["s"][:, q], start=False, stop=False,
                                 skip_group_check=True)
                return i
            lp.step("tensor", mm, [f"hot{L}", f"rows{L}"], done=f"mm{L}", apart=True)

        lp.pipeline([(0, s_hot)], lanes)
        lp.run()
        ch = Chain(nc, "source")
        ch("vector", lambda e: e.tensor_scalar(source[:], psrc[:, 0:SLOTS], float(T // 2), None, ALU.add))
        ch.run()


def experts(nc, xn1, yg, w13, w2, source, expert, K, C, KC, E, SLOTS, F):
    KF = -(-F // P)
    FR = F - (KF - 1) * P
    H = F // 2
    with memory(nc, "ex") as (sb, ps):
        lp = Loop(nc, SLOTS // 2, "ex")
        hb = [ps(f"hb{i}", [P, 512]) for i in range(4)]
        tb, xb, yb = [ps("tb0", [P, 512]), ps("tb1", [P, 512])], ps("xb", [P, 512]), ps("yb", [P, 512])
        lanes = [{n: sb(f"{n}{L}", s, I32 if n == "idx" else F32) for n, s in (
            ("xa", [P, C]), ("xT", [P, KC, P]), ("g", [P, F]), ("gT", [P, KF, P]), ("yo", [P, C]),
            ("idx", [P, 1]))} for L in LANES]

        def s_in(L, d):
            lp.step("gpsimd", lambda e, t: e.tensor_copy(d["idx"][:], source[:, bass.ds(2 * t + L, 1)]),
                    frees=[f"xTp{L}"], done=f"idx{L}", apart=True)
            lp.step("gpsimd", lambda e, t: e.indirect_dma_start(
                d["xa"][:], None, xn1, bass.IndirectOffsetOnAxis(ap=d["idx"][:, 0:1], axis=0)),
                [f"idx{L}"], done=f"xa{L}", dma=True, apart=True)

        def s_xT(L, d):
            r, f = lp.before("xT", L)
            transposes(lp, L, "xT", d["xa"], xb, d["xT"][:], K["ident"], [f"xa{L}", *r], frees=f,
                       keeps=[f"h1{L}"])

        def s_expert(L, d):
            d["register"] = x = {}

            def load(e, t):
                x[0] = e.value_load(expert[0:1, bass.ds(2 * t + L, 1)], min_val=0, max_val=E - 1)
            lp.step("tensor", load)

        def s_h(L, d):
            x = d["register"]

            def up(half, part):
                def f(e, t):
                    for k in range(KC):
                        i = e.matmul(hb[2 * half + part][:, 0:H], d["xT"][:, k, :],
                                     w13[:, bass.ds(2 * x[0] + part, 1), k, half * H:(half + 1) * H],
                                     start=(k == 0), stop=(k == KC - 1))
                    return i
                return f
            for half in range(2):
                r, f = lp.before(f"g{half}", L)
                lp.step("tensor", up(half, 0), [f"xT{L}", *r], f)
                lp.step("tensor", up(half, 1), done=f"h{half}{L}")
                g = d["g"][:, half * H:(half + 1) * H]
                lp.step("scalar", lambda e, t, g=g, half=half: e.activation(g, hb[2 * half][:, 0:H], ACT.Silu),
                        [f"h{half}{L}"], frees=[f"gTp{L}"], done=f"si{half}{L}")
                lp.step("vector", lambda e, t, g=g, half=half: e.tensor_tensor(g, g, hb[2 * half + 1][:, 0:H],
                                                                               ALU.mult),
                        [f"si{half}{L}"], done=f"g{half}{L}")

        def s_gT(L, d):
            ra, fa = lp.before("ta", L)
            rc, fc = lp.before("tc", L)

            def tr(e, t):
                for k in range(KF):
                    n = P if k < KF - 1 else FR
                    i = e.transpose(tb[k // 4][0:n, (k % 4) * P:(k % 4 + 1) * P], d["g"][:, k * P:k * P + n],
                                    K["ident"])
                return i
            lp.step("tensor", tr, [f"g1{L}", *ra, *rc], [*fa, *fc], done=f"gTp{L}")
            lp.step("scalar", lambda e, t: e.copy(d["gT"][:, 0:4], chunks(tb[0][:], 4)), [f"gTp{L}"],
                    frees=[f"y{L}"], done=f"ta{L}")

            def rest(e, t):
                e.tensor_copy(d["gT"][:, 4, :], tb[1][:, 0:P])
                return e.tensor_copy(d["gT"][0:FR, 5, :], tb[1][0:FR, P:2 * P])
            lp.step("vector", rest, [f"gTp{L}"], frees=[f"y{L}"], done=f"tc{L}")

        def s_y(L, d):
            r, f = lp.before("yo", L)

            def y(e, t):
                x = e.value_load(expert[0:1, bass.ds(2 * t + L, 1)], min_val=0, max_val=E - 1)
                for k in range(KF):
                    n = P if k < KF - 1 else FR
                    i = e.matmul(yb[:, 0:C], d["gT"][0:n, k, :], w2[0:n, bass.ds(KF * x + k, 1), :],
                                 start=(k == 0), stop=(k == KF - 1))
                return i
            lp.step("tensor", y, [f"ta{L}", f"tc{L}", *r], f, done=f"y{L}", apart=True)
            lp.step("scalar", lambda e, t: e.copy(d["yo"][:], yb[:, 0:C]), [f"y{L}"], frees=[f"yst{L}"],
                    done=f"yo{L}")
            lp.step("sync", lambda e, t: e.dma_start(tile_rows(yg, t, L), d["yo"][:]), [f"yo{L}"],
                    done=f"yst{L}", dma=True)

        lp.pipeline([(0, s_in), (2, s_expert), (1, s_xT), (3, s_gT), (2, s_h), (3, s_y)], lanes)
        lp.run()


TWO_PI = 2 * np.pi
TURN_HI = 6.28125
TURN_MID = float(np.float32(round((TWO_PI - TURN_HI) * 2 ** 21) / 2 ** 21))
TURN_LO = float(TWO_PI - TURN_HI - TURN_MID)
TO_INT = 1.5 * 2 ** 23
PI_BELOW = float(np.nextafter(np.float32(np.pi), np.float32(0)))


def attention_weights(sb, A, C, KC):
    W = {n: sb(f"la_{n}", s) for n, s in (
        ("wqk", [P, KC, 2 * C]), ("wv", [P, KC, C]), ("wo", [P, KC, C]),
        ("g1", [P, KC, P]), ("g2", [P, C]),
        ("gamma", [P, C]), ("beta", [P, C]), ("theta", [P, C]))}
    return W, ([(W[n][:], kcn(A[a])) for n, a in (("wqk", "Wqk"), ("wv", "Wv"), ("wo", "Wo"), ("g1", "G1"))]
               + [(W["g2"][:], A["G2"])]
               + [(W[n][:], A[n].partition_broadcast(P)) for n in ("gamma", "beta", "theta")])


def linear_attention(nc, A, W, x1, ysh, yg, weight, place, x2, x3, xn3T, K, T, C, KC, loads,
                     later_pairs):
    S = T // 2
    CH = 4
    HD = C // HEADS
    ident = K["ident"]
    with memory(nc, "la") as (sb, ps):
        wqk, wv, wo, g1, g2, gamma, beta, theta = (W[n] for n in (
            "wqk", "wv", "wo", "g1", "g2", "gamma", "beta", "theta"))
        pos, ang = sb("pos", [P, 1]), sb("ang", [P, C])
        trn, red, cs = (sb(n, [P, 2, C]) for n in ("trn", "red", "cs"))
        lanes = []
        for L in LANES:
            d = {n: sb(f"{n}{L}", s) for n, s in (
                ("xa", [P, C]), ("ys", [P, C]), ("a0", [P, C]), ("a1", [P, C]), ("ym", [P, C]), ("zm", [P, C]),
                ("x2", [P, C]), ("xb", [P, C]), ("xn", [P, C]), ("xnT", [P, KC, P]), ("t1", [P, P]),
                ("gt", [P, C]), ("qks", [P, 2, C]), ("qr", [P, 2 * C]), ("kr", [P, 2 * C]), ("qT", [P, CH, P]),
                ("kT", [P, CH, P]),
                ("qM", [P, CH, 4, P]), ("v", [P, HEADS, 2 * HD]), ("state", [P, CH, 64]),
                ("em", [P, CH, 4, P]), ("up", [P, CH, 64]), ("oT", [P, KC, P]), ("y", [P, C]), ("yn", [P, C]),
                ("yb", [P, C]), ("zn", [P, C]), ("xo", [P, C]), ("w", [P, C]), ("wT", [P, KC, P]))}
            d["idx"] = sb(f"idx{L}", [P, 2], I32)
            for n in ("0", "x", "1", "2", "3"):
                d[f"ln{n}"] = LayerNorm(sb, f"ln{n}_{L}", K["half"])
            lanes.append(d)
        bE = ps("E", [P, CH, 512])
        bA, bB, bX, bO = ps("A", [P, 512]), ps("B", [P, 512]), ps("X", [P, 512]), ps("O", [P, 512])
        lp = Loop(nc, S // P, "la")
        lp.open("vector", lambda e: e.tensor_scalar(pos[:], K["token"][:, 0:1], float(T // 2), None, ALU.add))
        for d, engine in zip(lanes, ("vector", "gpsimd")):
            for n in ("state", "v", "qM"):
                lp.open(engine, lambda e, d=d, n=n: e.memset(d[n][:], 0.0))
        later = Loads(nc, "l_later", later_pairs, (lp, 1))

        def rows(dr, t, L):
            return dr[bass.ds(t * P + L * S, P), :]

        def less(part, src, before, done, last=()):
            lp.step("vector", lambda e, t: e.scalar_tensor_tensor(red[:], trn[:], -part, src, ALU.mult, ALU.add),
                    [before], last=last, done=done)

        def s_turns(L, d):
            if not L:
                return
            lp.lag = 0

            lp.step("scalar", lambda e, t: e.activation(ang[:], theta[:], ACT.Copy, scale=pos[:]), last=["pos"],
                    frees=["hi"], done="ang")
            lp.step("vector", lambda e, t: e.tensor_scalar(pos[:], pos[:], float(P), None, ALU.add), ["ang"],
                    done="pos")

            def turns(e, t):
                for x, quarter in enumerate((0.25, 0.0)):
                    i = e.activation(trn[:, x], ang[:], ACT.Copy, scale=float(1 / TWO_PI), bias=quarter)
                return i
            lp.step("scalar", turns, ["ang"], frees=["lo"], done="trn_q")
            lp.step("vector", lambda e, t: e.tensor_scalar(trn[:], trn[:], TO_INT, TO_INT, ALU.add, ALU.subtract),
                    ["trn_q"], done="trn")
            less(TURN_HI, bc(ang[:], 1, 2), "trn", "hi", last=["cs"])

        def s_reduce(L, d):
            if L:
                return
            lp.lag = 1
            less(TURN_MID, red[:], "hi", "mid")
            less(TURN_LO, red[:], "mid", "lo")
            lp.step("vector", lambda e, t: e.tensor_scalar(red[:, 0], red[:, 0], float(np.pi / 2), None, ALU.add),
                    ["lo"], done="ahead")
            lp.step("vector", lambda e, t: e.tensor_scalar(red[:], red[:], PI_BELOW, -PI_BELOW, ALU.min, ALU.max),
                    ["ahead"], done="red")

        def s_sin(L, d):
            if not L:
                return
            lp.lag = 1
            lp.step("scalar", lambda e, t: e.activation(cs[:], red[:], ACT.Sin), ["red"], frees=["kr0", "kr1"],
                    done="cs")

        def s_in(L, d):
            lp.step("sync", lambda e, t: e.dma_start(d["xa"][:], rows(x1, t, L)), frees=[f"x2{L}"],
                    done=f"xa{L}", dma=True)
            lp.step("sync", lambda e, t: e.dma_start(d["ys"][:], rows(ysh, t, L)), frees=[f"y0{L}"],
                    done=f"ys{L}", dma=True)
            lp.step("gpsimd", lambda e, t: e.tensor_copy(
                d["idx"][:].unsqueeze(2), place[:, :, bass.ds(t + L * (S // P), 1)]), frees=[f"y1{L}"],
                done=f"idx{L}", apart=True)
            for k in range(2):
                lp.step("gpsimd", lambda e, t, k=k: e.indirect_dma_start(
                    d[f"a{k}"][:], None, yg, bass.IndirectOffsetOnAxis(ap=d["idx"][:, k:k + 1], axis=0)),
                    [f"idx{L}"], done=f"a{k}{L}", dma=True, apart=True)

        def s_mix(L, d):
            src = d["ys"]
            for k in range(2):
                def mix(e, t, k=k, src=src):
                    return e.scalar_tensor_tensor(d["ym"][:], d[f"a{k}"][:],
                                                  weight[:, k, bass.ds(t + L * (S // P), 1)], src[:],
                                                  ALU.mult, ALU.add)
                lp.step("vector", mix, [f"a{k}{L}", f"ys{L}" if k == 0 else f"y0{L}"],
                        frees=[f"ln_0{L}"], done=f"y{k}{L}")
                src = d["ym"]
            d["ln0"].stats(lp, f"0{L}", d["ym"][:], [f"y1{L}"])

        def s_x2(L, d):
            d["ln0"].apply(lp, f"0{L}", d["ym"][:], d["zm"][:], frees=[f"x2{L}"])
            lp.step("gpsimd", lambda e, t: e.tensor_tensor(d["x2"][:], d["zm"][:], d["xa"][:], ALU.add),
                    [f"ln_0{L}", f"xa{L}"], frees=[f"x2st{L}", f"ln_x{L}"], done=f"x2{L}")
            lp.step("sync", lambda e, t: e.dma_start(rows(x2, t, L), d["x2"][:]), [f"x2{L}"], done=f"x2st{L}",
                    dma=True)

        def s_norm(L, d):
            d["lnx"].stats(lp, f"x{L}", d["x2"][:], [f"x2{L}"])

        def s_xn(L, d):
            d["lnx"].apply(lp, f"x{L}", d["x2"][:], d["xn"][:], frees=[f"xnTp{L}"])

        def s_xT(L, d):
            transposes(lp, L, "xnT", d["xn"], bX, d["xnT"][:], ident, [f"ln_x{L}"], keeps=[f"qkp{L}"],
                       last=[f"wT{L}", f"xnT{1 - L}"])

        def s_t1(L, d):
            def t1(e, t):
                for k in range(KC):
                    i = e.matmul(bO[:, C:C + P], g1[:, k, :], d["xnT"][:, k, :], start=(k == 0),
                                 stop=(k == KC - 1))
                return i
            lp.step("tensor", t1, [f"xnT{L}"], last=[f"oT{L}", f"t1{1 - L}"], done=f"t1p{L}")
            lp.step("scalar", lambda e, t: e.copy(d["t1"][:], bO[:, C:C + P]), [f"t1p{L}"], frees=[f"g2{L}"],
                    done=f"t1{L}")

        def s_gate(L, d):
            lp.step("tensor", lambda e, t: e.matmul(bA[:, 0:C], d["t1"][:], g2[:], start=True, stop=True),
                    [f"t1{L}"], last=[f"up{1 - L}", f"th{1 - L}"], done=f"g2{L}")
            lp.step("scalar", lambda e, t: e.activation(d["gt"][:], bA[:, 0:C], ACT.Tanh, scale=0.5),
                    [f"g2{L}"], frees=[f"y{L}"], done=f"th{L}")
            lp.step("scalar", lambda e, t: e.activation(d["gt"][:], d["gt"][:], ACT.Copy, scale=0.5, bias=0.5),
                    [f"th{L}"], done=f"gt{L}")

        def s_v(L, d):
            def v(e, t):
                for k in range(KC):
                    i = e.matmul(bB[:, 0:C], d["xnT"][:, k, :], wv[:, k, :], start=(k == 0), stop=(k == KC - 1))
                return i
            lp.step("tensor", v, [f"xnT{L}"], last=[f"y{1 - L}", f"v{1 - L}"], done=f"vp{L}")

            def cp(e, t):
                pair = d["v"][:].rearrange("p (b h) d -> p b (h d)", h=2)
                src = bB[:, 0:C].rearrange("p (b h d) -> p b h d", h=2, d=HD)
                for h in range(2):
                    i = e.copy(pair[:, :, 3 * HD * h:3 * HD * h + HD], src[:, :, h])
                return i
            lp.step("scalar", cp, [f"vp{L}"], frees=[f"O{L}", f"ust{L}"], done=f"v{L}")

        def s_qk(L, d):
            def f(e, t):
                for k in range(KC):
                    i = e.matmul(bE[:, 2], d["xnT"][:, k, :], wqk[:, k, :], start=(k == 0), stop=(k == KC - 1))
                return i
            lp.step("tensor", f, [f"xnT{L}"], last=[f"em2{1 - L}", f"qks{1 - L}"], done=f"qkp{L}")
            lp.step("scalar", lambda e, t: e.activation(d["qks"][:], chunks(bE[:, 2], 2), ACT.Silu), [f"qkp{L}"],
                    frees=[f"kr{L}"], done=f"qks{L}")
            cos_sin = cs[:].rearrange("p x (h d) -> p h x d", h=HEADS)
            for i, (n, frees) in enumerate((("qr", [f"turn_q{L}"]), ("kr", [f"turn_k{L}", f"ust{L}"]))):
                lp.step("gpsimd", lambda e, t, i=i, n=n: e.tensor_tensor(
                    d[n][:].rearrange("p (h x d) -> p h x d", h=HEADS, x=2),
                    bc(d["qks"][:, i].rearrange("p (h d) -> p h d", h=HEADS), 2, 2), cos_sin, ALU.mult),
                    [f"qks{L}", "cs"], frees=frees, done=f"{n}{L}")

        def s_turn(L, d):
            def tr(src, bank):
                def f(e, t):
                    for c in range(CH):
                        i = e.transpose(bank[:, c * P:(c + 1) * P], src[:, c * P:(c + 1) * P], ident)
                    return i
                return f

            def own(e, t):
                for r in range(4):
                    i = e.copy(d["qM"][32 * r:32 * r + 32, :, r, :], chunks(bE[32 * r:32 * r + 32, 2], CH))
                return i
            lp.step("tensor", tr(d["qr"], bE[:, 2]), [f"qr{L}"], done=f"turn_q{L}")
            lp.step("tensor", tr(d["kr"], bE[:, 3]), [f"kr{L}"], last=[f"em3{1 - L}"], done=f"turn_k{L}")
            lp.step("scalar", own, [f"turn_q{L}"], frees=[f"en3{L}"], done=f"qM{L}")
            lp.step("vector", lambda e, t: e.tensor_copy(d["kT"][:], chunks(bE[:, 3], CH)), [f"turn_k{L}"],
                    frees=[f"en3{L}"], done=f"kT{L}")
            lp.step("scalar", lambda e, t: e.copy(d["qT"][:], chunks(bE[:, 2], CH)), frees=[f"O{L}"], done=f"qT{L}")

        def s_energy(L, d):
            for c in range(CH):
                lp.step("tensor", lambda e, t, c=c: e.matmul(
                    bE[:, c, :], d["kT"][:, c, :], d["qM"][:, c].rearrange("p r n -> p (r n)"), start=True, stop=True),
                    [f"kT{L}", f"qM{L}"] + ([f"qT{L}"] if c == 2 else []), last=[f"em{c}{1 - L}"], done=f"en{c}{L}")
        def s_mask(L, d):
            for c in range(CH):
                lp.step("vector", lambda e, t, c=c: e.tensor_tensor(
                    d["em"][:, c], chunks(bE[:, c], 4), bc(K["causal"], 1, 4), ALU.mult),
                    [f"en{c}{L}"], frees=[f"O{L}"], done=f"em{c}{L}")

        def s_state(L, d):
            def u(e, t):
                pair = d["v"][:].rearrange("p (b h) (x d) -> p b (h x) d", h=2, d=HD)
                for c in range(CH):
                    i = e.matmul(bA[:, c * P:(c + 1) * P], d["kr"][:, c * P:(c + 1) * P], pair[:, 4 * (c // 2):4 * (c // 2) + 4, ::3],
                                 start=True, stop=True)
                return i
            lp.step("tensor", u, [f"kr{L}", f"v{L}"], last=[f"th{L}", f"up{1 - L}"], done=f"ust{L}")
            own = bA[:].rearrange("p (b x n) -> p b x n", b=2, n=64)[:, :, ::3]
            mask = K["own_head"].unsqueeze(1).unsqueeze(1).broadcast_to([P, 2, 2, 64])
            lp.step("vector", lambda e, t: e.tensor_tensor(d["up"][:].rearrange("p (b x) n -> p b x n", b=2), own,
                                                           mask, ALU.mult), [f"ust{L}"], done=f"up{L}")

        def s_keep(L, d):
            lp.step("vector", lambda e, t: e.tensor_tensor(d["state"][:], d["state"][:], d["up"][:], ALU.add),
                    [f"up{L}", f"O{L}"], done=f"st{L}")

        def s_attend(L, d):
            def o(e, t):
                for c in range(CH):
                    i = e.matmul(bO[64 * (c % 2):64 * (c % 2) + 64, (c // 2) * P:(c // 2 + 1) * P],
                                 d["state"][:, c, :], d["qT"][:, c, :], start=(c < 2), stop=False,
                                 skip_group_check=True)
                for h in range(HEADS):
                    g = h // 2 % 4
                    i = e.matmul(bO[32 * g:32 * g + 32, (h // 8) * P:(h // 8 + 1) * P], d["v"][:, h, :],
                                 d["em"][:, h // 4, h % 4, :], start=False, stop=(h >= HEADS - 8),
                                 skip_group_check=True)
                return i
            lp.step("tensor", o, [*(f"em{c}{L}" for c in range(CH)), f"v{L}", f"qT{L}"], frees=[f"st{L}"],
                    last=[f"t1{1 - L}", f"oT{1 - L}"], done=f"O{L}", apart=True)
            lp.step("scalar", lambda e, t: e.copy(d["oT"][:], chunks(bO[:, 0:C], KC)), [f"O{L}"],
                    frees=[f"z{L}"], done=f"oT{L}")

        def s_z(L, d):
            def z(e, t):
                for k in range(KC):
                    i = e.matmul(bB[:, C:2 * C], d["oT"][:, k, :], wo[:, k, :], start=(k == 0), stop=(k == KC - 1))
                return i
            lp.step("tensor", z, [f"oT{L}"], last=[f"v{L}", f"y{1 - L}"], done=f"z{L}")
            lp.step("vector", lambda e, t: e.tensor_tensor(d["y"][:], bB[:, C:2 * C], d["gt"][:], ALU.mult),
                    [f"z{L}", f"gt{L}"], done=f"y{L}")
            d["ln1"].stats(lp, f"1{L}", d["y"][:], [f"y{L}"])
            lp.step("sync", lambda e, t: e.dma_start(d["xb"][:], rows(x2, t, L)), [f"x2st{L}"], frees=[f"xo{L}"],
                    done=f"xb{L}", dma=True)

        def s_affine(L, d):
            ln = d["ln1"]
            lp.step("vector", lambda e, t: e.scalar_tensor_tensor(d["yn"][:], d["y"][:], ln.mv[:, 0:1], gamma[:],
                                                                  ALU.subtract, ALU.mult), done=f"ga{L}")
            lp.step("vector", lambda e, t: e.scalar_tensor_tensor(d["yb"][:], d["yn"][:], ln.rstd[:], beta[:],
                                                                  ALU.mult, ALU.add),
                    [f"rs_1{L}", f"ga{L}"], done=f"ln_1{L}")

        def s_norm2(L, d):
            d["ln2"].stats(lp, f"2{L}", d["yb"][:], [f"ln_1{L}"])

        def s_x3(L, d):
            d["ln2"].apply(lp, f"2{L}", d["yb"][:], d["zn"][:], frees=[f"xo{L}"])
            lp.step("gpsimd", lambda e, t: e.tensor_tensor(d["xo"][:], d["zn"][:], d["xb"][:], ALU.add),
                    [f"ln_2{L}", f"xb{L}"], frees=[f"out{L}", f"ln_3{L}"], done=f"xo{L}")
            lp.step("sync", lambda e, t: e.dma_start(rows(x3, t, L), d["xo"][:]), [f"xo{L}"], done=f"out{L}",
                    dma=True)

        def s_norm3(L, d):
            d["ln3"].stats(lp, f"3{L}", d["xo"][:], [f"xo{L}"])

        def s_w(L, d):
            d["ln3"].apply(lp, f"3{L}", d["xo"][:], d["w"][:], frees=[f"wTp{L}"])

        def s_wT(L, d):
            transposes(lp, L, "wT", d["w"], bX[:, C:2 * C], d["wT"][:], ident, [f"ln_3{L}"], keeps=[f"wst{L}"],
                       last=[f"xnT{1 - L}", f"wT{1 - L}"])
            lp.step("sync", lambda e, t: e.dma_start(
                xn3T.rearrange("(k p) n -> p k n", p=P)[:, :, bass.ds(t * P + L * S, P)], d["wT"][:]), [f"wT{L}"],
                done=f"wst{L}", dma=True)

        lp.pipeline([(0, s_in), (3, s_v), (3, s_t1), (4, s_turn), (4, s_state), (6, s_norm2), (5, s_z), (8, s_wT),
                     (2, s_x2), (4, s_energy), (4, s_mask), (2, s_norm), (7, s_norm3),
                     (3, s_gate), (2, s_xn), (0, s_sin), (3, s_qk), (4, s_attend), (2, s_xT),
                     (5, s_affine), (6, s_x3), (7, s_w), (1, s_mix), (4, s_keep), (0, s_turns), (0, s_reduce)],
                    lanes)
        lp.run(loads)
        return later


def recurrence_weights(sb, A, C, KC):
    names = ("wf", "wi", "wc", "wo", "uf", "ui", "uc", "uo")
    W = {n: sb(n, [P, KC, C]) for n in names}
    W |= {"bias": sb("bias", [P, 3, KC]), "c_start": sb("c_start", [P, KC]), "bo": sb("bo_row", [P, C])}
    return W, ([(W[n][:], kcn(A[n])) for n in names]
               + [(W["bias"][:, g, :], A[n]) for g, n in enumerate(("bf", "bi", "bc"))]
               + [(W["c_start"][:], A["in_c"]), (W["bo"][:], A["bo"].partition_broadcast(P))])


def gated_recurrence(nc, A, w, x3, xn3T, K, T, C, KC, loads):
    S = T // 2
    R = 256
    G = ("f", "i", "c")
    out = A["out"]
    b, c0, bo = w["bias"], w["c_start"], w["bo"]
    with memory(nc, "gr") as (sb, ps):
        b0 = sb("b_first", [P, 3, KC])
        gb = [[ps(f"g{s}{g}", [P, 512]) for g in range(3)] for s in range(2)]
        ob = [ps(f"o{s}", [P, 512]) for s in range(2)]
        lp = Loop(nc, S // (2 * R), "gr")

        def uc0(e):
            for g, n in enumerate(G):
                for m in range(KC):
                    for k in range(KC):
                        i = e.matmul(ob[0][:, g * KC + m:g * KC + m + 1], w["u" + n][:, k, m * P:(m + 1) * P],
                                     c0[:, k:k + 1], start=(k == 0), stop=(k == KC - 1))
            return i
        lp.open("tensor", uc0)
        lp.open("vector", lambda e: e.tensor_tensor(b0[:], ob[0][:, 0:3 * KC].rearrange("p (g k) -> p g k", g=3), b[:],
                                                    ALU.add), after=1)
        lanes = [{n: sb(f"{n}{L}", s) for n, s in (
            ("x0", [P, KC, R]), ("x1", [P, KC, R]), ("y0", [P, KC, R]), ("y1", [P, KC, R]),
            ("f", [P, KC, R]), ("i", [P, KC, R]), ("c", [P, KC, R]),
            ("ig", [P, KC, R]), ("fc", [P, KC, R]), ("c1", [P, KC, R]), ("c2", [P, KC, R]),
            ("h0", [P, 2, C]), ("h1", [P, 2, C]), ("r0", [P, 2, C]), ("r1", [P, 2, C]),
            *((f"{n}_{s}_", z) for s in range(2) for n, z in (
                ("st", [P, 2, 6]), ("mv", [P, 2, 2]), ("ve", [P, 2]), ("rs", [P, 2]))))} for L in LANES]

        def cols(s, t, L):
            return xn3T.rearrange("(k p) n -> p k n", p=P)[:, :, bass.ds(t * 2 * R + L * R + s * S, R)]

        def tok(dr, s, t, L):
            return dr[bass.ds(t * 2 * R + L * R + s * S, R), :].rearrange("(q p) c -> p q c", p=P)

        def s_load(name, s, used):
            def stage(L, d):
                lp.step("sync", lambda e, t: e.dma_start(d[f"{name}{s}"][:], cols(s, t, L)), frees=[f"{used}{L}"],
                        done=f"{name}{s}{L}", dma=True)
            return stage

        def s_rows(s):
            def stage(L, d):
                lp.step("sync", lambda e, t: e.dma_start(d[f"r{s}"][:], tok(x3, s, t, L)), frees=[f"xo{s}{L}"],
                        done=f"r{s}{L}", dma=True)
            return stage

        def s_gates(s):
            def stage(L, d):
                for g, n in enumerate(G):
                    bank = gb[s][g]

                    def wx(e, t, n=n, bank=bank):
                        for m in range(KC):
                            o = bank[:, m * R:(m + 1) * R]
                            for k in range(KC):
                                i = e.matmul(o, w["w" + n][:, k, m * P:(m + 1) * P], d[f"x{s}"][:, k, :],
                                             start=(k == 0), stop=(s == 0 and k == KC - 1))
                            if s:
                                for k in range(KC):
                                    i = e.matmul(o, w["u" + n][:, k, m * P:(m + 1) * P], d["c1"][:, k, :],
                                                 start=False, stop=(k == KC - 1))
                        return i
                    lp.step("tensor", wx, [f"x{s}{L}"] + ([f"c1{L}"] if s else []), last=[f"n{n}{s}{1 - L}"],
                            done=f"g{n}{s}{L}")

                    def act(e, t, n=n, bank=bank, g=g):
                        for m in range(KC):
                            i = e.activation(d[n][:, m], bank[:, m * R:(m + 1) * R],
                                             ACT.Tanh if n == "c" else ACT.Sigmoid,
                                             bias=(b if s else b0)[:, g, m:m + 1])
                        return i
                    lp.step("scalar", act, [f"g{n}{s}{L}"] + ([f"c1{L}"] if s else []),
                            frees=[] if s else [f"c2{L}"], done=f"n{n}{s}{L}")
                lp.step("vector", lambda e, t: e.tensor_tensor(d["ig"][:], d["i"][:], d["c"][:], ALU.mult),
                        [f"nc{s}{L}"], done=f"ig{s}{L}")
                if s == 0:
                    def c1(e, t):
                        for m in range(KC):
                            i = e.scalar_tensor_tensor(d["c1"][:, m], d["f"][:, m], c0[:, m:m + 1], d["ig"][:, m],
                                                       ALU.mult, ALU.add)
                        return i
                    lp.step("vector", c1, [f"ig0{L}"], frees=[f"gc1{L}"], done=f"c1{L}")
                else:
                    lp.step("vector", lambda e, t: e.tensor_tensor(d["fc"][:], d["f"][:], d["c1"][:], ALU.mult),
                            done=f"fc{L}")
                    lp.step("vector", lambda e, t: e.tensor_tensor(d["c2"][:], d["fc"][:], d["ig"][:], ALU.add),
                            [f"fc{L}", f"ig1{L}"], frees=[f"o1{L}"], done=f"c2{L}")
            return stage

        def s_out(s):
            def stage(L, d):
                h = d[f"h{s}"]
                st, mv, ve, rs = (d[f"{n}_{s}_"] for n in ("st", "mv", "ve", "rs"))

                def o(e, t):
                    for q in range(2):
                        for m, (a, wt) in enumerate(((d[f"y{s}"], w["wo"]), (d["c2"], w["uo"]))):
                            for k in range(KC):
                                i = e.matmul(ob[s][:, q * C:(q + 1) * C], a[:, k, q * P:(q + 1) * P], wt[:, k, :],
                                             start=(m == 0 and k == 0), stop=(m == 1 and k == KC - 1))
                    return i
                lp.step("tensor", o, [f"c2{L}", f"y{s}{L}"], last=[f"hb{s}{1 - L}"], done=f"o{s}{L}")
                lp.step("vector", lambda e, t: e.tensor_tensor(h[:], chunks(ob[s][:], 2), bc(bo[:], 1, 2), ALU.add),
                        [f"o{s}{L}"], frees=[f"out{s}{L}"], done=f"hb{s}{L}")
                lp.step("scalar", lambda e, t: e.activation(h[:], h[:], ACT.Tanh), [f"hb{s}{L}"], done=f"h{s}{L}")

                def each(fn):
                    def f(e, t):
                        for q in range(2):
                            i = fn(e, q)
                        return i
                    return f
                lp.step("vector", each(lambda e, q: e.bn_stats(st[:, q], h[:, q])), [f"h{s}{L}"], done=f"st{s}{L}")
                lp.step("vector", each(lambda e, q: e.bn_aggr(mv[:, q], st[:, q])), [f"st{s}{L}"],
                        done=f"mv{s}{L}", apart=True)
                lp.step("gpsimd", lambda e, t: e.tensor_scalar(ve[:], mv[:, :, 1], LN_EPS, None, ALU.add),
                        [f"mv{s}{L}"], done=f"ve{s}{L}", apart=True)
                lp.step("gpsimd", lambda e, t: e.tensor_tensor(rs[:], ve[:], K["half"].broadcast_to([P, 2]), ALU.pow),
                        [f"ve{s}{L}"], done=f"rs{s}{L}")
                lp.step("vector", each(lambda e, q: e.tensor_scalar(h[:, q], h[:, q], mv[:, q, 0:1], rs[:, q:q + 1],
                                                                    ALU.subtract, ALU.mult)),
                        [f"rs{s}{L}"], done=f"ln{s}{L}")
                lp.step("gpsimd", lambda e, t: e.tensor_tensor(h[:], h[:], d[f"r{s}"][:], ALU.add),
                        [f"ln{s}{L}", f"r{s}{L}"], done=f"xo{s}{L}")
                lp.step("sync", lambda e, t: e.dma_start(tok(out, s, t, L), h[:]), [f"xo{s}{L}"],
                        done=f"out{s}{L}", dma=True)
            return stage

        lp.pipeline([(0, s_load("x", 0, "gc0")), (1, s_load("x", 1, "gc1")), (2, s_load("y", 0, "o0")),
                     (2, s_load("y", 1, "o1")), (2, s_rows(0)), (2, s_rows(1)), (2, s_gates(1)), (3, s_out(0)),
                     (1, s_gates(0)), (3, s_out(1))], lanes)
        lp.run(loads)



def inputs(given):
    def g(name):
        return np.asarray(given[name])

    def t(name):
        return np.ascontiguousarray(g(name).T)

    def padded(a, shape):
        out = np.zeros(shape, a.dtype)
        out[:a.shape[0], :a.shape[1]] = a
        return out
    ffn, att, rec = "L0_ffn_", "L1_attn_", "L1_ffn_"
    d = {"x": np.ascontiguousarray(g("L0_attn_x").reshape(-1, 256)), "w_attnT": t("L0_attn_w_attn"),
         "w_projT": t("L0_attn_w_proj"), "gateT": padded(t(ffn + "gate_w"), (256, 96)),
         "G1": padded(g(att + "G1"), (256, P)), "G2": padded(g(att + "G2"), (P, 256))}
    d |= {n: g(ffn + n) for n in ("sw1", "sw2", "sw3")}
    d["w13"] = np.stack([g(ffn + "w1"), g(ffn + "w3")], 1).reshape(-1, g(ffn + "w1").shape[-1])
    d["w2"] = np.concatenate([padded(a, (-(-a.shape[0] // P) * P, 256)) for a in g(ffn + "w2")])
    d |= {n: g(att + n) for n in ("Wv", "Wo", "gamma", "beta")}
    d |= {"Wqk": np.concatenate([g(att + "Wq"), g(att + "Wk")], 1), "theta": g(att + "theta").reshape(-1)}
    d |= {n: t(rec + n) for n in ("wf", "wi", "wc", "wo", "uf", "ui", "uc", "uo")}
    d |= {n: np.ascontiguousarray(g(rec + n).reshape(-1, P).T) for n in ("bf", "bi", "bc", "in_c")}
    d["bo"] = g(rec + "bo")
    d["consts"] = np.concatenate([np.asarray(v, np.float32) for v in const_layout().values()], 1)
    return d


def kernel(**given):
    import concourse.bacc as bacc
    from concourse.bass_utils import run_bass_kernel_spmd

    nc = bacc.Bacc("TRN2", target_bir_lowering=False, num_devices=1)
    arrays, A = {}, {}
    for name, a in inputs(given).items():
        arrays[f"in_{name}"] = a
        A[name] = nc.dram_tensor(f"in_{name}", a.shape, mybir.dt.from_np(a.dtype), kind="ExternalInput").ap()
    shape = given["L0_attn_x"].shape
    A["out"] = nc.dram_tensor("out", [shape[0] * shape[1], shape[2]], F32, kind="ExternalOutput").ap()

    def dram(name, shape, dt):
        return nc.dram_tensor(name, list(shape), dt, kind="Internal").ap()
    build(nc, A, dram)
    r = run_bass_kernel_spmd(nc, [arrays], core_ids=[0])
    return r.results[0]["out"].reshape(shape)
```
